# Optimizing a Trainium2 kernel written in Bass

```python
import numpy as np
import jax
import jax.numpy as jnp

def _softmax(x, axis=-1):
    return jax.nn.softmax(x, axis=axis)

def _gelu(x):
    return jax.nn.gelu(x, approximate=True)

def _silu(x):
    return jax.nn.silu(x)

def _sigmoid(x):
    return jax.nn.sigmoid(x)

def _layernorm(x, axis=-1, eps=1e-05):
    m = jnp.mean(x, axis=axis, keepdims=True)
    v = jnp.var(x, axis=axis, keepdims=True)
    return (x - m) / jnp.sqrt(v + eps)

def _scatter_add(tgt, idx, src, axis=0):
    return tgt.at[idx].add(src)

def _segment_sum(src, seg, n):
    return jax.ops.segment_sum(src, seg, n)
kernel_name = 'mk_cond_resid_d4_seqx_r4_2487bc'

def setup_inputs(seed: int=0):
    np.random.seed(seed)
    _w = jnp.asarray

    def _rec_inputs():
        import jax
        import jax.numpy as jnp
        _rk = jax.random.key(seed)
        x = -0.0002928 + 1 * jax.random.normal(jax.random.fold_in(_rk, 1), (8, 512, 256), jnp.float32)
        _lenS = 512 - jax.random.randint(jax.random.fold_in(_rk, 7), (8,), 0, max(1, 512 // 4) + 1, jnp.int32)
        _lenS2 = 512 - jax.random.randint(jax.random.fold_in(_rk, 8), (8,), 0, max(1, 512 // 4) + 1, jnp.int32)
        cond_256 = -0.106481 + 1.03144 * jax.random.normal(jax.random.fold_in(_rk, 12), (8, 64), jnp.float32)
        cond_64 = 0.0223021 + 1.01123 * jax.random.normal(jax.random.fold_in(_rk, 13), (8, 64), jnp.float32)
        _validS = jnp.arange(512)[None, :] < _lenS[:, None]
        _validS2 = jnp.arange(512)[None, :] < _lenS2[:, None]
        _causal = jnp.tril(jnp.ones((512, 512), dtype=bool))
        mask_SxS_bk1 = jnp.broadcast_to(_validS[0:1, :], (512, 512))
        return (x, cond_256, cond_64, mask_SxS_bk1)
    x, cond_256, cond_64, mask_SxS_bk1 = _rec_inputs()

    def _L0_cond_setup():
        import jax, jax.numpy as jnp
        import numpy as np
        EPS = 1e-06
        key = jax.random.key(seed)
        ks = jax.random.split(key, 8)
        B, S, E, C = (2, 512, 256, 64)
        x = jax.random.normal(ks[0], (B, S, E), dtype=jnp.float32)
        mask = jnp.triu(jnp.ones((S, S), dtype=bool), k=1)
        conditioning = jax.random.normal(ks[1], (B, C), dtype=jnp.float32)
        sc = 1.0 / np.sqrt(E)
        Wq = jax.random.normal(ks[2], (E, E), dtype=jnp.float32) * sc
        Wk = jax.random.normal(ks[3], (E, E), dtype=jnp.float32) * sc
        Wv = jax.random.normal(ks[4], (E, E), dtype=jnp.float32) * sc
        Wo = jax.random.normal(ks[5], (E, E), dtype=jnp.float32) * sc
        rms_scale = jnp.ones((E,), dtype=jnp.float32)
        Wc = jax.random.normal(ks[6], (2 * E, C), dtype=jnp.float32) * 0.02
        bc = jax.random.normal(ks[7], (2 * E,), dtype=jnp.float32) * 0.02
        return {'x': x, 'mask': mask, 'conditioning': conditioning, 'Wq': Wq, 'Wk': Wk, 'Wv': Wv, 'Wo': Wo, 'rms_scale': rms_scale, 'Wc': Wc, 'bc': bc}
    _L0_cond_all = _L0_cond_setup()
    _L0_cond_in = {k: v for k, v in _L0_cond_all.items() if k in ('Wq', 'Wk', 'Wv', 'Wo', 'rms_scale', 'Wc', 'bc')}
    del _L0_cond_all

    def _L1_cond_setup():
        import jax, jax.numpy as jnp
        import numpy as np
        TOP_K = 2
        EPS = 1e-06
        B, S, H, G, E, M = (2, 512, 256, 64, 8, 512)
        key = jax.random.key(seed)
        ks = jax.random.split(key, 16)
        s_h = 1.0 / np.sqrt(H)
        s_g = 1.0 / np.sqrt(G)
        s_m = 1.0 / np.sqrt(M)
        return {'x': jax.random.normal(ks[0], (B, S, H), jnp.float32), 'genre_embed': jax.random.normal(ks[1], (B, 1, G), jnp.float32), 'rms_w': jnp.ones((H,), jnp.float32), 'wg_W': jax.random.normal(ks[2], (H, E), jnp.float32) * s_h, 'wg_b': jnp.zeros((E,), jnp.float32), 'gg_W': jax.random.normal(ks[3], (G, E), jnp.float32) * s_g, 'gg_b': jnp.zeros((E,), jnp.float32), 'W1': jax.random.normal(ks[4], (E, H, M), jnp.float32) * s_h, 'b1': jnp.zeros((E, M), jnp.float32), 'W2': jax.random.normal(ks[5], (E, M, M), jnp.float32) * s_m, 'b2': jnp.zeros((E, M), jnp.float32), 'W3': jax.random.normal(ks[6], (E, M, H), jnp.float32) * s_m, 'b3': jnp.zeros((E, H), jnp.float32)}
    _L1_cond_all = _L1_cond_setup()
    _L1_cond_in = {k: v for k, v in _L1_cond_all.items() if k in ('rms_w', 'wg_W', 'wg_b', 'gg_W', 'gg_b', 'W1', 'b1', 'W2', 'b2', 'W3', 'b3')}
    del _L1_cond_all

    def _L2_cond_setup():
        import math
        import jax, jax.numpy as jnp
        import numpy as np
        from jax.scipy.linalg import cholesky, solve_triangular
        B, S, D, O, K, R = (4, 2048, 256, 256, 64, 64)

        def build_dct_basis(dim: int, num_bases: int) -> np.ndarray:
            num_bases = min(num_bases, dim)
            positions = np.arange(dim, dtype=np.float32)[None, :]
            modes = np.arange(num_bases, dtype=np.float32)[:, None]
            basis = np.cos(math.pi / float(dim) * (positions + 0.5) * modes)
            basis[0] = basis[0] / math.sqrt(2.0)
            basis = basis * math.sqrt(2.0 / float(dim))
            return basis.astype(np.float32)

        def _orthogonalize_mode_to_rank(raw: jnp.ndarray) -> jnp.ndarray:
            raw = raw.astype(jnp.float32)
            gram = raw.T @ raw
            eye = jnp.eye(raw.shape[1], dtype=jnp.float32)
            chol = cholesky(gram + 0.0001 * eye, lower=True)
            inv_chol = solve_triangular(chol, eye, lower=True)
            q = raw @ inv_chol.T
            signs = jnp.sign(jnp.sum(q * raw, axis=0, keepdims=True))
            signs = jnp.where(signs == 0, jnp.ones_like(signs), signs)
            return q * signs
        key = jax.random.key(seed)
        k1, k2, k3, k4, k5 = jax.random.split(key, 5)
        x = jax.random.normal(k1, (B, S, D), dtype=jnp.float32)
        spectral_coeff = jax.random.normal(k2, (B, K), dtype=jnp.float32)
        rank_coeff = jax.random.normal(k3, (B, R), dtype=jnp.float32)
        input_basis = jnp.asarray(build_dct_basis(D, K))
        diag = min(K, R)
        mode_to_rank = 0.02 * jax.random.normal(k4, (K, R), dtype=jnp.float32)
        mode_to_rank = mode_to_rank.at[:diag, :diag].add(jnp.eye(diag, dtype=jnp.float32))
        output_basis = 0.02 * jax.random.normal(k5, (R, O), dtype=jnp.float32)
        return {'x': x, 'spectral_coeff': spectral_coeff, 'rank_coeff': rank_coeff, 'input_basis': input_basis, 'mode_to_rank': mode_to_rank, 'output_basis': output_basis}
    _L2_cond_all = _L2_cond_setup()
    _L2_cond_in = {k: v for k, v in _L2_cond_all.items() if k in ('input_basis', 'mode_to_rank', 'output_basis')}
    del _L2_cond_all

    def _L3_cond_setup():
        import jax, jax.numpy as jnp
        import numpy as np
        EPS = 1e-08

        def hamilton(q1, q2):
            w1, x1, y1, z1 = (q1[..., i, :] for i in range(4))
            w2, x2, y2, z2 = (q2[..., i, :] for i in range(4))
            w = w1 * w2 - x1 * x2 - y1 * y2 - z1 * z2
            x = w1 * x2 + x1 * w2 + y1 * z2 - z1 * y2
            y = w1 * y2 - x1 * z2 + y1 * w2 + z1 * x2
            z = w1 * z2 + x1 * y2 - y1 * x2 + z1 * w2
            return jnp.stack([w, x, y, z], axis=-2)

        def _normalize(q):
            return q / jnp.sqrt(jnp.sum(q * q, axis=0, keepdims=True) + EPS)
        key = jax.random.key(seed)
        k1, k2, k3, k4 = jax.random.split(key, 4)
        B, T, d_model = (4, 1024, 256)
        quat_dim = d_model // 4
        x = jax.random.normal(k1, (B, T, d_model), dtype=jnp.float32)
        q_left = jax.random.normal(k2, (4, quat_dim), dtype=jnp.float32)
        q_right = jax.random.normal(k3, (4, quat_dim), dtype=jnp.float32)
        spectral_gate = jax.random.uniform(k4, (1, 1, 1, quat_dim), dtype=jnp.float32)
        return {'x': x, 'q_left': q_left, 'q_right': q_right, 'spectral_gate': spectral_gate}
    _L3_cond_all = _L3_cond_setup()
    _L3_cond_in = {k: v for k, v in _L3_cond_all.items() if k in ('q_right', 'spectral_gate')}
    del _L3_cond_all
    return {'x': x, 'cond_256': cond_256, 'cond_64': cond_64, 'mask_SxS_bk1': mask_SxS_bk1, 'L0_cond_Wq': _L0_cond_in['Wq'], 'L0_cond_Wk': _L0_cond_in['Wk'], 'L0_cond_Wv': _L0_cond_in['Wv'], 'L0_cond_Wo': _L0_cond_in['Wo'], 'L0_cond_rms_scale': _L0_cond_in['rms_scale'], 'L0_cond_Wc': _L0_cond_in['Wc'], 'L0_cond_bc': _L0_cond_in['bc'], 'L1_cond_rms_w': _L1_cond_in['rms_w'], 'L1_cond_wg_W': _L1_cond_in['wg_W'], 'L1_cond_wg_b': _L1_cond_in['wg_b'], 'L1_cond_gg_W': _L1_cond_in['gg_W'], 'L1_cond_gg_b': _L1_cond_in['gg_b'], 'L1_cond_W1': _L1_cond_in['W1'], 'L1_cond_b1': _L1_cond_in['b1'], 'L1_cond_W2': _L1_cond_in['W2'], 'L1_cond_b2': _L1_cond_in['b2'], 'L1_cond_W3': _L1_cond_in['W3'], 'L1_cond_b3': _L1_cond_in['b3'], 'L2_cond_input_basis': _L2_cond_in['input_basis'], 'L2_cond_mode_to_rank': _L2_cond_in['mode_to_rank'], 'L2_cond_output_basis': _L2_cond_in['output_basis'], 'L3_cond_q_right': _L3_cond_in['q_right'], 'L3_cond_spectral_gate': _L3_cond_in['spectral_gate']}

def reference(x, cond_256, cond_64, mask_SxS_bk1, L0_cond_Wq, L0_cond_Wk, L0_cond_Wv, L0_cond_Wo, L0_cond_rms_scale, L0_cond_Wc, L0_cond_bc, L1_cond_rms_w, L1_cond_wg_W, L1_cond_wg_b, L1_cond_gg_W, L1_cond_gg_b, L1_cond_W1, L1_cond_b1, L1_cond_W2, L1_cond_b2, L1_cond_W3, L1_cond_b3, L2_cond_input_basis, L2_cond_mode_to_rank, L2_cond_output_basis, L3_cond_q_right, L3_cond_spectral_gate):
    import jax
    import jax.numpy as jnp

    def _L0_cond_ref(x, mask, conditioning, Wq, Wk, Wv, Wo, rms_scale, Wc, bc):
        import jax, jax.numpy as jnp
        import numpy as np
        EPS = 1e-06
        B, S, E = x.shape
        H = 16
        D = E // H
        scale = D ** (-0.5)

        def proj(W):
            return (x @ W.T).reshape(B, S, H, D).transpose(0, 2, 1, 3)
        q, k, v = (proj(Wq), proj(Wk), proj(Wv))
        scores = jnp.einsum('bhsd,bhtd->bhst', q, k) * scale
        scores = jnp.where(mask[None, None, :, :], -jnp.inf, scores)
        attn = jax.nn.softmax(scores, axis=-1)
        out = jnp.einsum('bhst,bhtd->bhsd', attn, v)
        out = out.transpose(0, 2, 1, 3).reshape(B, S, E)
        out = out @ Wo.T
        rms = jnp.sqrt(jnp.mean(out * out, axis=-1, keepdims=True) + EPS)
        xn = out / rms * rms_scale
        mod = jax.nn.silu(conditioning) @ Wc.T + bc
        shift, sc = jnp.split(mod, 2, axis=-1)
        xn = xn * (1.0 + sc[:, None, :]) + shift[:, None, :]
        return xn

    def _L1_cond_ref(x, genre_embed, rms_w, wg_W, wg_b, gg_W, gg_b, W1, b1, W2, b2, W3, b3):
        import jax, jax.numpy as jnp
        import numpy as np
        TOP_K = 2
        EPS = 1e-06
        E = W1.shape[0]
        var = jnp.mean(x * x, axis=-1, keepdims=True)
        xn = rms_w * (x * jax.lax.rsqrt(var + EPS))
        gate = xn @ wg_W + wg_b + (genre_embed @ gg_W + gg_b)
        gate_w = jax.nn.softmax(gate, axis=-1)
        topk_w, topk_i = jax.lax.top_k(gate_w, TOP_K)
        cw = jnp.sum(jax.nn.one_hot(topk_i, E, dtype=x.dtype) * topk_w[..., None], axis=-2)
        h1 = jax.nn.relu(jnp.einsum('bsh,ehm->bsem', x, W1) + b1)
        h2 = jax.nn.relu(jnp.einsum('bsem,emn->bsen', h1, W2) + b2)
        out_e = jnp.einsum('bsen,enh->bseh', h2, W3) + b3
        return jnp.einsum('bseh,bse->bsh', out_e, cw)

    def _L2_cond_ref(x, spectral_coeff, rank_coeff, input_basis, mode_to_rank, output_basis):
        import math
        import jax, jax.numpy as jnp
        import numpy as np
        from jax.scipy.linalg import cholesky, solve_triangular
        B, S, D, O, K, R = (4, 2048, 256, 256, 64, 64)

        def build_dct_basis(dim: int, num_bases: int) -> np.ndarray:
            num_bases = min(num_bases, dim)
            positions = np.arange(dim, dtype=np.float32)[None, :]
            modes = np.arange(num_bases, dtype=np.float32)[:, None]
            basis = np.cos(math.pi / float(dim) * (positions + 0.5) * modes)
            basis[0] = basis[0] / math.sqrt(2.0)
            basis = basis * math.sqrt(2.0 / float(dim))
            return basis.astype(np.float32)

        def _orthogonalize_mode_to_rank(raw: jnp.ndarray) -> jnp.ndarray:
            raw = raw.astype(jnp.float32)
            gram = raw.T @ raw
            eye = jnp.eye(raw.shape[1], dtype=jnp.float32)
            chol = cholesky(gram + 0.0001 * eye, lower=True)
            inv_chol = solve_triangular(chol, eye, lower=True)
            q = raw @ inv_chol.T
            signs = jnp.sign(jnp.sum(q * raw, axis=0, keepdims=True))
            signs = jnp.where(signs == 0, jnp.ones_like(signs), signs)
            return q * signs
        mtr = _orthogonalize_mode_to_rank(mode_to_rank).astype(x.dtype)
        proj = jnp.einsum('bsd,kd->bsk', x, input_basis.astype(x.dtype))
        proj = proj * spectral_coeff[:, None, :]
        hidden = jnp.einsum('bsk,kr->bsr', proj, mtr)
        hidden = hidden * rank_coeff[:, None, :]
        out = jnp.einsum('bsr,ro->bso', hidden, output_basis.astype(x.dtype))
        return out

    def _L3_cond_ref(x, q_left, q_right, spectral_gate):
        import jax, jax.numpy as jnp
        import numpy as np
        EPS = 1e-08

        def hamilton(q1, q2):
            w1, x1, y1, z1 = (q1[..., i, :] for i in range(4))
            w2, x2, y2, z2 = (q2[..., i, :] for i in range(4))
            w = w1 * w2 - x1 * x2 - y1 * y2 - z1 * z2
            x = w1 * x2 + x1 * w2 + y1 * z2 - z1 * y2
            y = w1 * y2 - x1 * z2 + y1 * w2 + z1 * x2
            z = w1 * z2 + x1 * y2 - y1 * x2 + z1 * w2
            return jnp.stack([w, x, y, z], axis=-2)

        def _normalize(q):
            return q / jnp.sqrt(jnp.sum(q * q, axis=0, keepdims=True) + EPS)
        B, T, d_model = x.shape
        quat_dim = d_model // 4
        x_quat = x.reshape(B, T, 4, quat_dim)
        x_spectral = jnp.fft.fft(x_quat, axis=1)
        x_filtered = jnp.fft.ifft(x_spectral * spectral_gate, axis=1).real.astype(x.dtype)
        q_left_n = _normalize(q_left)
        q_right_n = _normalize(q_right)
        conj_sign = jnp.array([1.0, -1.0, -1.0, -1.0], dtype=x.dtype)[:, None]
        q_right_conj = q_right_n * conj_sign
        x_right = hamilton(x_filtered, q_right_conj)
        x_rotated = hamilton(q_left_n, x_right)
        return x_rotated.reshape(B, T, d_model)
    x = x + _L0_cond_ref(x, mask_SxS_bk1, cond_256, L0_cond_Wq, L0_cond_Wk, L0_cond_Wv, L0_cond_Wo, L0_cond_rms_scale, L0_cond_Wc, L0_cond_bc)
    x = x + _L1_cond_ref(x, cond_256[:, None, :], L1_cond_rms_w, L1_cond_wg_W, L1_cond_wg_b, L1_cond_gg_W, L1_cond_gg_b, L1_cond_W1, L1_cond_b1, L1_cond_W2, L1_cond_b2, L1_cond_W3, L1_cond_b3)
    x = x + _L2_cond_ref(x, cond_256, cond_64, L2_cond_input_basis, L2_cond_mode_to_rank, L2_cond_output_basis)
    x = x + _L3_cond_ref(x, cond_256, L3_cond_q_right, L3_cond_spectral_gate)
    return x

_drawn_inputs = setup_inputs


def setup_inputs(seed=0):
    import zlib

    import numpy as np

    out = dict(_drawn_inputs(seed))
    spreads = {'L0_cond_rms_scale': (1.0, 0.2),
     'L1_cond_rms_w': (1.0, 0.2),
     'L1_cond_wg_b': (0.0, 0.1),
     'L1_cond_gg_b': (0.0, 0.1),
     'L1_cond_b1': (0.0, 0.484),
     'L1_cond_b2': (0.0, 0.337),
     'L1_cond_b3': (0.0, 0.1)}
    factors = {}
    for name, (base, spread) in spreads.items():
        noise = np.random.default_rng([zlib.crc32(name.encode()), seed]).standard_normal(out[name].shape)
        drawn = base * np.exp(spread * noise) if base else spread * noise
        out[name] = jnp.asarray(drawn.astype(out[name].dtype))
    for name, factor in factors.items():
        out[name] = (out[name] * factor).astype(out[name].dtype)
    return out
```

```python
import numpy as np
from contextlib import ExitStack
import concourse.bass as bass
import concourse.mybir as mybir

F32 = mybir.dt.float32
BF16 = mybir.dt.bfloat16
U8 = mybir.dt.uint8
I32 = mybir.dt.int32
U32 = mybir.dt.uint32
ALU = mybir.AluOpType
ACT = mybir.ActivationFunctionType
AX = mybir.AxisListType

P = 128
B, S, E = 8, 512, 256
H = 16
D = E // H
C = 64
NX = 8
M = 512
KT = E // P
ST = S // P
NT = B * ST
GH = 4
NG = H // GH
PARTS = 3
PAIRS = [(0, 0), (1, 0), (0, 1), (1, 1), (0, 2), (2, 0)]
KQ = len(PAIRS) * D
MASKED = -3.0e38
FLOOR = -1.0e38


TW = 256
TT = TW // P
TOPK = 2
NTILES = B * S * TOPK // TW + NX - 1
REGION = B * S + TW
NULL_ROW = NX * REGION
LOST_ROW = NULL_ROW + TW
RW = E + 2
KB = 64
BETA = 3


class Engine:

    def __init__(self, sem):
        self.sem, self.count, self.steps, self.passed = sem, 0, [], {}

    def wait(self, *tokens):
        for sem, value in tokens:
            if value > self.passed.get(sem.name, 0):
                self.passed[sem.name] = value
                self.steps.append((None, sem, value))

    def do(self, op, *args, after=(), mark=True, **kw):
        self.wait(*after)
        self.steps.append((op, args, kw, self.sem if mark else None, 1))
        self.count += mark
        return (self.sem, self.count)

    def now(self):
        return (self.sem, self.count)

    def emit(self, engine):
        for step in self.steps:
            if step[0] is None:
                engine.wait_ge(step[1], step[2])
            else:
                op, args, kw, sem, n = step
                ins = op(*args, **kw)
                if sem is not None:
                    ins.then_inc(sem, n)


class Lane:

    def __init__(self, sem):
        self.sem, self.count = sem, 0

    def start(self, queue, op, out, in_, after=()):
        queue.wait(*after)
        queue.steps.append((op, (out, in_), {}, self.sem, 16))
        self.count += 16
        return (self.sem, self.count)


class Ring:

    def __init__(self, bufs):
        self.bufs, self.free, self.n = bufs, [()] * len(bufs), 0

    def take(self):
        i = self.n % len(self.bufs)
        self.n += 1
        return i, self.bufs[i], self.free[i]

    def give(self, i, *tokens):
        self.free[i] = tokens


def build(nc, d, out):
    with ExitStack() as ctx:
        _build(nc, ctx, d, out)


def _build(nc, ctx, d, out):
    outer, phase = ctx, [ExitStack()]

    def sb(name, shape, dt=F32):
        return phase[0].enter_context(nc.sbuf_tensor(name, shape, dt))

    def sem(name):
        return ctx.enter_context(nc.semaphore(name))

    def lane(name):
        return Lane(sem("dma_" + name))

    pe, act, dve, pool, sp = (Engine(sem("progress_" + n)) for n in ("pe", "act", "dve", "pool", "sp"))
    V, A, G, T = nc.vector, nc.scalar, nc.gpsimd, nc.tensor
    load = nc.sync.dma_start

    bank = [ctx.enter_context(nc.psum_tensor(f"bank{i}", [P, 512], F32)) for i in range(8)]

    def lasting(name, shape, dt=F32):
        return outer.enter_context(nc.sbuf_tensor(name, shape, dt))

    ident = lasting("ident", [P, P])
    empty = lasting("empty", [P, TT, RW])
    table = lasting("table", [P, 2 * NTILES + NX], I32)
    mtrT = lasting("mtrT", [KB, KB])
    obm = lasting("obm", [KB, E])
    basis = lasting("basis", [KB, E])
    quat = lasting("quat", [P, KT, E])
    cond_cols = lasting("cond_cols", [C, 2, B])

    identb = sb("identb", [P, P], BF16)
    upper = sb("upper", [P, P], BF16)
    ones = sb("ones", [P, P], BF16)
    xw = [sb(f"xw{i}", [P, ST, RW]) for i in range(TOPK)]
    x1T = sb("x1T", [P, KT, S])
    wg = sb("wg", [P, KT, NX])
    rmsw = sb("rmsw", [P, KT])
    ggw = sb("ggw", [C + 2, NX])
    condR = sb("condR", [C + 2, B])
    below = sb("below", [KB, KB])
    elim = sb("elim", [KB, 2 * KB])
    raw = sb("raw", [KB, 2, KB])
    pivot = sb("pivot", [KB, 8])
    newton = sb("newton", [P, 4, ST])
    ints = sb("ints", [P, 2 * NX + NT + 1 + NTILES], I32)
    flts = sb("flts", [P, 2 * NX + NT + 1 + NTILES])
    gt = sb("gt", [P, 8, ST, NX])
    gs = sb("gs", [P, 8, ST])
    cnt = sb("cnt", [P, ST, NX], BF16)
    run = [sb(f"run{i}", [P, ST + 1, NX]) for i in range(2)]
    idx = [sb(f"idx{i}", [P, TOPK, ST], U32) for i in range(2)]
    tb = sb("tb", [P, 10, NX])
    tbi = sb("tbi", [P, NX], I32)
    x1T_flat = x1T[:, :, :].rearrange("p k s -> p (k s)")
    tj = x1T_flat[:, 0:2 * NTILES * NX].rearrange("p (a t x) -> p a t x", a=2, x=NX)
    tv = x1T_flat[:, 2 * NTILES * NX:(2 * NX + 6) * NTILES].rearrange("p (a t) -> p a t", a=6)

    wqk = sb("wqk", [P, 2, KT, E])
    wv = sb("wv", [P, KT, E])
    wo = sb("wo", [P, NG, E])
    mneg = sb("mneg", [P, 2, ST, S], BF16)
    xT = [sb(f"xT{i}", [P, KT, S]) for i in range(2)]
    xin = [sb(f"xin{i}", [P, ST, E]) for i in range(2)]
    parts = [sb(f"parts{i}", [P, 2, PARTS, S], BF16) for i in range(2)]
    rest = [sb(f"rest{i}", [P, S]) for i in range(2)]
    qst = [sb(f"qst{i}", [P, H, S], BF16) for i in range(2)]
    kst = [sb(f"kst{i}", [P, H, S], BF16) for i in range(2)]
    vaug = [sb(f"vaug{i}", [P, ST, H, 32]) for i in range(2)]
    junk = [sb(f"junk{i}", [P, S], BF16) for i in range(2)]
    rowmax = [sb(f"rowmax{i}", [P, GH, ST]) for i in range(2)]
    negm = [sb(f"negm{i}", [P, 2, GH, ST]) for i in range(2)]
    m3 = [sb(f"m3_{i}", [P, ST, GH, PARTS], BF16) for i in range(2)]
    mrow = [sb(f"mrow{i}", [GH * PARTS, S], BF16) for i in range(2)]
    pt = [sb(f"pt{i}", [P, S]) for i in range(8)]
    turned = [sb(f"turned{i}", [P, 16, 32]) for i in range(2)]
    rden = [sb(f"rden{i}", [P, 16]) for i in range(2)]
    oT = [sb(f"oT{i}", [P, NG, S]) for i in range(2)]
    osb = sb("osb", [P, ST, E])
    mask8 = osb[:, :, :].rearrange("p s e -> p (s e)").bitcast(U8).rearrange("p (a s t) -> p a s t", a=2, s=ST)
    ssq = sb("ssq", [P, 4, ST])
    condS = sb("condS", [C + 1, B])
    condw = sb("condw", [C, 3, B])
    wc = sb("wc", [C + 1, 2 * E])
    rmsb = sb("rmsb", [P, E])
    gain = [sb(f"gain{i}", [P, E]) for i in range(2)]
    shift = [sb(f"shift{i}", [P, E]) for i in range(2)]

    x_dram, xT_dram = d["x"], d["xT"]
    split_dram = nc.dram_tensor("split_parts", (B, 2, PARTS, H // 8 * P, S), BF16, kind="Internal").ap()

    l_w = lane("weights")
    t_w = None
    for i, n in enumerate(("WqT", "WkT")):
        l_w.start(sp, load, wqk[:, i], d[n].rearrange("(k p) e -> p k e", p=P))
    t_w = l_w.start(sp, load, wv[:, :, :], d["WvT"].rearrange("(k p) e -> p k e", p=P))
    l_x = [lane(f"xT{i}") for i in range(2)]
    l_xin = [lane(f"xin{i}") for i in range(2)]
    t_xT, t_xin = {}, {}
    last_x_use = {}

    def load_x(b):
        free = last_x_use.get(b - 2, ())
        t_xT[b] = l_x[b % 2].start(sp, load, xT[b % 2][:, :, :],
                                   xT_dram[:, b * S:(b + 1) * S].rearrange("(k p) s -> p k s", p=P), after=free)

    last_xin_use = {}

    def load_xin(b):
        t_xin[b] = l_xin[b % 2].start(sp, load, xin[b % 2][:, :, :],
                                      x_dram[b * S:(b + 1) * S, :].rearrange("(j p) e -> p j e", p=P),
                                      after=last_xin_use.get(b - 2, ()))

    load_x(0)
    l_m = lane("masks")
    l_m.start(sp, load, mask8[:, 0], d["mask"].rearrange("(j p) t -> p j t", p=P))
    t_mask = l_m.start(sp, load, mask8[:, 1], d["maskT"].rearrange("(j p) t -> p j t", p=P))
    l_c = lane("conditioning")
    l_c.start(sp, load, condw[:, 0], d["condT"])
    l_c.start(sp, load, wc[0:C], d["WcT"])
    l_c.start(sp, load, wc[C:C + 1], d["bc"].unsqueeze(0))
    t_c = l_c.start(sp, load, rmsb[:, :], d["rms_scale"].unsqueeze(0).to_broadcast([P, E]))

    t_id0 = pool.do(G.memset, ident[:, :], 0.0)
    t_id = pool.do(G.affine_select, out=ident[:, :], in_=ident[:, :], compare_op=ALU.not_equal, fill=1.0,
                   base=0, pattern=[[-1, P]], channel_multiplier=1, after=[t_id0])
    t_zero = []
    for i in range(2):
        t = pool.do(G.memset, vaug[i][:, :, :, D:32], 0.0, after=[pool.now()])
        t_zero.append(pool.do(G.memset, vaug[i][:, :, :, D:D + 1], 1.0, after=[t]))
        pool.do(G.memset, kst[i][KQ:KQ + PARTS, :, :], 1.0, after=[pool.now()])
    t_kones = pool.now()
    t_wo0 = pool.do(G.memset, wo[:, :, :], 0.0, after=[pool.now()])
    t_cond1 = pool.do(G.memset, condS[C:C + 1, :], 1.0, after=[pool.now()])
    l_wo = lane("wo")
    for g in range(GH):
        t_wo = l_wo.start(sp, load, wo[32 * g:32 * g + D],
                          d["WoT"].rearrange("(G g d) e -> g d G e", g=GH, d=D)[g], after=[t_wo0])
    load_x(1)
    load_xin(0)

    l_s = lane("small")
    for dst, src in ((wg[:, :, :], d["wg_W"].rearrange("(k p) x -> p k x", p=P)),
                     (rmsw[:, :], d["rms_w"]),
                     (ggw[0:C], d["gg_W"]), (ggw[C:C + 1], d["gg_b"].unsqueeze(0)),
                     (ggw[C + 1:C + 2], d["wg_b"].unsqueeze(0)), (condR[0:C], d["condT"]),
                     (cond_cols[:, 0], d["condT"]), (cond_cols[:, 1], d["cond64T"]),
                     (raw[:, 0], d["mtr"]), (raw[:, 1], d["mtrT"]), (basis[:, :], d["input_basis"]),
                     (obm[:, :], d["output_basis"])):
        t_small = l_s.start(sp, load, dst, src)

    def constant(op, *args, **kw):
        return pool.do(op, *args, after=[pool.now()], **kw)

    n_rev, n_base, n_tok, n_lost, n_tile = 0, NX, 2 * NX, 2 * NX + NT, 2 * NX + NT + 1
    constant(G.iota, ints[:, n_rev:n_rev + NX], [[-1, NX]], base=NX, channel_multiplier=0)
    constant(G.iota, ints[:, n_base:n_base + NX], [[REGION, NX]], base=0, channel_multiplier=0)
    constant(G.iota, ints[:, n_tok:n_tok + NT], [[P, NT]], base=0, channel_multiplier=1)
    constant(G.iota, ints[:, n_lost:n_lost + 1], [[1, 1]], base=LOST_ROW, channel_multiplier=1)
    constant(G.iota, ints[:, n_tile:n_tile + NTILES], [[1, NTILES]], base=0, channel_multiplier=0)
    constant(G.iota, empty[:, :, E + 1].bitcast(I32), [[P, TT]], base=B * S, channel_multiplier=1)
    constant(G.memset, empty[:, :, 0:E + 1], 0.0)
    constant(G.memset, condR[C:C + 2, :], 1.0)
    constant(G.memset, ones[:, :], 1.0)
    constant(G.memset, run[1][:, ST, :], 0.0)
    constant(G.affine_select, out=upper[:, :], in_=ones[:, :], compare_op=ALU.is_gt, fill=0.0, base=0,
             pattern=[[1, P]], channel_multiplier=-1)
    constant(G.memset, below[:, :], -1.0)
    t_const = constant(G.affine_select, out=below[:, :], in_=below[:, :], compare_op=ALU.is_gt, fill=0.0,
                       base=0, pattern=[[-1, KB]], channel_multiplier=1)
    t_flt = dve.do(V.tensor_copy, flts[:, :], ints[:, :], after=[t_const])
    rev, first_row = flts[:, n_rev:n_rev + NX], flts[:, n_base:n_base + NX]
    t_wg = None
    for k in range(KT):
        t_wg = dve.do(V.tensor_scalar, wg[:, k], wg[:, k], rmsw[:, k:k + 1], None, ALU.mult, after=[t_small])

    t_idb = dve.do(V.tensor_copy, identb[:, :], ident[:, :], after=[t_id])
    t_mn = dve.do(V.tensor_scalar, mneg[:, 0], mask8[:, 0], MASKED, None, ALU.mult, after=[t_mask])
    t_mn = dve.do(V.tensor_scalar, mneg[:, 1], mask8[:, 1], MASKED, None, ALU.mult)

    t_e = act.do(A.activation, condw[:, 1], condw[:, 0], ACT.Exp, scale=-1.0, after=[t_c])
    t = dve.do(V.tensor_scalar, condw[:, 2], condw[:, 1], 1.0, None, ALU.add, after=[t_e])
    t = dve.do(V.reciprocal, condw[:, 1], condw[:, 2], after=[t])
    t = dve.do(V.tensor_tensor, condS[0:C], condw[:, 0], condw[:, 1], ALU.mult, after=[t])
    t_cs = t

    row_scores = Ring(bank[0:2])
    col_scores = Ring(bank[2:5])
    misc = Ring(bank[6:8])
    av_bank, av_free = bank[5], [()]
    probs = Ring(pt)
    junks = Ring(junk)
    rests = Ring(rest)

    l_parts = [lane(f"parts{i}") for i in range(2)]
    l_stack = [lane(f"stack{i}") for i in range(2)]
    l_mrow = [lane(f"mrow{i}") for i in range(2)]
    parts_free = [(), ()]
    t_parts, t_stack, t_v = {}, {}, {}
    stack_free = {}
    v_free = {}

    def project(b, qk, half):
        i, ps, free = misc.take()
        for k in range(KT):
            t = pe.do(T.matmul, ps[:, :], wqk[:, qk, k, half * P:(half + 1) * P], xT[b % 2][:, k, :],
                      start=(k == 0), stop=(k == KT - 1), mark=(k == KT - 1), after=[t_w, t_xT[b], *free])
        pp = parts[qk]
        hi, mid, lo = (pp[:, half, n, :] for n in range(PARTS))
        t_hi = act.do(A.activation, hi, ps[:, :], ACT.Copy, after=[t, *parts_free[qk]])
        r, left, rfree = rests.take()
        t_r = dve.do(V.tensor_tensor, left[:, :], ps[:, :], hi, ALU.subtract, after=[t, t_hi, *rfree])
        misc.give(i, t_r)
        t_mid = act.do(A.activation, mid, left[:, :], ACT.Copy, after=[t_r])
        t_lo = pool.do(G.tensor_tensor, lo, left[:, :], mid, ALU.subtract, after=[t_mid])
        rests.give(r, t_lo)
        t_out = l_parts[qk].start(sp, load, split_dram[b, qk][:, half * P:(half + 1) * P, :].rearrange("n p s -> p n s"),
                                  pp[:, half], after=[t_lo])
        t_parts[b, qk] = t_out
        if half == 1:
            parts_free[qk] = (t_out,)

    def stack(b):
        for qk in range(2):
            dst = (qst, kst)[qk][b % 2]
            for r, pair in enumerate(PAIRS):
                t_stack[b, qk] = l_stack[qk].start(
                    sp, load, dst[r * D:(r + 1) * D, :, :],
                    split_dram[b, qk, pair[qk]].rearrange("(h d) s -> d h s", d=D),
                    after=[t_parts[b, qk], *(stack_free[b - 2] if b >= 2 else ())])

    def project_v(b, st):
        i, ps, free = misc.take()
        for k in range(KT):
            t = pe.do(T.matmul, ps[:, 0:E], xT[b % 2][:, k, st * P:(st + 1) * P], wv[:, k, :],
                      start=(k == 0), stop=(k == KT - 1), mark=(k == KT - 1), after=[t_w, t_xT[b], *free])
        t_v[b] = act.do(A.activation, vaug[b % 2][:, st, :, 0:D], ps[:, 0:E].rearrange("p (h d) -> p h d", d=D),
                        ACT.Copy, after=[t, *v_free.get(b - 2, ())])
        misc.give(i, t_v[b])
        if st == ST - 1:
            last_x_use[b] = (t,)
            if b + 2 < B:
                load_x(b + 2)

    t_gain, gain_free = {}, {}

    def modulation(b):
        i, ps, free = misc.take()
        t = pe.do(T.matmul, ps[:, :], condS[:, b:b + 1].to_broadcast([C + 1, P]), wc[:, :], start=True, stop=True,
                  after=[t_cs, t_cond1, t_c, *free])
        t_s = act.do(A.activation, shift[b % 2][:, :], ps[:, 0:E], ACT.Copy, after=[t, *gain_free.get(b - 2, ())])
        t_g = dve.do(V.scalar_tensor_tensor, gain[b % 2][:, :], ps[:, E:2 * E], 1.0, rmsb[:, :], ALU.add, ALU.mult,
                     after=[t_s, *gain_free.get(b - 2, ())])
        misc.give(i, t_s, t_g)
        t_gain[b] = (t_s, t_g)

    t_max, max_free, t_m3, m3_free, mrow_free, t_mrow = {}, {}, {}, {}, {}, {}

    def row_maxima(gi, hh, st):
        b, h = gi // NG, gi % NG * GH + hh
        i, ps, free = row_scores.take()
        t = pe.do(T.matmul, ps[:, :], qst[b % 2][0:KQ, h, st * P:(st + 1) * P], kst[b % 2][0:KQ, h, :],
                  start=True, stop=True, after=[t_stack[b, 0], t_stack[b, 1], *free])
        j, jk, jfree = junks.take()
        t_max[gi] = dve.do(V.tensor_tensor_reduce, jk[:, :], ps[:, :], mneg[:, 0, st, :], 1.0, FLOOR, ALU.add,
                           ALU.max, rowmax[gi % 2][:, hh, st:st + 1], after=[t, *jfree, *max_free.get(gi - 2, ())])
        junks.give(j, t_max[gi])
        row_scores.give(i, t_max[gi])

    def split_maxima(gi):
        n, dst = negm[gi % 2], m3[gi % 2]
        v = [dst[:, :, :, k].rearrange("p s h -> p h s") for k in range(PARTS)]
        t = pool.do(G.tensor_scalar, n[:, 0], rowmax[gi % 2][:, :, :], -1.0, None, ALU.mult, after=[t_max[gi]])
        max_free[gi] = (t,)
        t = pool.do(G.tensor_copy, v[0], n[:, 0], after=[t, *m3_free.get(gi - 2, ())])
        t = pool.do(G.tensor_tensor, n[:, 1], n[:, 0], v[0], ALU.subtract, after=[t])
        t = pool.do(G.tensor_copy, v[1], n[:, 1], after=[t])
        t_m3[gi] = pool.do(G.tensor_tensor, v[2], n[:, 1], v[1], ALU.subtract, after=[t])

    def maxima_rows(gi):
        i, ps, free = misc.take()
        for st in range(ST):
            t = pe.do(T.matmul, ps[0:GH * PARTS, st * P:(st + 1) * P],
                      m3[gi % 2][:, st].rearrange("p h n -> p (h n)"), identb[:, :], start=True, stop=True,
                      mark=(st == ST - 1), after=[t_m3[gi], t_idb, *free])
        m3_free[gi] = (t,)
        t = act.do(A.activation, mrow[gi % 2][:, :], ps[0:GH * PARTS, :], ACT.Copy,
                   after=[t, *mrow_free.get(gi - 2, ())])
        misc.give(i, t)
        b = gi // NG
        for hh in range(GH):
            h = gi % NG * GH + hh
            t_mrow[gi] = l_mrow[gi % 2].start(sp, load, qst[b % 2][KQ:KQ + PARTS, h, :],
                                              mrow[gi % 2][hh * PARTS:(hh + 1) * PARTS, :],
                                              after=[t, *stack_free.get(b - 2, ())])
        mrow_free[gi] = (t_mrow[gi],)

    t_prob = {}

    def exponentials(gi, kt, hh):
        b, h = gi // NG, gi % NG * GH + hh
        i, ps, free = col_scores.take()
        t = pe.do(T.matmul, ps[:, :], kst[b % 2][0:KQ + PARTS, h, kt * P:(kt + 1) * P],
                  qst[b % 2][0:KQ + PARTS, h, :], start=True, stop=False, mark=False,
                  after=[t_mrow[gi], t_kones, *free])
        t = pe.do(T.matmul, ps[:, :], identb[:, :], mneg[:, 1, kt, :], start=False, stop=True, after=[t_mn])
        if gi % NG == NG - 1 and kt == ST - 1 and hh == GH - 1:
            stack_free[b] = (t,)
        j, pr, pfree = probs.take()
        t = act.do(A.activation, pr[:, :], ps[:, :], ACT.Exp, scale=float(D) ** -0.5, after=[t, *pfree])
        col_scores.give(i, t)
        t_prob[gi, kt, hh] = (j, pr, t)

    t_av = {}

    def weighted_values(gi, kt):
        b = gi // NG
        js = []
        for hh in range(GH):
            h = gi % NG * GH + hh
            j, pr, tp = t_prob.pop((gi, kt, hh))
            js.append(j)
            t = pe.do(T.matmul, av_bank[32 * hh:32 * hh + 32, :], vaug[b % 2][:, kt, h, :], pr[:, :],
                      start=(kt == 0), stop=(kt == ST - 1), mark=(hh == GH - 1),
                      after=[tp, t_v[b], t_zero[b % 2], *(av_free[0] if kt == 0 else ())])
        for j in js:
            probs.give(j, t)
        t_av[gi] = t
        if gi % NG == NG - 1 and kt == ST - 1:
            v_free[b] = (t,)

    t_oT, turned_free, oT_free = {}, {}, {}

    def normalise(gi):
        b, tn, rd = gi // NG, turned[gi % 2], rden[gi % 2]
        flat = tn[:, :, :].rearrange("p a c -> p (a c)")
        t = dve.do(V.transpose, flat, av_bank[:, :], after=[t_av[gi], *turned_free.get(gi - 2, ())])
        av_free[0] = (t,)
        t = dve.do(V.reciprocal, rd[:, :], tn[:, :, D], after=[t])
        t = dve.do(V.tensor_tensor, tn[:, :, 0:D], tn[:, :, 0:D], rd[:, :].unsqueeze(2).to_broadcast([P, 16, D]),
                   ALU.mult, after=[t])
        t_oT[gi] = dve.do(V.transpose, oT[b % 2][:, gi % NG, :], flat, after=[t, *oT_free.get(b - 2, ())])
        turned_free[gi] = (t_oT[gi],)

    osb_free = [()]
    t_osb = {}

    def output_projection(b, st):
        i, ps, free = misc.take()
        for g in range(NG):
            t = pe.do(T.matmul, ps[:, 0:E], oT[b % 2][:, g, st * P:(st + 1) * P], wo[:, g, :],
                      start=(g == 0), stop=(g == NG - 1), mark=(g == NG - 1), after=[t_oT[b * NG + g], t_wo, *free])
        if st == ST - 1:
            oT_free[b] = (t,)
        t_osb[b] = act.do(A.activation, osb[:, st, :], ps[:, 0:E], ACT.Copy, after=[t, *osb_free[0]])
        misc.give(i, t_osb[b])

    t_x1 = {}
    l_x1 = lane("x1")
    t_xw, xw_free = {}, [(), ()]
    x2_dram = nc.dram_tensor("x2", (B * S + TW, E), F32, kind="Internal").ap()
    routed = nc.dram_tensor("routed", (LOST_ROW + P, RW), F32, kind="Internal").ap()

    def inverse_rms(sums, after):
        t = dve.do(V.tensor_scalar, sums[:, 1], sums[:, 0], 1.0 / E, 1e-6, ALU.mult, ALU.add, after=[after])
        return inverse_root(sums[:, 3], sums[:, 1], sums[:, 2], t)

    def inverse_root(y, v, tmp, t):
        t = dve.do(V.tensor_scalar, tmp.bitcast(I32), v.bitcast(I32), 1, None, ALU.arith_shift_right, after=[t])
        t = dve.do(V.tensor_scalar, y.bitcast(I32), tmp.bitcast(I32), -1.0, float(0x5f3759df), ALU.mult, ALU.add,
                   after=[t])
        for _ in range(BETA):
            t = dve.do(V.tensor_tensor, tmp, y, y, ALU.mult, after=[t])
            t = dve.do(V.scalar_tensor_tensor, tmp, tmp, -0.5, v, ALU.mult, ALU.mult, after=[t])
            t = dve.do(V.scalar_tensor_tensor, y, tmp, 1.5, y, ALU.add, ALU.mult, after=[t])
        return t

    def residual(b):
        if b == 0:
            load_xin(1)
        t_s = pool.do(G.tensor_tensor, xin[b % 2][:, :, :], xin[b % 2][:, :, :],
                      shift[b % 2][:, :].unsqueeze(1).to_broadcast([P, ST, E]), ALU.add,
                      after=[t_xin[b], *t_gain[b]])
        for st in range(ST):
            j, jk, jfree = junks.take()
            t = dve.do(V.tensor_tensor_reduce, jk[:, 0:E], osb[:, st, :], osb[:, st, :], 1.0, 0.0, ALU.mult,
                       ALU.add, ssq[:, 0, st:st + 1], after=[t_osb[b], *jfree])
            junks.give(j, t)
        t = inverse_rms(ssq, t)
        for st in range(ST):
            t_g = dve.do(V.scalar_tensor_tensor, osb[:, st, :], osb[:, st, :], ssq[:, 3, st:st + 1],
                         gain[b % 2][:, :], ALU.mult, ALU.mult, after=[t, *t_gain[b]])
        for k in range(TOPK):
            t = pool.do(G.tensor_tensor, xw[k][:, :, 0:E], xin[b % 2][:, :, :], osb[:, :, :], ALU.add,
                        after=[t_g, t_s, *xw_free[k]])
            t_xw[b, k] = t
        osb_free[0] = (t,)
        gain_free[b] = (t_g, t_s)
        last_xin_use[b] = (t,)
        t_x1[b] = l_x1.start(sp, load, x2_dram[b * S:(b + 1) * S, :].rearrange("(j p) e -> p j e", p=P),
                             xw[0][:, :, 0:E], after=[t_xw[b, 0]])
        if b + 2 < B:
            load_xin(b + 2)

    l_q = lane("quaternions")
    t_quat, t_obm = [], []

    def quaternions():
        QD = E // 4
        qc = pt[0][:, :].rearrange("p (r d) -> p r d", d=QD)
        qr = pt[1][:, 0:E].rearrange("p (r d) -> p r d", d=QD)
        gate, norm = pt[1][:, E:E + QD], pt[1][:, E + QD:E + 2 * QD]
        inv, tmp = pt[1][:, E + 2 * QD:E + 3 * QD], pt[1][:, E + 3 * QD:2 * E]
        sq = pt[2][:, :].rearrange("p (r d) -> p r d", d=QD)
        right = [pt[3 + i // 2][:, i % 2 * E:(i % 2 + 1) * E].rearrange("p (j d) -> p j d", d=QD) for i in range(4)]
        coef = [pt[5 + i // 2][:, i % 2 * E:(i % 2 + 1) * E].rearrange("p (j d) -> p j d", d=QD) for i in range(4)]
        prod = pt[7][:, 0:E].rearrange("p (j d) -> p j d", d=QD)
        l_q.start(sp, load, pt[0][:, :], d["cond"].rearrange("b c -> (b c)").unsqueeze(0).to_broadcast([P, B * C]))
        l_q.start(sp, load, pt[1][:, 0:E], d["q_right"].rearrange("b c -> (b c)").unsqueeze(0).to_broadcast([P, E]))
        t = l_q.start(sp, load, gate, d["gate"].unsqueeze(0).to_broadcast([P, QD]))

        def v(op, *args, **kw):
            return dve.do(op, *args, after=[dve.now(), t], **kw)

        for q, rows in ((qc, B), (qr, 4)):
            v(V.tensor_tensor, sq[:, 0:rows], q, q, ALU.mult)
            v(V.tensor_reduce, norm, sq[:, 0:rows].rearrange("p r d -> p d r"), AX.X, ALU.add)
            v(V.tensor_scalar, norm, norm, 1e-8, None, ALU.add)
            inverse_root(inv, norm, tmp, dve.now())
            v(V.tensor_tensor, q[:, 0:4], q[:, 0:4], inv.unsqueeze(1).to_broadcast([P, 4, QD]), ALU.mult)
        v(V.tensor_tensor, qr[:, :, :], qr[:, :, :], gate.unsqueeze(1).to_broadcast([P, 4, QD]), ALU.mult)
        R = (((0, 1), (1, 1), (2, 1), (3, 1)), ((1, -1), (0, 1), (3, -1), (2, 1)),
             ((2, -1), (3, 1), (0, 1), (1, -1)), ((3, -1), (2, -1), (1, 1), (0, 1)))
        L = (((0, 1), (1, -1), (2, -1), (3, -1)), ((1, 1), (0, 1), (3, -1), (2, 1)),
             ((2, 1), (3, 1), (0, 1), (1, -1)), ((3, 1), (2, -1), (1, 1), (0, 1)))
        for i in range(4):
            for j in range(4):
                n, sign = R[i][j]
                v(V.tensor_scalar, right[i][:, j], qr[:, n], float(sign), None, ALU.mult)
        for i in range(4):
            for k in range(4):
                n, sign = L[i][k]
                left = qc[:, n].unsqueeze(1).to_broadcast([P, 4, QD])
                if k == 0:
                    v(V.tensor_tensor, coef[i], right[k], left, ALU.mult)
                else:
                    v(V.tensor_tensor, prod, right[k], left, ALU.mult)
                    v(V.tensor_tensor, coef[i], coef[i], prod, ALU.add if sign > 0 else ALU.subtract)
        for j in range(4):
            rows = slice(j % 2 * QD, (j % 2 + 1) * QD)
            for i in range(4):
                t_quat[:] = [v(V.tensor_tensor, quat[rows, j // 2, i * QD:(i + 1) * QD],
                               ident[rows, rows], coef[i][rows, j], ALU.mult)]
        ob = obm[:, :].rearrange("p (j d) -> p j d", d=QD)
        acc = pt[2][0:KB, 0:E].rearrange("p (i d) -> p i d", d=QD)
        v(V.tensor_copy, pt[2][0:KB, 0:E], obm[:, :])
        for i in range(4):
            v(V.tensor_tensor, prod[0:KB], ob, coef[i][0:KB], ALU.mult)
            for j in range(4):
                v(V.tensor_tensor, acc[:, i], acc[:, i], prod[0:KB, j], ALU.add)
        t = v(V.tensor_copy, obm[:, :], pt[2][0:KB, 0:E])
        t_obm[:] = [t]
        for i in range(len(pt)):
            probs.give(i, t)

    t_elim = [None]

    def gram():
        i, ps, free = misc.take()
        t = pe.do(T.matmul, ps[0:KB, 0:KB], raw[:, 0], raw[:, 0], start=True, stop=True, after=[t_small, *free])
        t = dve.do(V.scalar_tensor_tensor, elim[:, 0:KB], ident[0:KB, 0:KB], 1e-4, ps[0:KB, 0:KB], ALU.mult,
                   ALU.add, after=[t, t_id])
        misc.give(i, t)
        t_elim[0] = dve.do(V.tensor_copy, elim[:, KB:2 * KB], raw[:, 1], after=[t])

    def eliminate(j):
        i, ps, free = misc.take()
        t = pe.do(T.matmul, ps[0:KB, 0:2 * KB], ident[0:KB, j:j + 1].to_broadcast([KB, KB]), elim[:, :],
                  start=True, stop=True, after=[t_elim[0], t_id, *free])
        t = dve.do(V.reciprocal, pivot[:, 0:1], ps[0:KB, j:j + 1], after=[t])
        t = dve.do(V.scalar_tensor_tensor, pivot[:, 1:2], elim[:, j:j + 1], pivot[:, 0:1], below[:, j:j + 1],
                   ALU.mult, ALU.mult, after=[t, t_const])
        t_elim[0] = dve.do(V.scalar_tensor_tensor, elim[:, :], ps[0:KB, 0:2 * KB], pivot[:, 1:2], elim[:, :],
                           ALU.mult, ALU.add, after=[t])
        misc.give(i, t_elim[0])

    t_mtr = []

    def orthogonalise():
        def v(op, *args, **kw):
            return dve.do(op, *args, after=[dve.now()], **kw)

        v(V.tensor_tensor_reduce, below[:, :], elim[:, 0:KB], ident[0:KB, 0:KB], 1.0, 0.0, ALU.mult, ALU.add,
          pivot[:, 2:3])
        inverse_root(pivot[:, 4:5], pivot[:, 2:3], pivot[:, 3:4], dve.now())
        v(V.tensor_scalar, mtrT[:, :], elim[:, KB:2 * KB], pivot[:, 4:5], None, ALU.mult)
        v(V.tensor_tensor_reduce, below[:, :], mtrT[:, :], raw[:, 1], 1.0, 0.0, ALU.mult, ALU.add, pivot[:, 5:6])
        v(V.tensor_scalar, pivot[:, 6:7], pivot[:, 5:6], 0.0, 2.0, ALU.is_ge, ALU.mult)
        v(V.tensor_scalar, pivot[:, 7:8], pivot[:, 6:7], -1.0, None, ALU.add)
        t_mtr[:] = [v(V.tensor_scalar, mtrT[:, :], mtrT[:, :], pivot[:, 7:8], None, ALU.mult)]

    x1T_free, t_gate, t_run, cnt_free = [()], {}, [t_const], [()]
    gate_ps = {}

    def gate_logits(b):
        for k in range(KT):
            i, ps, free = misc.take()
            for st in range(ST):
                t = pe.do(T.transpose, ps[:, st * P:(st + 1) * P], xw[0][:, st, k * P:(k + 1) * P], ident[:, :],
                          mark=(st == ST - 1), after=[t_xw[b, 0], t_id, *free])
            t = act.do(A.activation, x1T[:, k, :], ps[:, :], ACT.Copy, after=[t, *x1T_free[0]])
            misc.give(i, t)
        for st in range(ST):
            j, jk, jfree = junks.take()
            t_s = dve.do(V.tensor_tensor_reduce, jk[:, 0:E], xw[0][:, st, 0:E], xw[0][:, st, 0:E], 1.0, 0.0,
                         ALU.mult, ALU.add, newton[:, 0, st:st + 1], after=[t_xw[b, 0], *jfree])
            junks.give(j, t_s)
        t_s = inverse_rms(newton, t_s)
        t_gate[b] = (t, t_s)

    def route(b):
        i, ps, free = misc.take()
        for st in range(ST):
            for k in range(KT):
                pe.do(T.matmul, ps[:, st * NX:(st + 1) * NX], x1T[:, k, st * P:(st + 1) * P], wg[:, k],
                      start=(k == 0), stop=(k == KT - 1), mark=False, after=[*t_gate[b], t_wg, *free])
        t = pe.do(T.matmul, ps[:, ST * NX:(ST + 1) * NX], condR[:, b:b + 1].to_broadcast([C + 2, P]), ggw[:, :],
                  start=True, stop=True, after=[t_small, t_const])
        x1T_free[0] = (t,)
        t_ps = t

        def v(op, *args, after=(), **kw):
            return dve.do(op, *args, after=[dve.now(), *after], **kw)

        def wide(a):
            return a.unsqueeze(2).to_broadcast([P, ST, NX])

        revs = rev.unsqueeze(1).to_broadcast([P, ST, NX])
        lg, ex, w, eq, oh = gt[:, 0], gt[:, 1], gt[:, 2], gt[:, 3], (gt[:, 4], gt[:, 5])
        v(V.tensor_copy, gt[:, 6, 0], ps[:, ST * NX:(ST + 1) * NX], after=[t_ps, t_flt])
        v(V.tensor_tensor, lg, ps[:, 0:ST * NX].rearrange("p (s x) -> p s x", x=NX), wide(newton[:, 3]), ALU.mult)
        t = v(V.tensor_tensor, lg, lg, gt[:, 6, 0].unsqueeze(1).to_broadcast([P, ST, NX]), ALU.add)
        misc.give(i, t)
        v(V.tensor_reduce, gs[:, 0], lg, AX.X, ALU.max)
        t = v(V.tensor_tensor, lg, lg, wide(gs[:, 0]), ALU.subtract)
        t = act.do(A.activation, ex, lg, ACT.Exp, after=[t])
        v(V.tensor_reduce, gs[:, 1], ex, AX.X, ALU.add, after=[t])
        v(V.reciprocal, gs[:, 2], gs[:, 1])
        v(V.tensor_tensor, w, ex, wide(gs[:, 2]), ALU.mult)
        for k in range(TOPK):
            v(V.tensor_reduce, gs[:, 3], w, AX.X, ALU.max)
            v(V.tensor_copy, xw[k][:, :, E], gs[:, 3], after=xw_free[k])
            v(V.tensor_copy, xw[k][:, :, E + 1].bitcast(I32), ints[:, n_tok + b * ST:n_tok + (b + 1) * ST])
            v(V.tensor_tensor, eq, w, wide(gs[:, 3]), ALU.is_equal)
            v(V.tensor_tensor, eq, eq, revs, ALU.mult)
            v(V.tensor_reduce, gs[:, 4 + k], eq, AX.X, ALU.max)
            v(V.tensor_tensor, oh[k], revs, wide(gs[:, 4 + k]), ALU.is_equal)
            if k == 0:
                v(V.scalar_tensor_tensor, w, oh[k], -2.0, w, ALU.mult, ALU.add)
        t = v(V.tensor_tensor, cnt[:, :, :], oh[0], oh[1], ALU.add, after=cnt_free[0])
        i, ps, free = misc.take()
        flat = cnt[:, :, :].rearrange("p s x -> p (s x)")
        pe.do(T.matmul, ps[:, 0:ST * NX], upper[:, :], flat, start=True, stop=True, mark=False,
              after=[t, t_const, *free])
        t = pe.do(T.matmul, ps[:, 64:64 + ST * NX], ones[:, :], flat, start=True, stop=True)
        cnt_free[0] = (t,)
        now, before = run[b % 2], run[(b + 1) % 2]
        v(V.tensor_copy, now[:, 0], before[:, ST], after=[t])
        for st in range(ST):
            v(V.tensor_tensor, now[:, st + 1], now[:, st], ps[:, 64 + st * NX:64 + (st + 1) * NX], ALU.add)
        slot = gt[:, 6]
        t = v(V.tensor_tensor, slot, now[:, 0:ST], ps[:, 0:ST * NX].rearrange("p (s x) -> p s x", x=NX), ALU.add)
        misc.give(i, t)
        v(V.tensor_tensor, slot, slot, first_row.unsqueeze(1).to_broadcast([P, ST, NX]), ALU.add)
        for k in range(TOPK):
            v(V.tensor_tensor, eq, oh[k], slot, ALU.mult)
            v(V.tensor_reduce, gs[:, 6], eq, AX.X, ALU.add)
            v(V.tensor_scalar, gs[:, 7], gs[:, 4 + k], 0.0, None, ALU.is_equal)
            t = v(V.scalar_tensor_tensor, idx[b % 2][:, k], gs[:, 7], flts[:, n_lost:n_lost + 1], gs[:, 6], ALU.mult,
                  ALU.add, after=idx_free.get(b - 2, ()))
        t_run[0] = t
        for k in range(TOPK):
            for st in range(ST):
                t_sc[k] = start_scatter(l_sc[k], pool, idx[b % 2][:, k, st:st + 1], xw[k][:, st, :],
                                                after=[t, t_xw[b, k]])
        xw_free[0] = (t_sc[0], t_x1[b])
        xw_free[1] = (t_sc[1],)
        idx_free[b] = tuple(t_sc)

    idx_free, t_sc = {}, [None, None]
    l_sc = [lane(f"scatter{k}") for k in range(TOPK)]

    def scatter_rows(index, src):
        return G.indirect_dma_start(routed, bass.IndirectOffsetOnAxis(ap=index, axis=0), src, None)

    def start_scatter(lane_, queue, index, src, after=()):
        queue.wait(*after)
        queue.steps.append((scatter_rows, (index, src), {}, lane_.sem, 16))
        lane_.count += 16
        return (lane_.sem, lane_.count)


    def project_steps(b):
        return [lambda qk=qk, half=half: project(b, qk, half) for qk in range(2) for half in range(2)]

    def value_steps(b):
        return [lambda: stack(b)] + [lambda st=st: project_v(b, st) for st in range(ST)]

    def finish_steps(b):
        return ([lambda: modulation(b)] + [lambda st=st: output_projection(b, st) for st in range(ST)]
                + [lambda: residual(b), lambda: gate_logits(b), lambda: route(b)])

    quaternions()
    for step in project_steps(0) + value_steps(0):
        step()
    side = [gram] + [lambda j=j: eliminate(j) for j in range(KB - 1)] + [orthogonalise]
    n_groups = B * NG
    todo = []
    for i in range(n_groups + 3):
        b = i // NG
        if i % NG == 0 and b + 1 < B:
            todo += project_steps(b + 1)
        if i % NG == 2:
            if b + 1 < B:
                todo += value_steps(b + 1)
            if 0 <= b - 1 < B:
                todo += finish_steps(b - 1)
        for k in range(ST):
            if i < n_groups:
                for st in range(ST):
                    row_maxima(i, k, st)
            if k == 0 and 0 <= i - 1 < n_groups:
                split_maxima(i - 1)
            if 0 <= i - 2 < n_groups:
                for hh in range(GH):
                    exponentials(i - 2, k, hh)
            g, kt = (i - 2, k - 1) if k else (i - 3, ST - 1)
            if 0 <= g < n_groups:
                weighted_values(g, kt)
            if k == 0 and 0 <= i - 3 < n_groups:
                normalise(i - 3)
            if k == 2 and 0 <= i - 1 < n_groups:
                maxima_rows(i - 1)
            for _ in range(2 if len(todo) > 8 else 1):
                if todo:
                    todo.pop(0)()
            if i >= 4 and side:
                side.pop(0)()
    while todo:
        todo.pop(0)()

    def v(op, *args, after=(), **kw):
        return dve.do(op, *args, after=[dve.now(), *after], **kw)

    counts = run[(B - 1) % 2][:, ST, :]
    v(V.tensor_scalar, tbi[:, :], counts, float(TW - 1), None, ALU.add, after=[t_run[0]])
    v(V.tensor_scalar, tbi[:, :], tbi[:, :], TW.bit_length() - 1, None, ALU.arith_shift_right)
    v(V.tensor_copy, tb[:, 0], tbi[:, :])
    v(V.tensor_copy, tb[:, 1], tb[:, 0])
    for n, step in enumerate((1, 2, 4)):
        v(V.tensor_copy, tb[:, 2 + n, 0:step], tb[:, 1 + n, 0:step])
        v(V.tensor_tensor, tb[:, 2 + n, step:], tb[:, 1 + n, step:], tb[:, 1 + n, :NX - step], ALU.add)
    end, base = tb[:, 4], tb[:, 5]
    v(V.tensor_tensor, base, end, tb[:, 0], ALU.subtract)
    tile_no = flts[:, n_tile:n_tile + NTILES]

    def over_tiles(a):
        return a.unsqueeze(1).to_broadcast([P, NTILES, NX])

    def over_experts(a):
        return a.unsqueeze(2).to_broadcast([P, NTILES, NX])

    expert, left8, first, chunk, used = (tv[:, n] for n in range(5))
    v(V.tensor_tensor, tj[:, 0], over_tiles(end), over_experts(tile_no), ALU.is_le)
    v(V.tensor_reduce, expert, tj[:, 0], AX.X, ALU.add)
    v(V.tensor_scalar, left8, expert, -1.0, float(NX), ALU.mult, ALU.add)
    v(V.tensor_tensor, tj[:, 1], over_tiles(rev), over_experts(left8), ALU.is_equal)
    v(V.tensor_tensor, tj[:, 0], tj[:, 1], over_tiles(base), ALU.mult)
    v(V.tensor_reduce, first, tj[:, 0], AX.X, ALU.add)
    v(V.tensor_tensor, chunk, tile_no, first, ALU.subtract)
    v(V.tensor_scalar, used, expert, float(NX), float(TW), ALU.is_lt, ALU.mult)
    v(V.tensor_tensor, chunk, chunk, used, ALU.mult)
    v(V.scalar_tensor_tensor, table[:, 0:NTILES], expert, float(REGION), chunk, ALU.mult, ALU.add)
    v(V.tensor_scalar, table[:, NTILES:2 * NTILES], expert, float(NX - 1), None, ALU.min)
    t_table = v(V.tensor_tensor, table[:, 2 * NTILES:], first_row, counts, ALU.add)

    l_pad = lane("pad")
    regs = {}

    def read_table(key, column, top):
        def op():
            regs[key] = nc.sync.value_load(table[0:1, column:column + 1], min_val=0, max_val=top)
        sp.steps.append((op, (), {}, None, 0))

    def dynamic(lane_, out, in_, after=()):
        sp.wait(*after)
        sp.steps.append((lambda: load(out(), in_()), (), {}, lane_.sem, 16))
        lane_.count += 16
        return (lane_.sem, lane_.count)

    sp.wait(t_table)
    for x in range(NX):
        read_table(("pad", x), 2 * NTILES + x, NULL_ROW - TW)
        dynamic(l_pad, lambda x=x: routed[bass.ds(regs["pad", x], TW), :].rearrange("(t p) c -> p t c", p=P),
                lambda: empty[:, :, :])
    l_pad.start(sp, load, routed[NULL_ROW:NULL_ROW + TW, :].rearrange("(t p) c -> p t c", p=P), empty[:, :, :])
    t_pad = l_pad.start(sp, load, x2_dram[B * S:, :].rearrange("(t p) c -> p t c", p=P), empty[:, :, 0:E])
    attention_done = [pe.now(), act.now(), dve.now(), pool.now(), t_x1[B - 1], *t_sc, t_pad]
    for q in (pe, act, dve, pool, sp):
        q.wait(*attention_done)

    phase[0].close()
    phase[0] = ExitStack()
    NW = 3
    HT = M // P
    wts = [sb(f"wts{i}", [P, (KT + HT) * M + HT * E]) for i in range(NW)]
    bias = [sb(f"bias{i}", [P, 2 * HT]) for i in range(NW)]
    bias3 = [sb(f"bias3_{i}", [P, E]) for i in range(NW)]
    rows = [sb(f"rows{i}", [P, TT, RW]) for i in range(NW)]
    rowsT = [sb(f"rowsT{i}", [P, KT, TW]) for i in range(2)]
    hid1 = [sb(f"hid1_{i}", [P, HT, TW]) for i in range(2)]
    hid2 = [sb(f"hid2_{i}", [P, HT, TW]) for i in range(2)]
    ysum = [sb(f"ysum{i}", [P, TT, E]) for i in range(2)]
    yout = [sb(f"yout{i}", [P, TT, E]) for i in range(2)]
    ab = [sb(f"ab{i}", [P, KT, E]) for i in range(B)]
    rcob = [sb(f"rcob{i}", [KB, 2, E]) for i in range(2)]
    l_wt = [lane(f"wts{i}") for i in range(NW)]
    l_row = [lane(f"rows{i}") for i in range(NW)]

    hidden = Ring(bank[0:4])
    outs = Ring(bank[4:6])
    turns = Ring(bank[6:8])
    t_wt, t_rows, wt_free, rows_free = {}, {}, {}, {}
    t_rT, rT_free, t_h1, h1_free, t_h2, h2_free, t_y, y_free = {}, {}, {}, {}, {}, {}, {}, {}

    def fetch(j):
        n = j % NW
        read_table(("row", j), j, NULL_ROW)
        t_rows[j] = dynamic(l_row[n], lambda: rows[n][:, :, :],
                            lambda: routed[bass.ds(regs["row", j], TW), :].rearrange("(t p) c -> p t c", p=P),
                            after=rows_free.get(j - NW, ()))
        read_table(("x", j), NTILES + j, NX - 1)
        o1, o2 = KT * M, (KT + HT) * M
        for dst, src, how in (
                (wts[n][:, 0:o1].rearrange("p (k m) -> p k m", m=M), d["W1"], "e (k p) m -> p (e k) m"),
                (wts[n][:, o1:o2].rearrange("p (k m) -> p k m", m=M), d["W2"], "e (k p) m -> p (e k) m"),
                (wts[n][:, o2:].rearrange("p (k m) -> p k m", m=E), d["W3"], "e (k p) m -> p (e k) m")):
            dynamic(l_wt[n], lambda dst=dst: dst,
                    lambda src=src, how=how: src[bass.ds(regs["x", j], 1)].rearrange(how, p=P),
                    after=wt_free.get(j - NW, ()))
        dynamic(l_wt[n], lambda: bias[n][:, :],
                lambda: d["b12"][bass.ds(regs["x", j], 1)].rearrange("e p c -> p (e c)"))
        t_wt[j] = dynamic(l_wt[n], lambda: bias3[n][:, :],
                          lambda: d["b3"][bass.ds(regs["x", j], 1)].to_broadcast([P, E]))

    def turn(j):
        i, ps, free = turns.take()
        for k in range(KT):
            for tt in range(TT):
                t = pe.do(T.transpose, ps[:, k * TW + tt * P:k * TW + (tt + 1) * P],
                          rows[j % NW][:, tt, k * P:(k + 1) * P], ident[:, :],
                          mark=(k == KT - 1 and tt == TT - 1), after=[t_rows[j], *free])
        t_rT[j] = act.do(A.activation, rowsT[j % 2][:, :, :].rearrange("p k t -> p (k t)"), ps[:, :], ACT.Copy,
                         after=[t, *rT_free.get(j - 2, ())])
        turns.give(i, t_rT[j])

    def layer1(j):
        for m in range(HT):
            i, ps, free = hidden.take()
            for k in range(KT):
                t = pe.do(T.matmul, ps[:, 0:TW], wts[j % NW][:, k * M + m * P:k * M + (m + 1) * P],
                          rowsT[j % 2][:, k, :], start=(k == 0), stop=(k == KT - 1), mark=(k == KT - 1),
                          after=[t_wt[j], t_rT[j], *free])
            t_h1[j, m] = act.do(A.activation, hid1[j % 2][:, m, :], ps[:, 0:TW], ACT.Relu,
                                bias=bias[j % NW][:, m:m + 1], after=[t, *h1_free.get(j - 2, ())])
            hidden.give(i, t_h1[j, m])
        rT_free[j] = (t,)

    def layer2(j):
        o1 = KT * M
        for m in range(HT):
            i, ps, free = hidden.take()
            for k in range(HT):
                t = pe.do(T.matmul, ps[:, 0:TW], wts[j % NW][:, o1 + k * M + m * P:o1 + k * M + (m + 1) * P],
                          hid1[j % 2][:, k, :], start=(k == 0), stop=(k == HT - 1), mark=(k == HT - 1),
                          after=[t_h1[j, k], *free])
            t_h2[j, m] = dve.do(V.tensor_scalar, hid2[j % 2][:, m, :], ps[:, 0:TW],
                                bias[j % NW][:, HT + m:HT + m + 1], 0.0, ALU.add, ALU.max,
                                after=[t, *h2_free.get(j - 2, ())])
            hidden.give(i, t_h2[j, m])
        h1_free[j] = (t,)

    l_add = lane("add")
    t_add = [None]

    def add_rows(index, src):
        return G.indirect_dma_start(x2_dram, bass.IndirectOffsetOnAxis(ap=index, axis=0), src, None,
                                    compute_op=ALU.add)

    def layer3(j):
        o2 = (KT + HT) * M
        for tt in range(TT):
            i, ps, free = outs.take()
            for k in range(HT):
                t = pe.do(T.matmul, ps[:, 0:E], hid2[j % 2][:, k, tt * P:(tt + 1) * P],
                          wts[j % NW][:, o2 + k * E:o2 + (k + 1) * E], start=(k == 0), stop=(k == HT - 1),
                          mark=(k == HT - 1), after=[t_h2[j, k], *free])
            t_b = dve.do(V.tensor_tensor, ysum[j % 2][:, tt], ps[:, 0:E], bias3[j % NW][:, :], ALU.add,
                         after=[t, *y_free.get(j - 2, ())])
            outs.give(i, t_b)
            t_w = act.do(A.activation, yout[j % 2][:, tt], ysum[j % 2][:, tt], ACT.Copy,
                         scale=rows[j % NW][:, tt, E:E + 1], after=[t_b, *y_free.get(j - 2, ())])
            pool.wait(t_w, *([t_add[0]] if t_add[0] else []))
            pool.steps.append((add_rows, (rows[j % NW][:, tt, E + 1:E + 2].bitcast(U32), yout[j % 2][:, tt]), {},
                               l_add.sem, 16))
            l_add.count += 16
            t_add[0] = (l_add.sem, l_add.count)
        h2_free[j] = (t,)
        wt_free[j] = (t, t_b, *[t_h1[j, HT - 1]], *[t_h2[j, HT - 1]])
        y_free[j] = (t_add[0], t_w)
        rows_free[j] = (t_add[0], t_w)
        if j + NW < NTILES:
            fetch(j + NW)

    def combined(b):
        r = rcob[b % 2]
        t = dve.do(V.tensor_scalar, r[:, 0], obm[:, :], cond_cols[:, 1, b:b + 1], None, ALU.mult,
                   after=[*t_obm, t_small, *rc_free.get(b - 2, ())])
        i, ps, free = turns.take()
        t = pe.do(T.matmul, ps[0:KB, 0:E], mtrT[:, :], r[:, 0], start=True, stop=True, after=[t, *t_mtr, *free])
        t = act.do(A.activation, r[:, 1], ps[0:KB, 0:E], ACT.Copy, scale=cond_cols[:, 0, b:b + 1],
                   after=[t, *rc_free.get(b - 2, ())])
        turns.give(i, t)
        i, ps, free = turns.take()
        for k in range(KT):
            t = pe.do(T.matmul, ps[:, k * E:(k + 1) * E], basis[:, k * P:(k + 1) * P], r[:, 1], start=True, stop=True,
                      after=[t, *free])
        rc_free[b] = (t,)
        t_ab[b] = dve.do(V.tensor_tensor, ab[b][:, :, :].rearrange("p k e -> p (k e)"), ps[:, :],
                         quat[:, :, :].rearrange("p k e -> p (k e)"), ALU.add, after=[t, *t_quat])
        turns.give(i, t_ab[b])

    t_ab, rc_free = {}, {}
    for j in range(NW):
        fetch(j)
    for b in range(B):
        combined(b)
    turn(0)
    layer1(0)
    turn(1)
    for j in range(NTILES):
        layer2(j)
        if j + 1 < NTILES:
            layer1(j + 1)
        layer3(j)
        if j + 2 < NTILES:
            turn(j + 2)

    NL = 4
    x2b = [sb(f"x2b{i}", [P, ST, E]) for i in range(NL)]
    x2T = [sb(f"x2T{i}", [P, KT, S]) for i in range(2)]
    fin = [sb(f"fin{i}", [P, ST, E]) for i in range(2)]
    l_x2 = [lane(f"x2_{i}") for i in range(NL)]
    l_out = [lane(f"out{i}") for i in range(2)]
    t_x2, x2_free, x2T_free, t_out, fin_free = {}, {}, {}, {}, {}

    def load_x2(b):
        t_x2[b] = l_x2[b % NL].start(sp, load, x2b[b % NL][:, :, :],
                                     x2_dram[b * S:(b + 1) * S, :].rearrange("(j p) e -> p j e", p=P),
                                     after=[t_add[0], *x2_free.get(b - NL, ())])

    for b in range(NL):
        load_x2(b)
    for b in range(B):
        t_T = []
        for k in range(KT):
            i, ps, free = turns.take()
            for st in range(ST):
                t = pe.do(T.transpose, ps[:, st * P:(st + 1) * P], x2b[b % NL][:, st, k * P:(k + 1) * P], ident[:, :],
                          mark=(st == ST - 1), after=[t_x2[b], *free])
            t = act.do(A.activation, x2T[b % 2][:, k, :], ps[:, :], ACT.Copy, after=[t, *x2T_free.get(b - 2, ())])
            turns.give(i, t)
            t_T.append(t)
        for st in range(ST):
            i, ps, free = hidden.take()
            for k in range(KT):
                t = pe.do(T.matmul, ps[:, 0:E], x2T[b % 2][:, k, st * P:(st + 1) * P], ab[b][:, k, :],
                          start=(k == 0), stop=(k == KT - 1), mark=(k == KT - 1), after=[t_T[k], t_ab[b], *free])
            t_f = dve.do(V.tensor_tensor, fin[b % 2][:, st], ps[:, 0:E], x2b[b % NL][:, st], ALU.add,
                         after=[t, *fin_free.get(b - 2, ())])
            hidden.give(i, t_f)
        x2T_free[b] = (t,)
        x2_free[b] = (t_f,)
        if b + NL < B:
            load_x2(b + NL)
        t_out[b] = l_out[b % 2].start(sp, load, out[b * S:(b + 1) * S, :].rearrange("(j p) e -> p j e", p=P),
                                      fin[b % 2][:, :, :], after=[t_f])
        fin_free[b] = (t_out[b],)
    sp.wait(t_out[B - 2], t_out[B - 1])
    outer.enter_context(phase[0])

    block = ctx.enter_context(nc.Block())
    for name, q in (("sync", sp), ("scalar", act), ("vector", dve), ("gpsimd", pool), ("tensor", pe)):
        deco = {"sync": block.sync, "scalar": block.scalar, "vector": block.vector, "gpsimd": block.gpsimd,
                "tensor": block.tensor}[name]
        deco(q.emit)


def kernel(**inputs):
    import concourse.bacc as bacc
    from concourse.bass_utils import run_bass_kernel_spmd
    nc = bacc.Bacc("TRN2", target_bir_lowering=False, num_devices=1)
    a = {n: np.asarray(v) for n, v in inputs.items()}
    x = a["x"].reshape(B * S, E)
    mask = a["mask_SxS_bk1"]

    def columns(b):
        return b.reshape(NX, M // P, P).transpose(0, 2, 1)

    arrays = {
        "x": x, "xT": x.T, "mask": mask, "maskT": mask.T,
        "cond": a["cond_256"], "condT": a["cond_256"].T, "cond64T": a["cond_64"].T,
        "WqT": a["L0_cond_Wq"].T, "WkT": a["L0_cond_Wk"].T, "WvT": a["L0_cond_Wv"].T, "WoT": a["L0_cond_Wo"].T,
        "rms_scale": a["L0_cond_rms_scale"], "WcT": a["L0_cond_Wc"].T, "bc": a["L0_cond_bc"],
        "rms_w": a["L1_cond_rms_w"].reshape(KT, P).T, "wg_W": a["L1_cond_wg_W"], "wg_b": a["L1_cond_wg_b"],
        "gg_W": a["L1_cond_gg_W"], "gg_b": a["L1_cond_gg_b"],
        "W1": a["L1_cond_W1"], "W2": a["L1_cond_W2"], "W3": a["L1_cond_W3"],
        "b12": np.concatenate([columns(a["L1_cond_b1"]), columns(a["L1_cond_b2"])], axis=2), "b3": a["L1_cond_b3"],
        "input_basis": a["L2_cond_input_basis"], "mtr": a["L2_cond_mode_to_rank"],
        "mtrT": a["L2_cond_mode_to_rank"].T, "output_basis": a["L2_cond_output_basis"],
        "q_right": a["L3_cond_q_right"], "gate": a["L3_cond_spectral_gate"].reshape(-1),
    }
    arrays = {"in_" + n: np.ascontiguousarray(v) for n, v in arrays.items()}
    d = {n[3:]: nc.dram_tensor(n, v.shape, mybir.dt.from_np(v.dtype), kind="ExternalInput").ap()
         for n, v in arrays.items()}
    out = nc.dram_tensor("out", (B * S, E), F32, kind="ExternalOutput").ap()
    build(nc, d, out)
    r = run_bass_kernel_spmd(nc, [arrays], core_ids=[0])
    return r.results[0]["out"].reshape(B, S, E)
```

```python
import numpy as np
from contextlib import ExitStack
import concourse.bass as bass
import concourse.mybir as mybir

F32 = mybir.dt.float32
BF16 = mybir.dt.bfloat16
U8 = mybir.dt.uint8
I32 = mybir.dt.int32
U32 = mybir.dt.uint32
ALU = mybir.AluOpType
ACT = mybir.ActivationFunctionType
AX = mybir.AxisListType

P = 128
B, S, E = 8, 512, 256
H = 16
D = E // H
C = 64
NX = 8
M = 512
KT = E // P
ST = S // P
NT = B * ST
GH = 4
NG = H // GH
PARTS = 3
PAIRS = [(0, 0), (1, 0), (0, 1), (1, 1), (0, 2), (2, 0)]
KQ = len(PAIRS) * D
MASKED = -3.0e38
FLOOR = -1.0e38


TW = 256
TT = TW // P
TOPK = 2
NTILES = B * S * TOPK // TW + NX - 1
REGION = B * S + TW
NULL_ROW = NX * REGION
LOST_ROW = NULL_ROW + TW
RW = E + 2
KB = 64
BETA = 3


class Engine:

    def __init__(self, sem):
        self.sem, self.count, self.steps, self.passed = sem, 0, [], {}

    def wait(self, *tokens):
        for sem, value in tokens:
            if value > self.passed.get(sem.name, 0):
                self.passed[sem.name] = value
                self.steps.append((None, sem, value))

    def do(self, op, *args, after=(), mark=True, **kw):
        self.wait(*after)
        self.steps.append((op, args, kw, self.sem if mark else None, 1))
        self.count += mark
        return (self.sem, self.count)

    def now(self):
        return (self.sem, self.count)

    def emit(self, engine):
        for step in self.steps:
            if step[0] is None:
                engine.wait_ge(step[1], step[2])
            else:
                op, args, kw, sem, n = step
                ins = op(*args, **kw)
                if sem is not None:
                    ins.then_inc(sem, n)


class Lane:

    def __init__(self, sem):
        self.sem, self.count = sem, 0

    def start(self, queue, op, out, in_, after=()):
        queue.wait(*after)
        queue.steps.append((op, (out, in_), {}, self.sem, 16))
        self.count += 16
        return (self.sem, self.count)


class Ring:

    def __init__(self, bufs):
        self.bufs, self.free, self.n = bufs, [()] * len(bufs), 0

    def take(self):
        i = self.n % len(self.bufs)
        self.n += 1
        return i, self.bufs[i], self.free[i]

    def give(self, i, *tokens):
        self.free[i] = tokens


def build(nc, d, out):
    with ExitStack() as ctx:
        _build(nc, ctx, d, out)


def _build(nc, ctx, d, out):
    outer, phase = ctx, [ExitStack()]

    def sb(name, shape, dt=F32):
        return phase[0].enter_context(nc.sbuf_tensor(name, shape, dt))

    def sem(name):
        return ctx.enter_context(nc.semaphore(name))

    def lane(name):
        return Lane(sem("dma_" + name))

    pe, act, dve, pool, sp = (Engine(sem("progress_" + n)) for n in ("pe", "act", "dve", "pool", "sp"))
    V, A, G, T = nc.vector, nc.scalar, nc.gpsimd, nc.tensor
    load = nc.sync.dma_start

    bank = [ctx.enter_context(nc.psum_tensor(f"bank{i}", [P, 512], F32)) for i in range(8)]

    def lasting(name, shape, dt=F32):
        return outer.enter_context(nc.sbuf_tensor(name, shape, dt))

    ident = lasting("ident", [P, P])
    empty = lasting("empty", [P, TT, RW])
    table = lasting("table", [P, 2 * NTILES + NX], I32)
    mtrT = lasting("mtrT", [KB, KB])
    obm = lasting("obm", [KB, E])
    basis = lasting("basis", [KB, E])
    quat = lasting("quat", [P, KT, E])
    cond_cols = lasting("cond_cols", [C, 2, B])
    below = lasting("below", [KB, KB])
    elim = lasting("elim", [KB, 2 * KB])
    raw = lasting("raw", [KB, 2, KB])
    pivot = lasting("pivot", [KB, 8])

    identb = sb("identb", [P, P], BF16)
    upper = sb("upper", [P, P], BF16)
    ones = sb("ones", [P, P], BF16)
    xw = [sb(f"xw{i}", [P, ST, RW]) for i in range(TOPK)]
    x1T = sb("x1T", [P, KT, S])
    wg = sb("wg", [P, KT, NX])
    rmsw = sb("rmsw", [P, KT])
    ggw = sb("ggw", [C + 2, NX])
    condR = sb("condR", [C + 2, B])
    newton = sb("newton", [P, 4, ST])
    ints = sb("ints", [P, 2 * NX + NT + 1 + NTILES], I32)
    flts = sb("flts", [P, 2 * NX + NT + 1 + NTILES])
    gt = sb("gt", [P, 8, ST, NX])
    gs = sb("gs", [P, 8, ST])
    cnt = sb("cnt", [P, ST, NX], BF16)
    logits = sb("logits", [P, ST + 1, NX])
    ranks = sb("ranks", [P, 2 * ST, NX])
    run = [sb(f"run{i}", [P, ST + 1, NX]) for i in range(2)]
    idx = [sb(f"idx{i}", [P, TOPK, ST], U32) for i in range(2)]
    tb = sb("tb", [P, 10, NX])
    tbi = sb("tbi", [P, NX], I32)
    x1T_flat = x1T[:, :, :].rearrange("p k s -> p (k s)")
    tj = x1T_flat[:, 0:2 * NTILES * NX].rearrange("p (a t x) -> p a t x", a=2, x=NX)
    tv = x1T_flat[:, 2 * NTILES * NX:(2 * NX + 6) * NTILES].rearrange("p (a t) -> p a t", a=6)

    wqk = sb("wqk", [P, 2, KT, E])
    wv = sb("wv", [P, KT, E])
    wo = sb("wo", [P, NG // 2, E])
    mneg = sb("mneg", [P, 2, ST, S], BF16)
    xT = [sb(f"xT{i}", [P, KT, S]) for i in range(2)]
    xin = [sb(f"xin{i}", [P, ST, E]) for i in range(2)]
    parts = [sb(f"parts{i}", [P, 2, PARTS, S], BF16) for i in range(2)]
    rest = [sb(f"rest{i}", [P, S]) for i in range(2)]
    qst = [sb(f"qst{i}", [P, H, S], BF16) for i in range(2)]
    kst = [sb(f"kst{i}", [P, H, S], BF16) for i in range(2)]
    vaug = [sb(f"vaug{i}", [P, ST, H, 32]) for i in range(2)]
    junk = [sb(f"junk{i}", [P, S], BF16) for i in range(2)]
    rowmax = [sb(f"rowmax{i}", [P, GH, ST]) for i in range(2)]
    negm = [sb(f"negm{i}", [P, 2, GH, ST]) for i in range(2)]
    m3 = [sb(f"m3_{i}", [P, ST, GH, PARTS], BF16) for i in range(2)]
    mrow = [sb(f"mrow{i}", [GH * PARTS, S], BF16) for i in range(2)]
    pt = [sb(f"pt{i}", [P, S]) for i in range(8)]
    turned = [sb(f"turned{i}", [P, 16, 32]) for i in range(2)]
    rden = [sb(f"rden{i}", [P, 16]) for i in range(2)]
    oT = [sb(f"oT{i}", [P, NG // 2, S]) for i in range(2)]
    osb = sb("osb", [P, ST, E])
    mask8 = osb[:, :, :].rearrange("p s e -> p (s e)").bitcast(U8).rearrange("p (a s t) -> p a s t", a=2, s=ST)
    ssq = sb("ssq", [P, 4, ST])
    condS = sb("condS", [C + 1, B])
    condw = sb("condw", [C, 3, B])
    wc = sb("wc", [C + 1, 2 * E])
    rmsb = sb("rmsb", [P, E])
    gain = [sb(f"gain{i}", [P, E]) for i in range(2)]
    shift = [sb(f"shift{i}", [P, E]) for i in range(2)]

    x_dram, xT_dram = d["x"], d["xT"]
    split_dram = nc.dram_tensor("split_parts", (B, 2, PARTS, H // 8 * P, S), BF16, kind="Internal").ap()

    l_w = lane("weights")
    t_w = None
    for i, n in enumerate(("WqT", "WkT")):
        l_w.start(sp, load, wqk[:, i], d[n].rearrange("(k p) e -> p k e", p=P))
    t_w = l_w.start(sp, load, wv[:, :, :], d["WvT"].rearrange("(k p) e -> p k e", p=P))
    l_x = [lane(f"xT{i}") for i in range(2)]
    l_xin = [lane(f"xin{i}") for i in range(2)]
    t_xT, t_xin = {}, {}
    last_x_use = {}

    def load_x(b):
        free = last_x_use.get(b - 2, ())
        t_xT[b] = l_x[b % 2].start(sp, load, xT[b % 2][:, :, :],
                                   xT_dram[:, b * S:(b + 1) * S].rearrange("(k p) s -> p k s", p=P), after=free)

    last_xin_use = {}

    def load_xin(b):
        t_xin[b] = l_xin[b % 2].start(sp, load, xin[b % 2][:, :, :],
                                      x_dram[b * S:(b + 1) * S, :].rearrange("(j p) e -> p j e", p=P),
                                      after=last_xin_use.get(b - 2, ()))

    load_x(0)
    l_m = lane("masks")
    l_m.start(sp, load, mask8[:, 0], d["mask"].rearrange("(j p) t -> p j t", p=P))
    t_mask = l_m.start(sp, load, mask8[:, 1], d["maskT"].rearrange("(j p) t -> p j t", p=P))
    l_c = lane("conditioning")
    l_c.start(sp, load, condw[:, 0], d["condT"])
    l_c.start(sp, load, wc[0:C], d["WcT"])
    l_c.start(sp, load, wc[C:C + 1], d["bc"].unsqueeze(0))
    t_c = l_c.start(sp, load, rmsb[:, :], d["rms_scale"].unsqueeze(0).to_broadcast([P, E]))

    t_id0 = pool.do(G.memset, ident[:, :], 0.0)
    t_id = pool.do(G.affine_select, out=ident[:, :], in_=ident[:, :], compare_op=ALU.not_equal, fill=1.0,
                   base=0, pattern=[[-1, P]], channel_multiplier=1, after=[t_id0])
    t_zero = []
    for i in range(2):
        t = pool.do(G.memset, vaug[i][:, :, :, D:32], 0.0, after=[pool.now()])
        t_zero.append(pool.do(G.memset, vaug[i][:, :, :, D:D + 1], 1.0, after=[t]))
        pool.do(G.memset, kst[i][KQ:KQ + PARTS, :, :], 1.0, after=[pool.now()])
    t_kones = pool.now()
    t_cond1 = pool.do(G.memset, condS[C:C + 1, :], 1.0, after=[pool.now()])
    l_wo = lane("wo")
    for g in range(GH):
        for u in range(2):
            t_wo = l_wo.start(sp, load, wo[32 * g + D * u:32 * g + D * u + D],
                              d["WoT"].rearrange("(G u g d) e -> g u d G e", u=2, g=GH, d=D)[g, u])
    load_x(1)
    load_xin(0)

    l_s = lane("small")
    for dst, src in ((wg[:, :, :], d["wg_W"].rearrange("(k p) x -> p k x", p=P)),
                     (rmsw[:, :], d["rms_w"]),
                     (ggw[0:C], d["gg_W"]), (ggw[C:C + 1], d["gg_b"].unsqueeze(0)),
                     (ggw[C + 1:C + 2], d["wg_b"].unsqueeze(0)), (condR[0:C], d["condT"]),
                     (cond_cols[:, 0], d["condT"]), (cond_cols[:, 1], d["cond64T"]),
                     (raw[:, 0], d["mtr"]), (raw[:, 1], d["mtrT"]), (basis[:, :], d["input_basis"]),
                     (obm[:, :], d["output_basis"])):
        t_small = l_s.start(sp, load, dst, src)

    def constant(op, *args, **kw):
        return pool.do(op, *args, after=[pool.now()], **kw)

    n_rev, n_base, n_tok, n_lost, n_tile = 0, NX, 2 * NX, 2 * NX + NT, 2 * NX + NT + 1
    constant(G.iota, ints[:, n_rev:n_rev + NX], [[-1, NX]], base=NX, channel_multiplier=0)
    constant(G.iota, ints[:, n_base:n_base + NX], [[REGION, NX]], base=0, channel_multiplier=0)
    constant(G.iota, ints[:, n_tok:n_tok + NT], [[P, NT]], base=0, channel_multiplier=1)
    constant(G.iota, ints[:, n_lost:n_lost + 1], [[1, 1]], base=LOST_ROW, channel_multiplier=1)
    constant(G.iota, ints[:, n_tile:n_tile + NTILES], [[1, NTILES]], base=0, channel_multiplier=0)
    constant(G.iota, empty[:, :, E + 1].bitcast(I32), [[P, TT]], base=B * S, channel_multiplier=1)
    constant(G.memset, empty[:, :, 0:E + 1], 0.0)
    constant(G.memset, condR[C:C + 2, :], 1.0)
    constant(G.memset, ones[:, :], 1.0)
    constant(G.memset, run[1][:, ST, :], 0.0)
    constant(G.affine_select, out=upper[:, :], in_=ones[:, :], compare_op=ALU.is_gt, fill=0.0, base=0,
             pattern=[[1, P]], channel_multiplier=-1)
    constant(G.memset, below[:, :], -1.0)
    t_const = constant(G.affine_select, out=below[:, :], in_=below[:, :], compare_op=ALU.is_gt, fill=0.0,
                       base=0, pattern=[[-1, KB]], channel_multiplier=1)
    t_flt = dve.do(V.tensor_copy, flts[:, :], ints[:, :], after=[t_const])
    rev, first_row = flts[:, n_rev:n_rev + NX], flts[:, n_base:n_base + NX]
    t_wg = None
    for k in range(KT):
        t_wg = dve.do(V.tensor_scalar, wg[:, k], wg[:, k], rmsw[:, k:k + 1], None, ALU.mult, after=[t_small])

    t_idb = dve.do(V.tensor_copy, identb[:, :], ident[:, :], after=[t_id])
    t_mn = dve.do(V.tensor_scalar, mneg[:, 0], mask8[:, 0], MASKED, None, ALU.mult, after=[t_mask])
    t_mn = dve.do(V.tensor_scalar, mneg[:, 1], mask8[:, 1], MASKED, None, ALU.mult)

    t_e = act.do(A.activation, condw[:, 1], condw[:, 0], ACT.Exp, scale=-1.0, after=[t_c])
    t = dve.do(V.tensor_scalar, condw[:, 2], condw[:, 1], 1.0, None, ALU.add, after=[t_e])
    t = dve.do(V.reciprocal, condw[:, 1], condw[:, 2], after=[t])
    t = dve.do(V.tensor_tensor, condS[0:C], condw[:, 0], condw[:, 1], ALU.mult, after=[t])
    t_cs = t

    row_scores = Ring(bank[0:2])
    col_scores = Ring(bank[2:5])
    misc = Ring(bank[6:8])
    av_bank, av_free = bank[5], [()]
    probs = Ring(pt)
    junks = Ring(junk)
    rests = Ring(rest)

    l_parts = [lane(f"parts{i}") for i in range(2)]
    l_stack = [lane(f"stack{i}") for i in range(2)]
    l_mrow = [lane(f"mrow{i}") for i in range(2)]
    parts_free = [(), ()]
    t_parts, t_stack, t_v = {}, {}, {}
    stack_free = {}
    v_free = {}

    def project(b, qk, half):
        i, ps, free = misc.take()
        for k in range(KT):
            t = pe.do(T.matmul, ps[:, :], wqk[:, qk, k, half * P:(half + 1) * P], xT[b % 2][:, k, :],
                      start=(k == 0), stop=(k == KT - 1), mark=(k == KT - 1), after=[t_w, t_xT[b], *free])
        pp = parts[qk]
        hi, mid, lo = (pp[:, half, n, :] for n in range(PARTS))
        t_hi = act.do(A.activation, hi, ps[:, :], ACT.Copy, after=[t, *parts_free[qk]])
        r, left, rfree = rests.take()
        t_r = dve.do(V.tensor_tensor, left[:, :], ps[:, :], hi, ALU.subtract, after=[t, t_hi, *rfree])
        misc.give(i, t_r)
        t_mid = act.do(A.activation, mid, left[:, :], ACT.Copy, after=[t_r])
        t_lo = pool.do(G.tensor_tensor, lo, left[:, :], mid, ALU.subtract, after=[t_mid])
        rests.give(r, t_lo)
        t_out = l_parts[qk].start(sp, load, split_dram[b, qk][:, half * P:(half + 1) * P, :].rearrange("n p s -> p n s"),
                                  pp[:, half], after=[t_lo])
        t_parts[b, qk] = t_out
        if half == 1:
            parts_free[qk] = (t_out,)

    def stack(b):
        for qk in range(2):
            dst = (qst, kst)[qk][b % 2]
            for r, pair in enumerate(PAIRS):
                t_stack[b, qk] = l_stack[qk].start(
                    sp, load, dst[r * D:(r + 1) * D, :, :],
                    split_dram[b, qk, pair[qk]].rearrange("(h d) s -> d h s", d=D),
                    after=[t_parts[b, qk], *(stack_free[b - 2] if b >= 2 else ())])

    def project_v(b, st):
        i, ps, free = misc.take()
        for k in range(KT):
            t = pe.do(T.matmul, ps[:, 0:E], xT[b % 2][:, k, st * P:(st + 1) * P], wv[:, k, :],
                      start=(k == 0), stop=(k == KT - 1), mark=(k == KT - 1), after=[t_w, t_xT[b], *free])
        t_v[b] = act.do(A.activation, vaug[b % 2][:, st, :, 0:D], ps[:, 0:E].rearrange("p (h d) -> p h d", d=D),
                        ACT.Copy, after=[t, *v_free.get(b - 2, ())])
        misc.give(i, t_v[b])
        if st == ST - 1:
            last_x_use[b] = (t,)
            if b + 2 < B:
                load_x(b + 2)

    t_gain, gain_free = {}, {}

    def modulation(b):
        i, ps, free = misc.take()
        t = pe.do(T.matmul, ps[:, :], condS[:, b:b + 1].to_broadcast([C + 1, P]), wc[:, :], start=True, stop=True,
                  after=[t_cs, t_cond1, t_c, *free])
        t_s = act.do(A.activation, shift[b % 2][:, :], ps[:, 0:E], ACT.Copy, after=[t, *gain_free.get(b - 2, ())])
        t_g = dve.do(V.scalar_tensor_tensor, gain[b % 2][:, :], ps[:, E:2 * E], 1.0, rmsb[:, :], ALU.add, ALU.mult,
                     after=[t_s, *gain_free.get(b - 2, ())])
        misc.give(i, t_s, t_g)
        t_gain[b] = (t_s, t_g)

    t_max, max_free, t_m3, m3_free, mrow_free, t_mrow = {}, {}, {}, {}, {}, {}

    def row_maxima(gi, hh, st):
        b, h = gi // NG, gi % NG * GH + hh
        i, ps, free = row_scores.take()
        t = pe.do(T.matmul, ps[:, :], qst[b % 2][0:KQ, h, st * P:(st + 1) * P], kst[b % 2][0:KQ, h, :],
                  start=True, stop=True, after=[t_stack[b, 0], t_stack[b, 1], *free])
        j, jk, jfree = junks.take()
        t_max[gi] = dve.do(V.tensor_tensor_reduce, jk[:, :], ps[:, :], mneg[:, 0, st, :], 1.0, FLOOR, ALU.add,
                           ALU.max, rowmax[gi % 2][:, hh, st:st + 1], after=[t, *jfree, *max_free.get(gi - 2, ())])
        junks.give(j, t_max[gi])
        row_scores.give(i, t_max[gi])

    def split_maxima(gi):
        n, dst = negm[gi % 2], m3[gi % 2]
        v = [dst[:, :, :, k].rearrange("p s h -> p h s") for k in range(PARTS)]
        t = pool.do(G.tensor_scalar, n[:, 0], rowmax[gi % 2][:, :, :], -1.0, None, ALU.mult, after=[t_max[gi]])
        max_free[gi] = (t,)
        t = pool.do(G.tensor_copy, v[0], n[:, 0], after=[t, *m3_free.get(gi - 2, ())])
        t = pool.do(G.tensor_tensor, n[:, 1], n[:, 0], v[0], ALU.subtract, after=[t])
        t = pool.do(G.tensor_copy, v[1], n[:, 1], after=[t])
        t_m3[gi] = pool.do(G.tensor_tensor, v[2], n[:, 1], v[1], ALU.subtract, after=[t])

    def maxima_rows(gi):
        i, ps, free = misc.take()
        for st in range(ST):
            t = pe.do(T.matmul, ps[0:GH * PARTS, st * P:(st + 1) * P],
                      m3[gi % 2][:, st].rearrange("p h n -> p (h n)"), identb[:, :], start=True, stop=True,
                      mark=(st == ST - 1), after=[t_m3[gi], t_idb, *free])
        m3_free[gi] = (t,)
        t = act.do(A.activation, mrow[gi % 2][:, :], ps[0:GH * PARTS, :], ACT.Copy,
                   after=[t, *mrow_free.get(gi - 2, ())])
        misc.give(i, t)
        b = gi // NG
        for hh in range(GH):
            h = gi % NG * GH + hh
            t_mrow[gi] = l_mrow[gi % 2].start(sp, load, qst[b % 2][KQ:KQ + PARTS, h, :],
                                              mrow[gi % 2][hh * PARTS:(hh + 1) * PARTS, :],
                                              after=[t, *stack_free.get(b - 2, ())])
        mrow_free[gi] = (t_mrow[gi],)

    t_prob = {}

    def exponentials(gi, kt, hh):
        b, h = gi // NG, gi % NG * GH + hh
        i, ps, free = col_scores.take()
        t = pe.do(T.matmul, ps[:, :], kst[b % 2][0:KQ + PARTS, h, kt * P:(kt + 1) * P],
                  qst[b % 2][0:KQ + PARTS, h, :], start=True, stop=False, mark=False,
                  after=[t_mrow[gi], t_kones, *free])
        t = pe.do(T.matmul, ps[:, :], identb[:, :], mneg[:, 1, kt, :], start=False, stop=True, after=[t_mn])
        if gi % NG == NG - 1 and kt == ST - 1 and hh == GH - 1:
            stack_free[b] = (t,)
        j, pr, pfree = probs.take()
        t = act.do(A.activation, pr[:, :], ps[:, :], ACT.Exp, scale=float(D) ** -0.5, after=[t, *pfree])
        col_scores.give(i, t)
        t_prob[gi, kt, hh] = (j, pr, t)

    t_av = {}

    def weighted_values(gi, kt):
        b = gi // NG
        js = []
        for hh in range(GH):
            h = gi % NG * GH + hh
            j, pr, tp = t_prob.pop((gi, kt, hh))
            js.append(j)
            t = pe.do(T.matmul, av_bank[32 * hh:32 * hh + 32, :], vaug[b % 2][:, kt, h, :], pr[:, :],
                      start=(kt == 0), stop=(kt == ST - 1), mark=(hh == GH - 1),
                      after=[tp, t_v[b], t_zero[b % 2], *(av_free[0] if kt == 0 else ())])
        for j in js:
            probs.give(j, t)
        t_av[gi] = t
        if gi % NG == NG - 1 and kt == ST - 1:
            v_free[b] = (t,)

    t_oT, turned_free, oT_free = {}, [(), ()], {}

    def normalise(gi):
        b, u, tn, rd = gi // NG, gi % 2, turned[gi % 2], rden[gi % 2]
        t = dve.do(V.transpose, tn[:, :, :].rearrange("p a c -> p (a c)"), av_bank[:, :],
                   after=[t_av[gi], *turned_free[u]])
        av_free[0] = (t,)
        t = dve.do(V.reciprocal, rd[:, :], tn[:, :, D], after=[t])
        t_n = dve.do(V.tensor_tensor, turned[0][:, :, u * D:(u + 1) * D], tn[:, :, 0:D],
                     rd[:, :].unsqueeze(2).to_broadcast([P, 16, D]), ALU.mult, after=[t])
        if u:
            t_oT[gi // 2] = dve.do(V.transpose, oT[b % 2][:, gi % NG // 2, :],
                                   turned[0][:, :, :].rearrange("p a c -> p (a c)"),
                                   after=[t_n, *oT_free.get(b - 2, ())])
            turned_free[0], turned_free[1] = (t_oT[gi // 2],), (t_n,)

    osb_free = [()]
    t_osb = {}

    def output_projection(b, st):
        i, ps, free = misc.take()
        for g in range(NG // 2):
            t = pe.do(T.matmul, ps[:, 0:E], oT[b % 2][:, g, st * P:(st + 1) * P], wo[:, g, :], start=(g == 0),
                      stop=(g == NG // 2 - 1), mark=(g == NG // 2 - 1), after=[t_oT[b * NG // 2 + g], t_wo, *free])
        if st == ST - 1:
            oT_free[b] = (t,)
        t_osb[b] = act.do(A.activation, osb[:, st, :], ps[:, 0:E], ACT.Copy, after=[t, *osb_free[0]])
        misc.give(i, t_osb[b])

    t_x1 = {}
    l_x1 = lane("x1")
    t_xw, xw_free = {}, [(), ()]
    x2_dram = nc.dram_tensor("x2", (B * S + TW, E), F32, kind="Internal").ap()
    routed = nc.dram_tensor("routed", (LOST_ROW + P, RW), F32, kind="Internal").ap()

    def inverse_rms(sums, after):
        t = pool.do(G.tensor_scalar, sums[:, 1], sums[:, 0], 1.0 / E, 1e-6, ALU.mult, ALU.add, after=[after])
        return inverse_root(sums[:, 3], sums[:, 1], sums[:, 2], t)

    def inverse_root(y, v, tmp, t, on=None):
        q, O = on or (pool, G)
        t = q.do(O.tensor_scalar, y.bitcast(I32), v.bitcast(I32), -0.5, float(0x5f3759df), ALU.mult, ALU.add,
                 after=[t])
        for _ in range(BETA):
            t = q.do(O.tensor_tensor, tmp, y, y, ALU.mult, after=[t])
            t = q.do(O.tensor_tensor, tmp, tmp, v, ALU.mult, after=[t])
            t = q.do(O.tensor_scalar, tmp, tmp, -0.5, 1.5, ALU.mult, ALU.add, after=[t])
            t = q.do(O.tensor_tensor, y, y, tmp, ALU.mult, after=[t])
        return t

    def residual(b):
        if b == 0:
            load_xin(1)
        t_s = pool.do(G.tensor_tensor, xin[b % 2][:, :, :], xin[b % 2][:, :, :],
                      shift[b % 2][:, :].unsqueeze(1).to_broadcast([P, ST, E]), ALU.add,
                      after=[t_xin[b], *t_gain[b]])
        for st in range(ST):
            j, jk, jfree = junks.take()
            t = dve.do(V.tensor_tensor_reduce, jk[:, 0:E], osb[:, st, :], osb[:, st, :], 1.0, 0.0, ALU.mult,
                       ALU.add, ssq[:, 0, st:st + 1], after=[t_osb[b], *jfree])
            junks.give(j, t)
        t = inverse_rms(ssq, t)
        for _ in range(6):
            yield
        for st in range(ST):
            t_g = dve.do(V.scalar_tensor_tensor, osb[:, st, :], osb[:, st, :], ssq[:, 3, st:st + 1],
                         gain[b % 2][:, :], ALU.mult, ALU.mult, after=[t, *t_gain[b]])
        for k in range(TOPK):
            t = pool.do(G.tensor_tensor, xw[k][:, :, 0:E], xin[b % 2][:, :, :], osb[:, :, :], ALU.add,
                        after=[t_g, t_s, *xw_free[k]])
            t_xw[b, k] = t
        osb_free[0] = (t,)
        gain_free[b] = (t_g, t_s)
        last_xin_use[b] = (t,)
        t_x1[b] = l_x1.start(sp, load, x2_dram[b * S:(b + 1) * S, :].rearrange("(j p) e -> p j e", p=P),
                             xw[0][:, :, 0:E], after=[t_xw[b, 0]])
        if b + 2 < B:
            load_xin(b + 2)

    x1T_free, t_gate, t_run, cnt_free = [()], {}, [t_const], [()]
    gate_ps = {}

    def gate_logits(b):
        for k in range(KT):
            yield
            i, ps, free = misc.take()
            for st in range(ST):
                t = pe.do(T.transpose, ps[:, st * P:(st + 1) * P], xw[0][:, st, k * P:(k + 1) * P], ident[:, :],
                          mark=(st == ST - 1), after=[t_xw[b, 0], t_id, *free])
            t = act.do(A.activation, x1T[:, k, :], ps[:, :], ACT.Copy, after=[t, *x1T_free[0]])
            misc.give(i, t)
        for st in range(ST):
            j, jk, jfree = junks.take()
            t_s = dve.do(V.tensor_tensor_reduce, jk[:, 0:E], xw[0][:, st, 0:E], xw[0][:, st, 0:E], 1.0, 0.0,
                         ALU.mult, ALU.add, newton[:, 0, st:st + 1], after=[t_xw[b, 0], *jfree])
            junks.give(j, t_s)
            if st % 2:
                yield
        t_s = inverse_rms(newton, t_s)
        t_gate[b] = (t, t_s)

    def small(op, *args, after=(), **kw):
        return pool.do(op, *args, after=[pool.now(), *after], **kw)

    def wide(a):
        return a.unsqueeze(2).to_broadcast([P, ST, NX])

    oh, eq = (gt[:, 4], gt[:, 5]), gt[:, 3]
    t_cnt = {}

    def choose(b):
        i, ps, free = misc.take()
        for st in range(ST):
            for k in range(KT):
                pe.do(T.matmul, ps[:, st * NX:(st + 1) * NX], x1T[:, k, st * P:(st + 1) * P], wg[:, k],
                      start=(k == 0), stop=(k == KT - 1), mark=False, after=[t_gate[b][0], t_wg, *free])
        t = pe.do(T.matmul, ps[:, ST * NX:(ST + 1) * NX], condR[:, b:b + 1].to_broadcast([C + 2, P]), ggw[:, :],
                  start=True, stop=True, after=[t_small, t_const])
        x1T_free[0] = (t,)
        yield
        t = act.do(A.activation, logits[:, :, :].rearrange("p s x -> p (s x)"), ps[:, 0:(ST + 1) * NX], ACT.Copy,
                   after=[t, *t_lg_free])
        misc.give(i, t)
        revs = rev.unsqueeze(1).to_broadcast([P, ST, NX])
        lg, ex, w = gt[:, 0], gt[:, 1], gt[:, 2]
        small(G.tensor_tensor, lg, logits[:, 0:ST], wide(newton[:, 3]), ALU.mult, after=[t, t_gate[b][1], t_flt])
        t_lg_free[:] = [small(G.tensor_tensor, lg, lg, logits[:, ST].unsqueeze(1).to_broadcast([P, ST, NX]), ALU.add)]
        yield
        yield
        t = dve.do(V.tensor_reduce, gs[:, 0], lg, AX.X, ALU.max, after=t_lg_free)
        t = small(G.tensor_tensor, lg, lg, wide(gs[:, 0]), ALU.subtract, after=[t])
        yield
        t = act.do(A.activation, ex, lg, ACT.Exp, after=[t])
        yield
        t = dve.do(V.tensor_reduce, gs[:, 1], ex, AX.X, ALU.add, after=[t])
        t = dve.do(V.reciprocal, gs[:, 2], gs[:, 1], after=[t])
        t = small(G.tensor_tensor, w, ex, wide(gs[:, 2]), ALU.mult, after=[t])
        yield
        for k in range(TOPK):
            t = dve.do(V.tensor_reduce, gs[:, 3], w, AX.X, ALU.max, after=[t])
            small(G.tensor_copy, xw[k][:, :, E], gs[:, 3], after=[t, *xw_free[k]])
            small(G.tensor_copy, xw[k][:, :, E + 1].bitcast(I32), ints[:, n_tok + b * ST:n_tok + (b + 1) * ST])
            t = dve.do(V.tensor_tensor, eq, w, wide(gs[:, 3]), ALU.is_equal, after=[t])
            t = small(G.tensor_tensor, eq, eq, revs, ALU.mult, after=[t])
            yield
            t = dve.do(V.tensor_reduce, gs[:, 4 + k], eq, AX.X, ALU.max, after=[t])
            t = dve.do(V.tensor_tensor, oh[k], revs, wide(gs[:, 4 + k]), ALU.is_equal, after=[t])
            if k == 0:
                small(G.tensor_scalar, eq, oh[k], -2.0, None, ALU.mult, after=[t])
                t = small(G.tensor_tensor, w, w, eq, ALU.add)
                yield
        t_cnt[b] = small(G.tensor_tensor, cnt[:, :, :], oh[0], oh[1], ALU.add, after=[t, *cnt_free[0]])

    def place(b):
        i, ps, free = misc.take()
        flat = cnt[:, :, :].rearrange("p s x -> p (s x)")
        pe.do(T.matmul, ps[:, 0:ST * NX], upper[:, :], flat, start=True, stop=True, mark=False,
              after=[t_cnt[b], t_const, *free])
        t = pe.do(T.matmul, ps[:, ST * NX:2 * ST * NX], ones[:, :], flat, start=True, stop=True)
        cnt_free[0] = (t,)
        yield
        t = act.do(A.activation, ranks[:, :, :].rearrange("p s x -> p (s x)"), ps[:, 0:2 * ST * NX], ACT.Copy,
                   after=[t, *t_rank_free])
        misc.give(i, t)
        now, before = run[b % 2], run[(b + 1) % 2]
        small(G.tensor_copy, now[:, 0], before[:, ST], after=[t])
        for st in range(ST):
            small(G.tensor_tensor, now[:, st + 1], now[:, st], ranks[:, ST + st], ALU.add)
        slot = gt[:, 6]
        t_rank_free[:] = [small(G.tensor_tensor, slot, now[:, 0:ST], ranks[:, 0:ST], ALU.add)]
        small(G.tensor_tensor, slot, slot, first_row.unsqueeze(1).to_broadcast([P, ST, NX]), ALU.add)
        for k in range(TOPK):
            t = small(G.tensor_tensor, eq, oh[k], slot, ALU.mult)
            yield
            yield
            t = dve.do(V.tensor_reduce, gs[:, 6], eq, AX.X, ALU.add, after=[t])
            small(G.tensor_scalar, gs[:, 7], gs[:, 4 + k], 0.0, flts[:, n_lost:n_lost + 1], ALU.is_equal, ALU.mult,
                  after=[t])
            small(G.tensor_tensor, gs[:, 7], gs[:, 7], gs[:, 6], ALU.add)
            t = small(G.tensor_copy, idx[b % 2][:, k], gs[:, 7], after=idx_free.get(b - 2, ()))
        t_run[0] = t
        for k in range(TOPK):
            for st in range(ST):
                t_sc[k] = start_scatter(l_sc[k], pool, idx[b % 2][:, k, st:st + 1], xw[k][:, st, :],
                                        after=[t, t_xw[b, k]])
        xw_free[0] = (t_sc[0], t_x1[b])
        xw_free[1] = (t_sc[1],)
        idx_free[b] = tuple(t_sc)

    t_lg_free, t_rank_free = [], []
    idx_free, t_sc = {}, [None, None]
    l_sc = [lane(f"scatter{k}") for k in range(TOPK)]

    def scatter_rows(index, src):
        return G.indirect_dma_start(routed, bass.IndirectOffsetOnAxis(ap=index, axis=0), src, None)

    def start_scatter(lane_, queue, index, src, after=()):
        queue.wait(*after)
        queue.steps.append((scatter_rows, (index, src), {}, lane_.sem, 16))
        lane_.count += 16
        return (lane_.sem, lane_.count)


    def project_steps(b):
        return [lambda qk=qk, half=half: project(b, qk, half) for qk in range(2) for half in range(2)]

    def value_steps(b):
        return [lambda: stack(b)] + [lambda st=st: project_v(b, st) for st in range(ST)]

    def finish_steps(b):
        return ([lambda: modulation(b)] + [lambda st=st: output_projection(b, st) for st in range(ST)]
                + [lambda: chains.append(chain(b))])

    chains = []

    def chain(b):
        for part, pause in ((residual, 8), (gate_logits, 4), (choose, 4), (place, 0)):
            yield from part(b)
            for _ in range(pause):
                yield

    for step in project_steps(0) + value_steps(0):
        step()
    n_groups = B * NG
    todo = []
    for i in range(n_groups + 3):
        b = i // NG
        if i % NG == 0 and b + 1 < B:
            todo += project_steps(b + 1)
        if i % NG == 2:
            if b + 1 < B:
                todo += value_steps(b + 1)
            if 0 <= b - 1 < B:
                todo += finish_steps(b - 1)
        for k in range(ST):
            if k == 0 and 0 <= i - 1 < n_groups:
                split_maxima(i - 1)
            g, kt = (i - 2, k - 1) if k else (i - 3, ST - 1)
            for n in range(GH):
                if i < n_groups:
                    row_maxima(i, k, n)
                if 0 <= i - 2 < n_groups:
                    exponentials(i - 2, k, n)
                if n == 1 and 0 <= g < n_groups:
                    weighted_values(g, kt)
                if chains and next(chains[0], chains) is chains:
                    chains.pop(0)
            if k == 0 and 0 <= i - 3 < n_groups:
                normalise(i - 3)
            if k == 2 and 0 <= i - 1 < n_groups:
                maxima_rows(i - 1)
            for _ in range(2 if len(todo) > 12 else 1):
                if todo:
                    todo.pop(0)()
    while todo:
        todo.pop(0)()
    for rest_of_batch in chains:
        for _ in rest_of_batch:
            pass

    def v(op, *args, after=(), **kw):
        return dve.do(op, *args, after=[dve.now(), *after], **kw)

    counts = run[(B - 1) % 2][:, ST, :]
    v(V.tensor_scalar, tbi[:, :], counts, float(TW - 1), None, ALU.add, after=[t_run[0]])
    v(V.tensor_scalar, tbi[:, :], tbi[:, :], TW.bit_length() - 1, None, ALU.arith_shift_right)
    v(V.tensor_copy, tb[:, 0], tbi[:, :])
    v(V.tensor_copy, tb[:, 1], tb[:, 0])
    for n, step in enumerate((1, 2, 4)):
        v(V.tensor_copy, tb[:, 2 + n, 0:step], tb[:, 1 + n, 0:step])
        v(V.tensor_tensor, tb[:, 2 + n, step:], tb[:, 1 + n, step:], tb[:, 1 + n, :NX - step], ALU.add)
    end, base = tb[:, 4], tb[:, 5]
    v(V.tensor_tensor, base, end, tb[:, 0], ALU.subtract)
    tile_no = flts[:, n_tile:n_tile + NTILES]

    def over_tiles(a):
        return a.unsqueeze(1).to_broadcast([P, NTILES, NX])

    def over_experts(a):
        return a.unsqueeze(2).to_broadcast([P, NTILES, NX])

    expert, left8, first, chunk, used = (tv[:, n] for n in range(5))
    v(V.tensor_tensor, tj[:, 0], over_tiles(end), over_experts(tile_no), ALU.is_le)
    v(V.tensor_reduce, expert, tj[:, 0], AX.X, ALU.add)
    v(V.tensor_scalar, left8, expert, -1.0, float(NX), ALU.mult, ALU.add)
    v(V.tensor_tensor, tj[:, 1], over_tiles(rev), over_experts(left8), ALU.is_equal)
    v(V.tensor_tensor, tj[:, 0], tj[:, 1], over_tiles(base), ALU.mult)
    v(V.tensor_reduce, first, tj[:, 0], AX.X, ALU.add)
    v(V.tensor_tensor, chunk, tile_no, first, ALU.subtract)
    v(V.tensor_scalar, used, expert, float(NX), float(TW), ALU.is_lt, ALU.mult)
    v(V.tensor_tensor, chunk, chunk, used, ALU.mult)
    v(V.scalar_tensor_tensor, table[:, 0:NTILES], expert, float(REGION), chunk, ALU.mult, ALU.add)
    v(V.tensor_scalar, table[:, NTILES:2 * NTILES], expert, float(NX - 1), None, ALU.min)
    t_table = v(V.tensor_tensor, table[:, 2 * NTILES:], first_row, counts, ALU.add)

    l_pad = lane("pad")
    regs = {}

    def read_table(key, column, top):
        def op():
            regs[key] = nc.sync.value_load(table[0:1, column:column + 1], min_val=0, max_val=top)
        sp.steps.append((op, (), {}, None, 0))

    def dynamic(lane_, out, in_, after=()):
        sp.wait(*after)
        sp.steps.append((lambda: load(out(), in_()), (), {}, lane_.sem, 16))
        lane_.count += 16
        return (lane_.sem, lane_.count)

    sp.wait(t_table)
    for x in range(NX):
        read_table(("pad", x), 2 * NTILES + x, NULL_ROW - TW)
        dynamic(l_pad, lambda x=x: routed[bass.ds(regs["pad", x], TW), :].rearrange("(t p) c -> p t c", p=P),
                lambda: empty[:, :, :])
    l_pad.start(sp, load, routed[NULL_ROW:NULL_ROW + TW, :].rearrange("(t p) c -> p t c", p=P), empty[:, :, :])
    t_pad = l_pad.start(sp, load, x2_dram[B * S:, :].rearrange("(t p) c -> p t c", p=P), empty[:, :, 0:E])
    attention_done = [pe.now(), act.now(), dve.now(), pool.now(), t_x1[B - 1], *t_sc, t_pad]
    for q in (pe, act, dve, pool, sp):
        q.wait(*attention_done)

    phase[0].close()
    phase[0] = ExitStack()
    NW = 3
    HT = M // P
    wts = [sb(f"wts{i}", [P, (KT + HT) * M + HT * E]) for i in range(NW)]
    bias = [sb(f"bias{i}", [P, 2 * HT]) for i in range(NW)]
    bias3 = [sb(f"bias3_{i}", [P, E]) for i in range(NW)]
    rows = [sb(f"rows{i}", [P, TT, RW]) for i in range(NW)]
    rowsT = [sb(f"rowsT{i}", [P, KT, TW]) for i in range(2)]
    hid1 = [sb(f"hid1_{i}", [P, HT, TW]) for i in range(2)]
    hid2 = [sb(f"hid2_{i}", [P, HT, TW]) for i in range(2)]
    ysum = [sb(f"ysum{i}", [P, TT, E]) for i in range(2)]
    yout = [sb(f"yout{i}", [P, TT, E]) for i in range(2)]
    ab = [sb(f"ab{i}", [P, KT, E]) for i in range(B)]
    rcob = [sb(f"rcob{i}", [KB, 2, E]) for i in range(2)]
    l_wt = [lane(f"wts{i}") for i in range(NW)]
    l_row = [lane(f"rows{i}") for i in range(NW)]

    hidden = Ring(bank[0:4])
    outs = Ring(bank[4:6])
    turns = Ring(bank[6:8])
    t_wt, t_rows, wt_free, rows_free = {}, {}, {}, {}
    t_rT, rT_free, t_h1, h1_free, t_h2, h2_free, t_y, y_free = {}, {}, {}, {}, {}, {}, {}, {}

    def fetch(j):
        n = j % NW
        read_table(("row", j), j, NULL_ROW)
        t_rows[j] = dynamic(l_row[n], lambda: rows[n][:, :, :],
                            lambda: routed[bass.ds(regs["row", j], TW), :].rearrange("(t p) c -> p t c", p=P),
                            after=rows_free.get(j - NW, ()))
        read_table(("x", j), NTILES + j, NX - 1)
        o1, o2 = KT * M, (KT + HT) * M
        for dst, src, how in (
                (wts[n][:, 0:o1].rearrange("p (k m) -> p k m", m=M), d["W1"], "e (k p) m -> p (e k) m"),
                (wts[n][:, o1:o2].rearrange("p (k m) -> p k m", m=M), d["W2"], "e (k p) m -> p (e k) m"),
                (wts[n][:, o2:].rearrange("p (k m) -> p k m", m=E), d["W3"], "e (k p) m -> p (e k) m")):
            dynamic(l_wt[n], lambda dst=dst: dst,
                    lambda src=src, how=how: src[bass.ds(regs["x", j], 1)].rearrange(how, p=P),
                    after=wt_free.get(j - NW, ()))
        dynamic(l_wt[n], lambda: bias[n][:, :],
                lambda: d["b12"][bass.ds(regs["x", j], 1)].rearrange("e p c -> p (e c)"))
        t_wt[j] = dynamic(l_wt[n], lambda: bias3[n][:, :],
                          lambda: d["b3"][bass.ds(regs["x", j], 1)].to_broadcast([P, E]))

    def turn(j):
        i, ps, free = turns.take()
        for k in range(KT):
            for tt in range(TT):
                t = pe.do(T.transpose, ps[:, k * TW + tt * P:k * TW + (tt + 1) * P],
                          rows[j % NW][:, tt, k * P:(k + 1) * P], ident[:, :],
                          mark=(k == KT - 1 and tt == TT - 1), after=[t_rows[j], *free])
        t_rT[j] = act.do(A.activation, rowsT[j % 2][:, :, :].rearrange("p k t -> p (k t)"), ps[:, :], ACT.Copy,
                         after=[t, *rT_free.get(j - 2, ())])
        turns.give(i, t_rT[j])

    def layer1(j):
        for m in range(HT):
            i, ps, free = hidden.take()
            for k in range(KT):
                t = pe.do(T.matmul, ps[:, 0:TW], wts[j % NW][:, k * M + m * P:k * M + (m + 1) * P],
                          rowsT[j % 2][:, k, :], start=(k == 0), stop=(k == KT - 1), mark=(k == KT - 1),
                          after=[t_wt[j], t_rT[j], *free])
            t_h1[j, m] = act.do(A.activation, hid1[j % 2][:, m, :], ps[:, 0:TW], ACT.Relu,
                                bias=bias[j % NW][:, m:m + 1], after=[t, *h1_free.get(j - 2, ())])
            hidden.give(i, t_h1[j, m])
        rT_free[j] = (t,)

    def layer2(j):
        o1 = KT * M
        for m in range(HT):
            i, ps, free = hidden.take()
            for k in range(HT):
                t = pe.do(T.matmul, ps[:, 0:TW], wts[j % NW][:, o1 + k * M + m * P:o1 + k * M + (m + 1) * P],
                          hid1[j % 2][:, k, :], start=(k == 0), stop=(k == HT - 1), mark=(k == HT - 1),
                          after=[t_h1[j, k], *free])
            t_h2[j, m] = dve.do(V.tensor_scalar, hid2[j % 2][:, m, :], ps[:, 0:TW],
                                bias[j % NW][:, HT + m:HT + m + 1], 0.0, ALU.add, ALU.max,
                                after=[t, *h2_free.get(j - 2, ())])
            hidden.give(i, t_h2[j, m])
        h1_free[j] = (t,)

    l_add = lane("add")
    t_add = [None]

    def add_rows(index, src):
        return G.indirect_dma_start(x2_dram, bass.IndirectOffsetOnAxis(ap=index, axis=0), src, None,
                                    compute_op=ALU.add)

    def layer3(j):
        o2 = (KT + HT) * M
        for tt in range(TT):
            i, ps, free = outs.take()
            for k in range(HT):
                t = pe.do(T.matmul, ps[:, 0:E], hid2[j % 2][:, k, tt * P:(tt + 1) * P],
                          wts[j % NW][:, o2 + k * E:o2 + (k + 1) * E], start=(k == 0), stop=(k == HT - 1),
                          mark=(k == HT - 1), after=[t_h2[j, k], *free])
            t_b = dve.do(V.tensor_tensor, ysum[j % 2][:, tt], ps[:, 0:E], bias3[j % NW][:, :], ALU.add,
                         after=[t, *y_free.get(j - 2, ())])
            outs.give(i, t_b)
            t_w = act.do(A.activation, yout[j % 2][:, tt], ysum[j % 2][:, tt], ACT.Copy,
                         scale=rows[j % NW][:, tt, E:E + 1], after=[t_b, *y_free.get(j - 2, ())])
            pool.wait(t_w, *([t_add[0]] if t_add[0] else []))
            pool.steps.append((add_rows, (rows[j % NW][:, tt, E + 1:E + 2].bitcast(U32), yout[j % 2][:, tt]), {},
                               l_add.sem, 16))
            l_add.count += 16
            t_add[0] = (l_add.sem, l_add.count)
        h2_free[j] = (t,)
        wt_free[j] = (t, t_b, *[t_h1[j, HT - 1]], *[t_h2[j, HT - 1]])
        y_free[j] = (t_add[0], t_w)
        rows_free[j] = (t_add[0], t_w)
        if j + NW < NTILES:
            fetch(j + NW)

    l_q = lane("quaternions")
    t_quat, t_obm = [], []
    scratch = [sb(f"scratch{i}", [P, S]) for i in range(8)]

    QD = E // 4
    t_q = [None]

    def quaternions_load():
        for dst, src, n in ((scratch[0][:, :], "cond", B * C), (scratch[1][:, 0:E], "q_right", E)):
            l_q.start(sp, load, dst, d[src].rearrange("b c -> (b c)").unsqueeze(0).to_broadcast([P, n]))
        t_q[0] = l_q.start(sp, load, scratch[1][:, E:E + QD], d["gate"].unsqueeze(0).to_broadcast([P, QD]))

    def quaternions():
        qc = scratch[0][:, :].rearrange("p (r d) -> p r d", d=QD)
        qr = scratch[1][:, 0:E].rearrange("p (r d) -> p r d", d=QD)
        gate, norm = scratch[1][:, E:E + QD], scratch[1][:, E + QD:E + 2 * QD]
        inv, tmp = scratch[1][:, E + 2 * QD:E + 3 * QD], scratch[1][:, E + 3 * QD:2 * E]
        sq = scratch[2][:, :].rearrange("p (r d) -> p r d", d=QD)
        right = [scratch[3 + i // 2][:, i % 2 * E:(i % 2 + 1) * E].rearrange("p (j d) -> p j d", d=QD) for i in range(4)]
        coef = [scratch[5 + i // 2][:, i % 2 * E:(i % 2 + 1) * E].rearrange("p (j d) -> p j d", d=QD) for i in range(4)]
        prod = scratch[7][:, 0:E].rearrange("p (j d) -> p j d", d=QD)
        t = t_q[0]
        def v(op, *args, **kw):
            return dve.do(op, *args, after=[dve.now(), t], **kw)

        for q, rows in ((qc, B), (qr, 4)):
            v(V.tensor_tensor, sq[:, 0:rows], q, q, ALU.mult)
            v(V.tensor_reduce, norm, sq[:, 0:rows].rearrange("p r d -> p d r"), AX.X, ALU.add)
            v(V.tensor_scalar, norm, norm, 1e-8, None, ALU.add)
            inverse_root(inv, norm, tmp, dve.now(), on=(dve, V))
            v(V.tensor_tensor, q[:, 0:4], q[:, 0:4], inv.unsqueeze(1).to_broadcast([P, 4, QD]), ALU.mult)
        v(V.tensor_tensor, qr[:, :, :], qr[:, :, :], gate.unsqueeze(1).to_broadcast([P, 4, QD]), ALU.mult)
        R = (((0, 1), (1, 1), (2, 1), (3, 1)), ((1, -1), (0, 1), (3, -1), (2, 1)),
             ((2, -1), (3, 1), (0, 1), (1, -1)), ((3, -1), (2, -1), (1, 1), (0, 1)))
        L = (((0, 1), (1, -1), (2, -1), (3, -1)), ((1, 1), (0, 1), (3, -1), (2, 1)),
             ((2, 1), (3, 1), (0, 1), (1, -1)), ((3, 1), (2, -1), (1, 1), (0, 1)))
        for i in range(4):
            for j in range(4):
                n, sign = R[i][j]
                v(V.tensor_scalar, right[i][:, j], qr[:, n], float(sign), None, ALU.mult)
        for i in range(4):
            for k in range(4):
                n, sign = L[i][k]
                left = qc[:, n].unsqueeze(1).to_broadcast([P, 4, QD])
                if k == 0:
                    v(V.tensor_tensor, coef[i], right[k], left, ALU.mult)
                else:
                    v(V.tensor_tensor, prod, right[k], left, ALU.mult)
                    v(V.tensor_tensor, coef[i], coef[i], prod, ALU.add if sign > 0 else ALU.subtract)
        for j in range(4):
            rows = slice(j % 2 * QD, (j % 2 + 1) * QD)
            for i in range(4):
                t_quat[:] = [v(V.tensor_tensor, quat[rows, j // 2, i * QD:(i + 1) * QD],
                               ident[rows, rows], coef[i][rows, j], ALU.mult)]
        ob = obm[:, :].rearrange("p (j d) -> p j d", d=QD)
        acc = scratch[2][0:KB, 0:E].rearrange("p (i d) -> p i d", d=QD)
        v(V.tensor_copy, scratch[2][0:KB, 0:E], obm[:, :])
        for i in range(4):
            v(V.tensor_tensor, prod[0:KB], ob, coef[i][0:KB], ALU.mult)
            for j in range(4):
                v(V.tensor_tensor, acc[:, i], acc[:, i], prod[0:KB, j], ALU.add)
        t = v(V.tensor_copy, obm[:, :], scratch[2][0:KB, 0:E])
        t_obm[:] = [t]

    t_elim = [None]

    def gram():
        i, ps, free = turns.take()
        t = pe.do(T.matmul, ps[0:KB, 0:KB], raw[:, 0], raw[:, 0], start=True, stop=True, after=[t_small, *free])
        t = dve.do(V.scalar_tensor_tensor, elim[:, 0:KB], ident[0:KB, 0:KB], 1e-4, ps[0:KB, 0:KB], ALU.mult,
                   ALU.add, after=[t, t_id])
        turns.give(i, t)
        t_elim[0] = dve.do(V.tensor_copy, elim[:, KB:2 * KB], raw[:, 1], after=[t])

    def eliminate(j):
        i, ps, free = turns.take()
        t = pe.do(T.matmul, ps[0:KB, 0:2 * KB], ident[0:KB, j:j + 1].to_broadcast([KB, KB]), elim[:, :],
                  start=True, stop=True, after=[t_elim[0], t_id, *free])
        t = dve.do(V.reciprocal, pivot[:, 0:1], ps[0:KB, j:j + 1], after=[t])
        t = dve.do(V.scalar_tensor_tensor, pivot[:, 1:2], elim[:, j:j + 1], pivot[:, 0:1], below[:, j:j + 1],
                   ALU.mult, ALU.mult, after=[t, t_const])
        t_elim[0] = dve.do(V.scalar_tensor_tensor, elim[:, :], ps[0:KB, 0:2 * KB], pivot[:, 1:2], elim[:, :],
                           ALU.mult, ALU.add, after=[t])
        turns.give(i, t_elim[0])

    t_mtr = []

    def orthogonalise():
        def v(op, *args, **kw):
            return dve.do(op, *args, after=[dve.now()], **kw)

        v(V.tensor_tensor_reduce, below[:, :], elim[:, 0:KB], ident[0:KB, 0:KB], 1.0, 0.0, ALU.mult, ALU.add,
          pivot[:, 2:3])
        inverse_root(pivot[:, 4:5], pivot[:, 2:3], pivot[:, 3:4], dve.now(), on=(dve, V))
        v(V.tensor_scalar, mtrT[:, :], elim[:, KB:2 * KB], pivot[:, 4:5], None, ALU.mult)
        v(V.tensor_tensor_reduce, below[:, :], mtrT[:, :], raw[:, 1], 1.0, 0.0, ALU.mult, ALU.add, pivot[:, 5:6])
        v(V.tensor_scalar, pivot[:, 6:7], pivot[:, 5:6], 0.0, 2.0, ALU.is_ge, ALU.mult)
        v(V.tensor_scalar, pivot[:, 7:8], pivot[:, 6:7], -1.0, None, ALU.add)
        t_mtr[:] = [v(V.tensor_scalar, mtrT[:, :], mtrT[:, :], pivot[:, 7:8], None, ALU.mult)]

    def combined(b):
        r = rcob[b % 2]
        t = dve.do(V.tensor_scalar, r[:, 0], obm[:, :], cond_cols[:, 1, b:b + 1], None, ALU.mult,
                   after=[*t_obm, t_small, *rc_free.get(b - 2, ())])
        i, ps, free = turns.take()
        t = pe.do(T.matmul, ps[0:KB, 0:E], mtrT[:, :], r[:, 0], start=True, stop=True, after=[t, *t_mtr, *free])
        t = act.do(A.activation, r[:, 1], ps[0:KB, 0:E], ACT.Copy, scale=cond_cols[:, 0, b:b + 1],
                   after=[t, *rc_free.get(b - 2, ())])
        turns.give(i, t)
        i, ps, free = turns.take()
        for k in range(KT):
            t = pe.do(T.matmul, ps[:, k * E:(k + 1) * E], basis[:, k * P:(k + 1) * P], r[:, 1], start=True, stop=True,
                      after=[t, *free])
        rc_free[b] = (t,)
        t_ab[b] = dve.do(V.tensor_tensor, ab[b][:, :, :].rearrange("p k e -> p (k e)"), ps[:, :],
                         quat[:, :, :].rearrange("p k e -> p (k e)"), ALU.add, after=[t, *t_quat])
        turns.give(i, t_ab[b])

    t_ab, rc_free = {}, {}
    for j in range(NW):
        fetch(j)
    side = ([quaternions_load, gram] + [lambda j=j: eliminate(j) for j in range(KB - 1)]
            + [orthogonalise, quaternions] + [lambda b=b: combined(b) for b in range(B)])
    turn(0)
    layer1(0)
    turn(1)
    for j in range(NTILES):
        layer2(j)
        if side:
            side.pop(0)()
        if j + 1 < NTILES:
            layer1(j + 1)
        if side:
            side.pop(0)()
        layer3(j)
        if j + 2 < NTILES:
            turn(j + 2)
    assert not side

    NL = 4
    x2b = [sb(f"x2b{i}", [P, ST, E]) for i in range(NL)]
    x2T = [sb(f"x2T{i}", [P, KT, S]) for i in range(2)]
    fin = [sb(f"fin{i}", [P, ST, E]) for i in range(2)]
    l_x2 = [lane(f"x2_{i}") for i in range(NL)]
    l_out = [lane(f"out{i}") for i in range(2)]
    t_x2, x2_free, x2T_free, t_out, fin_free = {}, {}, {}, {}, {}

    def load_x2(b):
        t_x2[b] = l_x2[b % NL].start(sp, load, x2b[b % NL][:, :, :],
                                     x2_dram[b * S:(b + 1) * S, :].rearrange("(j p) e -> p j e", p=P),
                                     after=[t_add[0], *x2_free.get(b - NL, ())])

    for b in range(NL):
        load_x2(b)
    for b in range(B):
        t_T = []
        for k in range(KT):
            i, ps, free = turns.take()
            for st in range(ST):
                t = pe.do(T.transpose, ps[:, st * P:(st + 1) * P], x2b[b % NL][:, st, k * P:(k + 1) * P], ident[:, :],
                          mark=(st == ST - 1), after=[t_x2[b], *free])
            t = act.do(A.activation, x2T[b % 2][:, k, :], ps[:, :], ACT.Copy, after=[t, *x2T_free.get(b - 2, ())])
            turns.give(i, t)
            t_T.append(t)
        for st in range(ST):
            i, ps, free = hidden.take()
            for k in range(KT):
                t = pe.do(T.matmul, ps[:, 0:E], x2T[b % 2][:, k, st * P:(st + 1) * P], ab[b][:, k, :],
                          start=(k == 0), stop=(k == KT - 1), mark=(k == KT - 1), after=[t_T[k], t_ab[b], *free])
            t_f = dve.do(V.tensor_tensor, fin[b % 2][:, st], ps[:, 0:E], x2b[b % NL][:, st], ALU.add,
                         after=[t, *fin_free.get(b - 2, ())])
            hidden.give(i, t_f)
        x2T_free[b] = (t,)
        x2_free[b] = (t_f,)
        if b + NL < B:
            load_x2(b + NL)
        t_out[b] = l_out[b % 2].start(sp, load, out[b * S:(b + 1) * S, :].rearrange("(j p) e -> p j e", p=P),
                                      fin[b % 2][:, :, :], after=[t_f])
        fin_free[b] = (t_out[b],)
    sp.wait(t_out[B - 2], t_out[B - 1])
    outer.enter_context(phase[0])

    block = ctx.enter_context(nc.Block())
    for name, q in (("sync", sp), ("scalar", act), ("vector", dve), ("gpsimd", pool), ("tensor", pe)):
        deco = {"sync": block.sync, "scalar": block.scalar, "vector": block.vector, "gpsimd": block.gpsimd,
                "tensor": block.tensor}[name]
        deco(q.emit)


def kernel(**inputs):
    import concourse.bacc as bacc
    from concourse.bass_utils import run_bass_kernel_spmd
    nc = bacc.Bacc("TRN2", target_bir_lowering=False, num_devices=1)
    a = {n: np.asarray(v) for n, v in inputs.items()}
    x = a["x"].reshape(B * S, E)
    mask = a["mask_SxS_bk1"]

    def columns(b):
        return b.reshape(NX, M // P, P).transpose(0, 2, 1)

    arrays = {
        "x": x, "xT": x.T, "mask": mask, "maskT": mask.T,
        "cond": a["cond_256"], "condT": a["cond_256"].T, "cond64T": a["cond_64"].T,
        "WqT": a["L0_cond_Wq"].T, "WkT": a["L0_cond_Wk"].T, "WvT": a["L0_cond_Wv"].T, "WoT": a["L0_cond_Wo"].T,
        "rms_scale": a["L0_cond_rms_scale"], "WcT": a["L0_cond_Wc"].T, "bc": a["L0_cond_bc"],
        "rms_w": a["L1_cond_rms_w"].reshape(KT, P).T, "wg_W": a["L1_cond_wg_W"], "wg_b": a["L1_cond_wg_b"],
        "gg_W": a["L1_cond_gg_W"], "gg_b": a["L1_cond_gg_b"],
        "W1": a["L1_cond_W1"], "W2": a["L1_cond_W2"], "W3": a["L1_cond_W3"],
        "b12": np.concatenate([columns(a["L1_cond_b1"]), columns(a["L1_cond_b2"])], axis=2), "b3": a["L1_cond_b3"],
        "input_basis": a["L2_cond_input_basis"], "mtr": a["L2_cond_mode_to_rank"],
        "mtrT": a["L2_cond_mode_to_rank"].T, "output_basis": a["L2_cond_output_basis"],
        "q_right": a["L3_cond_q_right"], "gate": a["L3_cond_spectral_gate"].reshape(-1),
    }
    arrays = {"in_" + n: np.ascontiguousarray(v) for n, v in arrays.items()}
    d = {n[3:]: nc.dram_tensor(n, v.shape, mybir.dt.from_np(v.dtype), kind="ExternalInput").ap()
         for n, v in arrays.items()}
    out = nc.dram_tensor("out", (B * S, E), F32, kind="ExternalOutput").ap()
    build(nc, d, out)
    r = run_bass_kernel_spmd(nc, [arrays], core_ids=[0])
    return r.results[0]["out"].reshape(B, S, E)
```

```python
import numpy as np
from contextlib import ExitStack
import concourse.bass as bass
import concourse.mybir as mybir

F32 = mybir.dt.float32
F32R = mybir.dt.float32r
BF16 = mybir.dt.bfloat16
U8 = mybir.dt.uint8
I32 = mybir.dt.int32
U32 = mybir.dt.uint32
ALU = mybir.AluOpType
ACT = mybir.ActivationFunctionType
AX = mybir.AxisListType

P = 128
B, S, E = 8, 512, 256
H = 16
D = E // H
C = 64
NX = 8
M = 512
KT = E // P
ST = S // P
NT = B * ST
GH = 4
NG = H // GH
PARTS = 3
PAIRS = [(0, 0), (1, 0), (0, 1), (1, 1), (0, 2), (2, 0)]
KQ = len(PAIRS) * D
MASKED = -3.0e38
FLOOR = -1.0e38


TW = 256
TT = TW // P
TOPK = 2
NTILES = B * S * TOPK // TW + NX - 1
REGION = B * S + TW
NULL_ROW = NX * REGION
LOST_ROW = NULL_ROW + TW
RW = E + 2
KB = 64
BETA = 3


class Engine:

    def __init__(self, sem):
        self.sem, self.count, self.steps, self.passed = sem, 0, [], {}

    def wait(self, *tokens):
        for sem, value in tokens:
            if value > self.passed.get(sem.name, 0):
                self.passed[sem.name] = value
                self.steps.append((None, sem, value))

    def do(self, op, *args, after=(), mark=True, **kw):
        self.wait(*after)
        self.steps.append((op, args, kw, self.sem if mark else None, 1))
        self.count += mark
        return (self.sem, self.count)

    def now(self):
        return (self.sem, self.count)

    def emit(self, engine):
        for step in self.steps:
            if step[0] is None:
                engine.wait_ge(step[1], step[2])
            else:
                op, args, kw, sem, n = step
                ins = op(*args, **kw)
                if sem is not None:
                    ins.then_inc(sem, n)


class Lane:

    def __init__(self, sem):
        self.sem, self.count = sem, 0

    def start(self, queue, op, out, in_, after=()):
        queue.wait(*after)
        queue.steps.append((op, (out, in_), {}, self.sem, 16))
        self.count += 16
        return (self.sem, self.count)


class Ring:

    def __init__(self, bufs):
        self.bufs, self.free, self.n = bufs, [()] * len(bufs), 0

    def take(self):
        i = self.n % len(self.bufs)
        self.n += 1
        return i, self.bufs[i], self.free[i]

    def give(self, i, *tokens):
        self.free[i] = tokens


def build(nc, d, out):
    with ExitStack() as ctx:
        _build(nc, ctx, d, out)


def _build(nc, ctx, d, out):
    outer, phase = ctx, [ExitStack()]

    def sb(name, shape, dt=F32):
        return phase[0].enter_context(nc.sbuf_tensor(name, shape, dt))

    def sem(name):
        return ctx.enter_context(nc.semaphore(name))

    def lane(name):
        return Lane(sem("dma_" + name))

    pe, act, dve, pool, sp = (Engine(sem("progress_" + n)) for n in ("pe", "act", "dve", "pool", "sp"))
    V, A, G, T = nc.vector, nc.scalar, nc.gpsimd, nc.tensor
    load = nc.sync.dma_start

    bank = [ctx.enter_context(nc.psum_tensor(f"bank{i}", [P, 512], F32)) for i in range(8)]

    def lasting(name, shape, dt=F32):
        return outer.enter_context(nc.sbuf_tensor(name, shape, dt))

    ident = lasting("ident", [P, P])
    empty = lasting("empty", [P, TT, RW])
    table = lasting("table", [P, 2 * NTILES + NX], I32)
    mtrT = lasting("mtrT", [KB, KB])
    obm = lasting("obm", [KB, E])
    basis = lasting("basis", [KB, E])
    quat = lasting("quat", [P, KT, E])
    cond_cols = lasting("cond_cols", [C, 2, B])
    below = lasting("below", [KB, KB])
    elim = lasting("elim", [KB, 2 * KB])
    raw = lasting("raw", [KB, 2, KB])
    pivot = lasting("pivot", [KB, 8])
    stacks0 = [lasting(f"{n}0", [P, H, S], BF16) for n in ("qst", "kst")]

    identb = sb("identb", [P, P], BF16)
    upper = sb("upper", [P, P], BF16)
    ones = sb("ones", [P, P], BF16)
    xw = [sb(f"xw{i}", [P, ST, RW]) for i in range(TOPK)]
    x1T = sb("x1T", [P, KT, S])
    wg = sb("wg", [P, KT, NX])
    rmsw = sb("rmsw", [P, KT])
    ggw = sb("ggw", [C + 2, NX])
    condR = sb("condR", [C + 2, B])
    newton = sb("newton", [P, 4, ST])
    ints = sb("ints", [P, 2 * NX + NT + 1 + NTILES], I32)
    flts = sb("flts", [P, 2 * NX + NT + 1 + NTILES])
    gt = sb("gt", [P, 8, ST, NX])
    gs = sb("gs", [P, 8, ST])
    cnt = sb("cnt", [P, ST, NX], BF16)
    logits = sb("logits", [P, ST + 1, NX])
    ranks = sb("ranks", [P, 2 * ST, NX])
    run = [sb(f"run{i}", [P, ST + 1, NX]) for i in range(2)]
    idx = [sb(f"idx{i}", [P, TOPK, ST], U32) for i in range(2)]
    tb = sb("tb", [P, 10, NX])
    tbi = sb("tbi", [P, NX], I32)
    x1T_flat = x1T[:, :, :].rearrange("p k s -> p (k s)")
    tj = x1T_flat[:, 0:2 * NTILES * NX].rearrange("p (a t x) -> p a t x", a=2, x=NX)
    tv = x1T_flat[:, 2 * NTILES * NX:(2 * NX + 6) * NTILES].rearrange("p (a t) -> p a t", a=6)

    wqk = sb("wqk", [P, 2, KT, E])
    wv = sb("wv", [P, KT, E])
    wo = sb("wo", [P, NG // 2, E])
    mneg = sb("mneg", [P, 2, ST, S], BF16)
    most = sb("most", [P, ST, S], BF16)
    xT = [sb(f"xT{i}", [P, KT, S]) for i in range(2)]
    xin = [sb(f"xin{i}", [P, ST, E]) for i in range(2)]
    parts = [sb(f"parts{i}", [P, 2, PARTS, S], BF16) for i in range(2)]
    rest = [sb(f"rest{i}", [P, S]) for i in range(2)]
    qst = [stacks0[0], sb("qst1", [P, H, S], BF16)]
    kst = [stacks0[1], sb("kst1", [P, H, S], BF16)]
    vaug = [sb(f"vaug{i}", [P, ST, H, 32]) for i in range(2)]
    junk = [sb(f"junk{i}", [P, S], BF16) for i in range(2)]
    rowmax = [sb(f"rowmax{i}", [P, GH, ST]) for i in range(2)]
    negm = [sb(f"negm{i}", [P, 2, GH, ST]) for i in range(2)]
    m3 = [sb(f"m3_{i}", [P, ST, GH, PARTS], BF16) for i in range(2)]
    mrow = [sb(f"mrow{i}", [GH * PARTS, S], BF16) for i in range(2)]
    pt = [sb(f"pt{i}", [P, S]) for i in range(11)]
    turned = [sb(f"turned{i}", [P, 16, 32]) for i in range(2)]
    rden = [sb(f"rden{i}", [P, 16]) for i in range(2)]
    oT = [sb(f"oT{i}", [P, NG // 2, S]) for i in range(2)]
    osb = sb("osb", [P, ST, E])
    mask8 = osb[:, :, :].rearrange("p s e -> p (s e)").bitcast(U8).rearrange("p (a s t) -> p a s t", a=2, s=ST)
    ssq = sb("ssq", [P, 4, ST])
    condS = sb("condS", [C + 1, B])
    condw = sb("condw", [C, 3, B])
    wc = sb("wc", [C + 1, 2 * E])
    rmsb = sb("rmsb", [P, E])
    gain = [sb(f"gain{i}", [P, E]) for i in range(2)]
    shift = [sb(f"shift{i}", [P, E]) for i in range(2)]

    x_dram, xT_dram = d["x"], d["xT"]
    split_dram = nc.dram_tensor("split_parts", (B, 2, PARTS, H // 8 * P, S), BF16, kind="Internal").ap()

    l_w = lane("weights")
    t_w = None
    for i, n in enumerate(("WqT", "WkT")):
        t_w = l_w.start(sp, load, wqk[:, i], d[n].rearrange("(k p) e -> p k e", p=P))
    l_x = [lane(f"xT{i}") for i in range(2)]
    l_xin = [lane(f"xin{i}") for i in range(2)]
    t_xT, t_xin = {}, {}
    last_x_use = {}

    def load_x(b):
        free = last_x_use.get(b - 2, ())
        t_xT[b] = l_x[b % 2].start(sp, load, xT[b % 2][:, :, :],
                                   xT_dram[:, b * S:(b + 1) * S].rearrange("(k p) s -> p k s", p=P), after=free)

    last_xin_use = {}

    def load_xin(b):
        t_xin[b] = l_xin[b % 2].start(sp, load, xin[b % 2][:, :, :],
                                      x_dram[b * S:(b + 1) * S, :].rearrange("(j p) e -> p j e", p=P),
                                      after=last_xin_use.get(b - 2, ()))

    load_x(0)
    t_wv = lane("value_weights").start(sp, load, wv[:, :, :], d["WvT"].rearrange("(k p) e -> p k e", p=P))
    l_m = lane("masks")
    l_m.start(sp, load, mask8[:, 0], d["mask"].rearrange("(j p) t -> p j t", p=P))
    t_mask = l_m.start(sp, load, mask8[:, 1], d["maskT"].rearrange("(j p) t -> p j t", p=P))
    load_x(1)

    t_id0 = pool.do(G.memset, ident[:, :], 0.0)
    t_id = pool.do(G.affine_select, out=ident[:, :], in_=ident[:, :], compare_op=ALU.not_equal, fill=1.0,
                   base=0, pattern=[[-1, P]], channel_multiplier=1, after=[t_id0])

    row_scores = Ring(bank[0:3])
    col_scores = Ring(bank[3:5])
    misc = Ring(bank[6:8])
    av_bank, av_free = bank[5], [()]
    probs = Ring(pt)
    junks = Ring(junk)
    rests = Ring(rest)

    l_parts = [lane(f"parts{i}") for i in range(2)]
    l_stack = [lane(f"stack{i}") for i in range(2)]
    l_mrow = [lane(f"mrow{i}") for i in range(2)]
    parts_free = [(), ()]
    t_parts, t_stack, t_v = {}, {}, {}
    stack_free = {}
    v_free = {}

    def project(b, qk, half):
        i, ps, free = misc.take()
        for k in range(KT):
            t = pe.do(T.matmul, ps[:, :], wqk[:, qk, k, half * P:(half + 1) * P], xT[b % 2][:, k, :],
                      start=(k == 0), stop=(k == KT - 1), mark=(k == KT - 1), after=[t_w, t_xT[b], *free])
        pp = parts[qk]
        hi, mid, lo = (pp[:, half, n, :] for n in range(PARTS))
        t_hi = act.do(A.activation, hi, ps[:, :], ACT.Copy, after=[t, *parts_free[qk]])
        r, left, rfree = rests.take()
        t_r = dve.do(V.tensor_tensor, left[:, :], ps[:, :], hi, ALU.subtract, after=[t, t_hi, *rfree])
        misc.give(i, t_r)
        t_mid = act.do(A.activation, mid, left[:, :], ACT.Copy, after=[t_r])
        t_lo = pool.do(G.tensor_tensor, lo, left[:, :], mid, ALU.subtract, after=[t_mid])
        rests.give(r, t_lo)
        t_out = l_parts[qk].start(sp, load, split_dram[b, qk][:, half * P:(half + 1) * P, :].rearrange("n p s -> p n s"),
                                  pp[:, half], after=[t_lo])
        t_parts[b, qk] = t_out
        if half == 1:
            parts_free[qk] = (t_out,)

    def stack(b):
        for qk in range(2):
            dst = (qst, kst)[qk][b % 2]
            for r, pair in enumerate(PAIRS):
                t_stack[b, qk] = l_stack[qk].start(
                    sp, load, dst[r * D:(r + 1) * D, :, :],
                    split_dram[b, qk, pair[qk]].rearrange("(h d) s -> d h s", d=D),
                    after=[t_parts[b, qk], *(stack_free[b - 2] if b >= 2 else ())])

    def project_v(b, st):
        i, ps, free = misc.take()
        for k in range(KT):
            t = pe.do(T.matmul, ps[:, 0:E], xT[b % 2][:, k, st * P:(st + 1) * P], wv[:, k, :],
                      start=(k == 0), stop=(k == KT - 1), mark=(k == KT - 1), after=[t_wv, t_xT[b], *free])
        t_v[b] = act.do(A.activation, vaug[b % 2][:, st, :, 0:D], ps[:, 0:E].rearrange("p (h d) -> p h d", d=D),
                        ACT.Copy, after=[t, *v_free.get(b - 2, ())])
        misc.give(i, t_v[b])
        if st == ST - 1:
            last_x_use[b] = (t,)
            if b + 2 < B:
                load_x(b + 2)

    t_gain, gain_free = {}, {}

    def modulation(b):
        i, ps, free = misc.take()
        t = pe.do(T.matmul, ps[:, :], condS[:, b:b + 1].to_broadcast([C + 1, P]), wc[:, :], start=True, stop=True,
                  after=[t_cs, t_cond1, t_c, *free])
        t_s = act.do(A.activation, shift[b % 2][:, :], ps[:, 0:E], ACT.Copy, after=[t, *gain_free.get(b - 2, ())])
        t_g = dve.do(V.scalar_tensor_tensor, gain[b % 2][:, :], ps[:, E:2 * E], 1.0, rmsb[:, :], ALU.add, ALU.mult,
                     after=[t_s, *gain_free.get(b - 2, ())])
        misc.give(i, t_s, t_g)
        t_gain[b] = (t_s, t_g)

    t_max, max_free, t_m3, m3_free, mrow_free, t_mrow = {}, {}, {}, {}, {}, {}

    def row_maxima(gi, hh, st):
        b, h = gi // NG, gi % NG * GH + hh
        i, ps, free = row_scores.take()
        t = pe.do(T.matmul, ps[:, :], qst[b % 2][0:KQ, h, st * P:(st + 1) * P], kst[b % 2][0:KQ, h, :],
                  start=True, stop=True, after=[t_stack[b, 0], t_stack[b, 1], *free])
        j, jk, jfree = junks.take()
        t_max[gi] = dve.do(V.tensor_tensor_reduce, jk[:, :], ps[:, :], mneg[:, 0, st, :], 1.0, FLOOR, ALU.add,
                           ALU.max, rowmax[gi % 2][:, hh, st:st + 1], after=[t, t_mn, *jfree, *max_free.get(gi - 2, ())])
        junks.give(j, t_max[gi])
        row_scores.give(i, t_max[gi])

    def split_maxima(gi):
        n, dst = negm[gi % 2], m3[gi % 2]
        v = [dst[:, :, :, k].rearrange("p s h -> p h s") for k in range(PARTS)]
        t = pool.do(G.tensor_scalar, n[:, 0], rowmax[gi % 2][:, :, :], -1.0, None, ALU.mult, after=[t_max[gi]])
        max_free[gi] = (t,)
        t = pool.do(G.tensor_copy, v[0], n[:, 0], after=[t, *m3_free.get(gi - 2, ())])
        t = pool.do(G.tensor_tensor, n[:, 1], n[:, 0], v[0], ALU.subtract, after=[t])
        t = pool.do(G.tensor_copy, v[1], n[:, 1], after=[t])
        t_m3[gi] = pool.do(G.tensor_tensor, v[2], n[:, 1], v[1], ALU.subtract, after=[t])

    def maxima_rows(gi):
        i, ps, free = misc.take()
        for st in range(ST):
            t = pe.do(T.matmul, ps[0:GH * PARTS, st * P:(st + 1) * P],
                      m3[gi % 2][:, st].rearrange("p h n -> p (h n)"), identb[:, :], start=True, stop=True,
                      mark=(st == ST - 1), after=[t_m3[gi], t_idb, *free])
        m3_free[gi] = (t,)
        t = act.do(A.activation, mrow[gi % 2][:, :], ps[0:GH * PARTS, :], ACT.Copy,
                   after=[t, *mrow_free.get(gi - 2, ())])
        misc.give(i, t)
        b = gi // NG
        for hh in range(GH):
            h = gi % NG * GH + hh
            t_mrow[gi] = l_mrow[gi % 2].start(sp, load, qst[b % 2][KQ:KQ + PARTS, h, :],
                                              mrow[gi % 2][hh * PARTS:(hh + 1) * PARTS, :],
                                              after=[t, *stack_free.get(b - 2, ())])
        mrow_free[gi] = (t_mrow[gi],)

    t_prob = {}

    def exponentials(gi, kt, hh):
        b, h = gi // NG, gi % NG * GH + hh
        i, ps, free = col_scores.take()
        limit = kt % 2 == 0 and hh == 1
        t = pe.do(T.matmul, ps[:, :], kst[b % 2][0:KQ + PARTS, h, kt * P:(kt + 1) * P],
                  qst[b % 2][0:KQ + PARTS, h, :], start=True, stop=limit, mark=limit,
                  after=[t_mrow[gi], t_kones, *free])
        if not limit:
            t = pe.do(T.matmul, ps[:, :], identb[:, :], mneg[:, 1, kt, :], start=False, stop=True, after=[t_mn])
        if gi % NG == NG - 1 and kt == ST - 1 and hh == GH - 1:
            stack_free[b] = (t,)
        j, pr, pfree = probs.take()
        t = act.do(A.activation, pr[:, :], ps[:, :], ACT.Exp, scale=float(D) ** -0.5, after=[t, *pfree])
        col_scores.give(i, t)
        if limit:
            t = dve.do(V.tensor_tensor, pr[:, :], pr[:, :], most[:, kt, :], ALU.min, after=[t, t_mn])
        t_prob[gi, kt, hh] = (j, pr, t)

    t_av = {}

    def weighted_values(gi, kt):
        b = gi // NG
        js = []
        for hh in range(GH):
            h = gi % NG * GH + hh
            j, pr, tp = t_prob.pop((gi, kt, hh))
            js.append(j)
            t = pe.do(T.matmul, av_bank[32 * hh:32 * hh + 32, :], vaug[b % 2][:, kt, h, :], pr[:, :],
                      start=(kt == 0), stop=(kt == ST - 1), mark=(hh == GH - 1),
                      after=[tp, t_v[b], t_zero[b % 2], *(av_free[0] if kt == 0 else ())])
        for j in js:
            probs.give(j, t)
        t_av[gi] = t
        if gi % NG == NG - 1 and kt == ST - 1:
            v_free[b] = (t,)

    t_oT, turned_free, oT_free = {}, [(), ()], {}

    def normalise(gi):
        b, u, tn, rd = gi // NG, gi % 2, turned[gi % 2], rden[gi % 2]
        t = dve.do(V.transpose, tn[:, :, :].rearrange("p a c -> p (a c)"), av_bank[:, :],
                   after=[t_av[gi], *turned_free[u]])
        av_free[0] = (t,)
        t = dve.do(V.reciprocal, rd[:, :], tn[:, :, D], after=[t])
        t_n = dve.do(V.tensor_tensor, turned[0][:, :, u * D:(u + 1) * D], tn[:, :, 0:D],
                     rd[:, :].unsqueeze(2).to_broadcast([P, 16, D]), ALU.mult, after=[t])
        if u:
            t_oT[gi // 2] = dve.do(V.transpose, oT[b % 2][:, gi % NG // 2, :],
                                   turned[0][:, :, :].rearrange("p a c -> p (a c)"),
                                   after=[t_n, *oT_free.get(b - 2, ())])
            turned_free[0], turned_free[1] = (t_oT[gi // 2],), (t_n,)

    osb_free = [()]
    t_osb = {}

    def output_projection(b, st):
        i, ps, free = misc.take()
        for g in range(NG // 2):
            t = pe.do(T.matmul, ps[:, 0:E], oT[b % 2][:, g, st * P:(st + 1) * P], wo[:, g, :], start=(g == 0),
                      stop=(g == NG // 2 - 1), mark=(g == NG // 2 - 1), after=[t_oT[b * NG // 2 + g], t_wo, *free])
        if st == ST - 1:
            oT_free[b] = (t,)
        t_osb[b] = act.do(A.activation, osb[:, st, :], ps[:, 0:E], ACT.Copy, after=[t, *osb_free[0]])
        misc.give(i, t_osb[b])

    t_x1 = {}
    l_x1 = lane("x1")
    t_xw, xw_free = {}, [(), ()]
    x2_dram = nc.dram_tensor("x2", (B * S + TW, E), F32, kind="Internal").ap()
    routed = nc.dram_tensor("routed", (LOST_ROW + P, RW), F32, kind="Internal").ap()

    def inverse_rms(sums, after, on):
        q, O = on
        t = q.do(O.tensor_scalar, sums[:, 1], sums[:, 0], 1.0 / E, 1e-6, ALU.mult, ALU.add, after=[after])
        return inverse_root(sums[:, 3], sums[:, 1], sums[:, 2], t, on)

    def inverse_root(y, v, tmp, t, on):
        q, O = on
        t = q.do(O.tensor_scalar, y.bitcast(I32), v.bitcast(I32), -0.5, float(0x5f3759df), ALU.mult, ALU.add,
                 after=[t])
        for _ in range(BETA):
            t = q.do(O.tensor_tensor, tmp, y, y, ALU.mult, after=[t])
            t = q.do(O.tensor_tensor, tmp, tmp, v, ALU.mult, after=[t])
            t = q.do(O.tensor_scalar, tmp, tmp, -0.5, 1.5, ALU.mult, ALU.add, after=[t])
            t = q.do(O.tensor_tensor, y, y, tmp, ALU.mult, after=[t])
        return t

    def helper(b):
        return (pool, G) if b < B - 1 else (dve, V)

    def residual(b):
        q, O = helper(b)
        if b == 0:
            load_xin(1)
        t_s = q.do(O.tensor_tensor, xin[b % 2][:, :, :], xin[b % 2][:, :, :],
                      shift[b % 2][:, :].unsqueeze(1).to_broadcast([P, ST, E]), ALU.add,
                      after=[t_xin[b], *t_gain[b]])
        for st in range(ST):
            j, jk, jfree = junks.take()
            t = dve.do(V.tensor_tensor_reduce, jk[:, 0:E], osb[:, st, :], osb[:, st, :], 1.0, 0.0, ALU.mult,
                       ALU.add, ssq[:, 0, st:st + 1], after=[t_osb[b], *jfree])
            junks.give(j, t)
        t = inverse_rms(ssq, t, helper(b))
        for _ in range(6 if b < B - 1 else 0):
            yield
        for st in range(ST):
            t_g = dve.do(V.scalar_tensor_tensor, osb[:, st, :], osb[:, st, :], ssq[:, 3, st:st + 1],
                         gain[b % 2][:, :], ALU.mult, ALU.mult, after=[t, *t_gain[b]])
        for k in range(TOPK):
            q, O = (pool, G) if k else helper(b)
            t = q.do(O.tensor_tensor, xw[k][:, :, 0:E], xin[b % 2][:, :, :], osb[:, :, :], ALU.add,
                        after=[t_g, t_s, *xw_free[k]])
            t_xw[b, k] = t
        osb_free[0] = last_xin_use[b] = (t, t_xw[b, 0])
        gain_free[b] = (t_g, t_s)
        t_x1[b] = l_x1.start(sp, load, x2_dram[b * S:(b + 1) * S, :].rearrange("(j p) e -> p j e", p=P),
                             xw[0][:, :, 0:E], after=[t_xw[b, 0]])
        if b + 2 < B:
            load_xin(b + 2)

    spare = [misc]

    t_elim = [None]

    def gram():
        i, ps, free = spare[0].take()
        t = pe.do(T.matmul, ps[0:KB, 0:KB], raw[:, 0], raw[:, 0], start=True, stop=True, after=[t_small, *free])
        t = dve.do(V.scalar_tensor_tensor, elim[:, 0:KB], ident[0:KB, 0:KB], 1e-4, ps[0:KB, 0:KB], ALU.mult,
                   ALU.add, after=[t, t_id])
        spare[0].give(i, t)
        t_elim[0] = dve.do(V.tensor_copy, elim[:, KB:2 * KB], raw[:, 1], after=[t])

    def eliminate(j):
        i, ps, free = spare[0].take()
        t = pe.do(T.matmul, ps[0:KB, 0:2 * KB], ident[0:KB, j:j + 1].to_broadcast([KB, KB]), elim[:, :],
                  start=True, stop=True, after=[t_elim[0], t_id, *free])
        t = dve.do(V.reciprocal, pivot[:, 0:1], ps[0:KB, j:j + 1], after=[t])
        t = dve.do(V.scalar_tensor_tensor, pivot[:, 1:2], elim[:, j:j + 1], pivot[:, 0:1], below[:, j:j + 1],
                   ALU.mult, ALU.mult, after=[t, t_const])
        t_elim[0] = dve.do(V.scalar_tensor_tensor, elim[:, :], ps[0:KB, 0:2 * KB], pivot[:, 1:2], elim[:, :],
                           ALU.mult, ALU.add, after=[t])
        spare[0].give(i, t_elim[0])

    t_mtr = []

    def orthogonalise():
        def v(op, *args, **kw):
            return dve.do(op, *args, after=[dve.now()], **kw)

        v(V.tensor_tensor_reduce, below[:, :], elim[:, 0:KB], ident[0:KB, 0:KB], 1.0, 0.0, ALU.mult, ALU.add,
          pivot[:, 2:3])
        inverse_root(pivot[:, 4:5], pivot[:, 2:3], pivot[:, 3:4], dve.now(), on=(dve, V))
        v(V.tensor_scalar, mtrT[:, :], elim[:, KB:2 * KB], pivot[:, 4:5], None, ALU.mult)
        v(V.tensor_tensor_reduce, below[:, :], mtrT[:, :], raw[:, 1], 1.0, 0.0, ALU.mult, ALU.add, pivot[:, 5:6])
        v(V.tensor_scalar, pivot[:, 6:7], pivot[:, 5:6], 0.0, 2.0, ALU.is_ge, ALU.mult)
        v(V.tensor_scalar, pivot[:, 7:8], pivot[:, 6:7], -1.0, None, ALU.add)
        t_mtr[:] = [v(V.tensor_scalar, mtrT[:, :], mtrT[:, :], pivot[:, 7:8], None, ALU.mult)]

    def last_matrices():
        gram()
        yield
        for j in range(KB - 1):
            eliminate(j)
            yield
        orthogonalise()
        yield
        yield from quaternions()
        for b in range(B):
            yield from combined(b)
            yield

    x1T_free, t_gate, t_run, cnt_free = [()], {}, [()], [()]
    gate_ps = {}

    def gate_logits(b):
        for k in range(KT):
            yield
            i, ps, free = misc.take()
            for st in range(ST):
                t = pe.do(T.transpose, ps[:, st * P:(st + 1) * P], xw[0][:, st, k * P:(k + 1) * P], ident[:, :],
                          mark=(st == ST - 1), after=[t_xw[b, 0], t_id, *free])
            t = act.do(A.activation, x1T[:, k, :], ps[:, :], ACT.Copy, after=[t, *x1T_free[0]])
            misc.give(i, t)
        for st in range(ST):
            j, jk, jfree = junks.take()
            t_s = dve.do(V.tensor_tensor_reduce, jk[:, 0:E], xw[0][:, st, 0:E], xw[0][:, st, 0:E], 1.0, 0.0,
                         ALU.mult, ALU.add, newton[:, 0, st:st + 1], after=[t_xw[b, 0], *jfree])
            junks.give(j, t_s)
            if st % 2:
                yield
        t_s = inverse_rms(newton, t_s, helper(b))
        t_gate[b] = (t, t_s)

    def small(op, *args, after=(), **kw):
        return pool.do(op, *args, after=[pool.now(), *after], **kw)

    def wide(a):
        return a.unsqueeze(2).to_broadcast([P, ST, NX])

    oh, eq = (gt[:, 4], gt[:, 5]), gt[:, 3]
    t_cnt = {}

    def choose(b):
        i, ps, free = misc.take()
        for st in range(ST):
            for k in range(KT):
                pe.do(T.matmul, ps[:, st * NX:(st + 1) * NX], x1T[:, k, st * P:(st + 1) * P], wg[:, k],
                      start=(k == 0), stop=(k == KT - 1), mark=False, after=[t_gate[b][0], t_wg, *free])
        t = pe.do(T.matmul, ps[:, ST * NX:(ST + 1) * NX], condR[:, b:b + 1].to_broadcast([C + 2, P]), ggw[:, :],
                  start=True, stop=True, after=[t_small, t_const])
        x1T_free[0] = (t,)
        yield
        t = act.do(A.activation, logits[:, :, :].rearrange("p s x -> p (s x)"), ps[:, 0:(ST + 1) * NX], ACT.Copy,
                   after=[t, *t_lg_free])
        misc.give(i, t)
        revs = rev.unsqueeze(1).to_broadcast([P, ST, NX])
        lg, ex, w = gt[:, 0], gt[:, 1], gt[:, 2]
        small(G.tensor_tensor, lg, logits[:, 0:ST], wide(newton[:, 3]), ALU.mult, after=[t, t_gate[b][1], t_flt])
        t_lg_free[:] = [small(G.tensor_tensor, lg, lg, logits[:, ST].unsqueeze(1).to_broadcast([P, ST, NX]), ALU.add)]
        yield
        yield
        t = dve.do(V.tensor_reduce, gs[:, 0], lg, AX.X, ALU.max, after=t_lg_free)
        t = small(G.tensor_tensor, lg, lg, wide(gs[:, 0]), ALU.subtract, after=[t])
        yield
        t = act.do(A.activation, ex, lg, ACT.Exp, after=[t])
        yield
        t = dve.do(V.tensor_reduce, gs[:, 1], ex, AX.X, ALU.add, after=[t])
        t = dve.do(V.reciprocal, gs[:, 2], gs[:, 1], after=[t])
        t = small(G.tensor_tensor, w, ex, wide(gs[:, 2]), ALU.mult, after=[t])
        yield
        for k in range(TOPK):
            t = dve.do(V.tensor_reduce, gs[:, 3], w, AX.X, ALU.max, after=[t])
            small(G.tensor_copy, xw[k][:, :, E], gs[:, 3], after=[t, *xw_free[k]])
            small(G.tensor_copy, xw[k][:, :, E + 1].bitcast(I32), ints[:, n_tok + b * ST:n_tok + (b + 1) * ST])
            t = dve.do(V.tensor_tensor, eq, w, wide(gs[:, 3]), ALU.is_equal, after=[t])
            t = small(G.tensor_tensor, eq, eq, revs, ALU.mult, after=[t])
            yield
            t = dve.do(V.tensor_reduce, gs[:, 4 + k], eq, AX.X, ALU.max, after=[t])
            t = dve.do(V.tensor_tensor, oh[k], revs, wide(gs[:, 4 + k]), ALU.is_equal, after=[t])
            if k == 0:
                small(G.tensor_scalar, eq, oh[k], -2.0, None, ALU.mult, after=[t])
                t = small(G.tensor_tensor, w, w, eq, ALU.add)
                yield
        t_cnt[b] = small(G.tensor_tensor, cnt[:, :, :], oh[0], oh[1], ALU.add, after=[t, *cnt_free[0]])

    def place(b):
        i, ps, free = misc.take()
        flat = cnt[:, :, :].rearrange("p s x -> p (s x)")
        pe.do(T.matmul, ps[:, 0:ST * NX], upper[:, :], flat, start=True, stop=True, mark=False,
              after=[t_cnt[b], t_const, *free])
        t = pe.do(T.matmul, ps[:, ST * NX:2 * ST * NX], ones[:, :], flat, start=True, stop=True)
        cnt_free[0] = (t,)
        yield
        t = act.do(A.activation, ranks[:, :, :].rearrange("p s x -> p (s x)"), ps[:, 0:2 * ST * NX], ACT.Copy,
                   after=[t, *t_rank_free])
        misc.give(i, t)
        now, before = run[b % 2], run[(b + 1) % 2]
        small(G.tensor_copy, now[:, 0], before[:, ST], after=[t])
        for st in range(ST):
            small(G.tensor_tensor, now[:, st + 1], now[:, st], ranks[:, ST + st], ALU.add)
        slot = gt[:, 6]
        t_rank_free[:] = [small(G.tensor_tensor, slot, now[:, 0:ST], ranks[:, 0:ST], ALU.add)]
        small(G.tensor_tensor, slot, slot, first_row.unsqueeze(1).to_broadcast([P, ST, NX]), ALU.add)
        for k in range(TOPK):
            t = small(G.tensor_tensor, eq, oh[k], slot, ALU.mult)
            yield
            yield
            t = dve.do(V.tensor_reduce, gs[:, 6], eq, AX.X, ALU.add, after=[t])
            small(G.tensor_scalar, gs[:, 7], gs[:, 4 + k], 0.0, flts[:, n_lost:n_lost + 1], ALU.is_equal, ALU.mult,
                  after=[t])
            small(G.tensor_tensor, gs[:, 7], gs[:, 7], gs[:, 6], ALU.add)
            t = small(G.tensor_copy, idx[b % 2][:, k], gs[:, 7], after=idx_free.get(b - 2, ()))
        t_run[0] = t
        for k in range(TOPK):
            for st in range(ST):
                t_sc[k] = start_scatter(l_sc[k], pool, idx[b % 2][:, k, st:st + 1], xw[k][:, st, :],
                                        after=[t, t_xw[b, k]])
                if b < B - 1 and st % 2:
                    yield
        xw_free[0] = (t_sc[0], t_x1[b])
        xw_free[1] = (t_sc[1],)
        idx_free[b] = tuple(t_sc)

    t_lg_free, t_rank_free = [], []
    idx_free, t_sc = {}, [None, None]
    l_sc = [lane(f"scatter{k}") for k in range(TOPK)]

    def scatter_rows(index, src):
        return G.indirect_dma_start(routed, bass.IndirectOffsetOnAxis(ap=index, axis=0), src, None)

    def start_scatter(lane_, queue, index, src, after=()):
        queue.wait(*after)
        queue.steps.append((scatter_rows, (index, src), {}, lane_.sem, 16))
        lane_.count += 16
        return (lane_.sem, lane_.count)

    def project_steps(b):
        return [lambda qk=qk, half=half: project(b, qk, half) for qk in range(2) for half in range(2)]

    def value_steps(b):
        return [lambda: stack(b)] + [lambda st=st: project_v(b, st) for st in range(ST)]

    def finish_steps(b):
        return ([lambda: modulation(b)] + [lambda st=st: output_projection(b, st) for st in range(ST)]
                + [lambda: chains.append(chain(b))])

    chains = []

    def chain(b):
        for part, pause in ((residual, 8), (gate_logits, 4), (choose, 4), (place, 0)):
            yield from part(b)
            if b < B - 1:
                for _ in range(pause):
                    yield

    for step in project_steps(0) + value_steps(0):
        step()

    l_c = lane("conditioning")
    l_c.start(sp, load, condw[:, 0], d["condT"])
    l_c.start(sp, load, wc[0:C], d["WcT"])
    l_c.start(sp, load, wc[C:C + 1], d["bc"].unsqueeze(0))
    t_c = l_c.start(sp, load, rmsb[:, :], d["rms_scale"].unsqueeze(0).to_broadcast([P, E]))

    t_zero = []
    for i in range(2):
        t = pool.do(G.memset, vaug[i][:, :, :, D:32], 0.0, after=[pool.now()])
        t_zero.append(pool.do(G.memset, vaug[i][:, :, :, D:D + 1], 1.0, after=[t]))
        pool.do(G.memset, kst[i][KQ:KQ + PARTS, :, :], 1.0, after=[pool.now()])
    t_kones = pool.now()
    t_cond1 = pool.do(G.memset, condS[C:C + 1, :], 1.0, after=[pool.now()])
    l_wo = lane("wo")
    for g in range(GH):
        for u in range(2):
            t_wo = l_wo.start(sp, load, wo[32 * g + D * u:32 * g + D * u + D],
                              d["WoT"].rearrange("(G u g d) e -> g u d G e", u=2, g=GH, d=D)[g, u])
    load_xin(0)

    l_s = lane("small")
    for dst, src in ((wg[:, :, :], d["wg_W"].rearrange("(k p) x -> p k x", p=P)),
                     (rmsw[:, :], d["rms_w"]),
                     (ggw[0:C], d["gg_W"]), (ggw[C:C + 1], d["gg_b"].unsqueeze(0)),
                     (ggw[C + 1:C + 2], d["wg_b"].unsqueeze(0)), (condR[0:C], d["condT"]),
                     (cond_cols[:, 0], d["condT"]), (cond_cols[:, 1], d["cond64T"]),
                     (raw[:, 0], d["mtr"]), (raw[:, 1], d["mtrT"]), (basis[:, :], d["input_basis"]),
                     (obm[:, :], d["output_basis"])):
        t_small = l_s.start(sp, load, dst, src)

    def constant(op, *args, **kw):
        return pool.do(op, *args, after=[pool.now()], **kw)

    n_rev, n_base, n_tok, n_lost, n_tile = 0, NX, 2 * NX, 2 * NX + NT, 2 * NX + NT + 1
    constant(G.iota, ints[:, n_rev:n_rev + NX], [[-1, NX]], base=NX, channel_multiplier=0)
    constant(G.iota, ints[:, n_base:n_base + NX], [[REGION, NX]], base=0, channel_multiplier=0)
    constant(G.iota, ints[:, n_tok:n_tok + NT], [[P, NT]], base=0, channel_multiplier=1)
    constant(G.iota, ints[:, n_lost:n_lost + 1], [[1, 1]], base=LOST_ROW, channel_multiplier=1)
    constant(G.iota, ints[:, n_tile:n_tile + NTILES], [[1, NTILES]], base=0, channel_multiplier=0)
    constant(G.iota, empty[:, :, E + 1].bitcast(I32), [[P, TT]], base=B * S, channel_multiplier=1)
    constant(G.memset, empty[:, :, 0:E + 1], 0.0)
    constant(G.memset, condR[C:C + 2, :], 1.0)
    constant(G.memset, ones[:, :], 1.0)
    constant(G.memset, run[1][:, ST, :], 0.0)
    constant(G.affine_select, out=upper[:, :], in_=ones[:, :], compare_op=ALU.is_gt, fill=0.0, base=0,
             pattern=[[1, P]], channel_multiplier=-1)
    constant(G.memset, below[:, :], -1.0)
    t_const = constant(G.affine_select, out=below[:, :], in_=below[:, :], compare_op=ALU.is_gt, fill=0.0,
                       base=0, pattern=[[-1, KB]], channel_multiplier=1)
    rev, first_row = flts[:, n_rev:n_rev + NX], flts[:, n_base:n_base + NX]
    t_idb = dve.do(V.tensor_copy, identb[:, :], ident[:, :], after=[t_id])
    t_mn = dve.do(V.tensor_scalar, mneg[:, 0], mask8[:, 0], MASKED, None, ALU.mult, after=[t_mask])
    dve.do(V.tensor_scalar, mneg[:, 1], mask8[:, 1], MASKED, None, ALU.mult)
    t_mn = dve.do(V.tensor_scalar, most[:, :, :], mask8[:, 1], MASKED, -MASKED, ALU.mult, ALU.add)


    t_flt = t_wg = t_cs = t_null = None

    l_pad = lane("pad")

    def prepare():
        nonlocal t_flt, t_wg, t_cs, t_null
        t_flt = dve.do(V.tensor_copy, flts[:, :], ints[:, :], after=[t_const])
        for k in range(KT):
            t_wg = dve.do(V.tensor_scalar, wg[:, k], wg[:, k], rmsw[:, k:k + 1], None, ALU.mult, after=[t_small])

        t_e = act.do(A.activation, condw[:, 1], condw[:, 0], ACT.Exp, scale=-1.0, after=[t_c])
        t = dve.do(V.tensor_scalar, condw[:, 2], condw[:, 1], 1.0, None, ALU.add, after=[t_e])
        t = dve.do(V.reciprocal, condw[:, 1], condw[:, 2], after=[t])
        t = dve.do(V.tensor_tensor, condS[0:C], condw[:, 0], condw[:, 1], ALU.mult, after=[t])
        t_cs = t

        t_null = l_pad.start(sp, load, routed[NULL_ROW:NULL_ROW + TW, :].rearrange("(t p) c -> p t c", p=P),
                             empty[:, :, :], after=[t_const])
        t_null = l_pad.start(sp, load, x2_dram[B * S:, :].rearrange("(t p) c -> p t c", p=P), empty[:, :, 0:E])

    n_groups = B * NG
    todo = []
    for i in range(n_groups + 4):
        b = i // NG
        if (i == 2 or i % NG == 0 and i) and b + 1 < B:
            todo += project_steps(b + 1)
        if i == 1:
            todo.append(prepare)
        if i % NG == 2:
            if b + 1 < B:
                todo += value_steps(b + 1)
        if i % NG == 3 and 0 <= b - 1 < B:
            todo += finish_steps(b - 1)
        for k in range(ST):
            if k == 0 and 0 <= i - 1 < n_groups:
                split_maxima(i - 1)
            g, kt = (i - 2, k - 2) if k > 1 else (i - 3, ST - 2 + k)
            for n in range(GH):
                if i < n_groups:
                    row_maxima(i, k, n)
                if 0 <= i - 2 < n_groups:
                    exponentials(i - 2, k, n)
                if n == 1 and 0 <= g < n_groups:
                    weighted_values(g, kt)
                if chains and next(chains[0], chains) is chains:
                    chains.pop(0)
            if k == 1 and 0 <= i - 3 < n_groups:
                normalise(i - 3)
            if k == 2 and 0 <= i - 1 < n_groups:
                maxima_rows(i - 1)
            for _ in range(2 if len(todo) > 12 else 1):
                if todo:
                    todo.pop(0)()
    while todo:
        todo.pop(0)()
    side = last_matrices()
    for rest_of_batch in chains:
        for n, _ in enumerate(rest_of_batch):
            if n % 2:
                next(side)

    def v(op, *args, after=(), **kw):
        return dve.do(op, *args, after=[dve.now(), *after], **kw)

    counts = run[(B - 1) % 2][:, ST, :]
    v(V.tensor_scalar, tbi[:, :], counts, float(TW - 1), None, ALU.add, after=[t_run[0]])
    v(V.tensor_scalar, tbi[:, :], tbi[:, :], TW.bit_length() - 1, None, ALU.arith_shift_right)
    v(V.tensor_copy, tb[:, 0], tbi[:, :])
    v(V.tensor_copy, tb[:, 1], tb[:, 0])
    for n, step in enumerate((1, 2, 4)):
        v(V.tensor_copy, tb[:, 2 + n, 0:step], tb[:, 1 + n, 0:step])
        v(V.tensor_tensor, tb[:, 2 + n, step:], tb[:, 1 + n, step:], tb[:, 1 + n, :NX - step], ALU.add)
    end, base = tb[:, 4], tb[:, 5]
    v(V.tensor_tensor, base, end, tb[:, 0], ALU.subtract)
    tile_no = flts[:, n_tile:n_tile + NTILES]

    def over_tiles(a):
        return a.unsqueeze(1).to_broadcast([P, NTILES, NX])

    def over_experts(a):
        return a.unsqueeze(2).to_broadcast([P, NTILES, NX])

    expert, left8, first, chunk, used = (tv[:, n] for n in range(5))
    v(V.tensor_tensor, tj[:, 0], over_tiles(end), over_experts(tile_no), ALU.is_le)
    v(V.tensor_reduce, expert, tj[:, 0], AX.X, ALU.add)
    v(V.tensor_scalar, left8, expert, -1.0, float(NX), ALU.mult, ALU.add)
    v(V.tensor_tensor, tj[:, 1], over_tiles(rev), over_experts(left8), ALU.is_equal)
    v(V.tensor_tensor, tj[:, 0], tj[:, 1], over_tiles(base), ALU.mult)
    v(V.tensor_reduce, first, tj[:, 0], AX.X, ALU.add)
    v(V.tensor_tensor, chunk, tile_no, first, ALU.subtract)
    v(V.tensor_scalar, used, expert, float(NX), float(TW), ALU.is_lt, ALU.mult)
    v(V.tensor_tensor, chunk, chunk, used, ALU.mult)
    v(V.scalar_tensor_tensor, table[:, 0:NTILES], expert, float(REGION), chunk, ALU.mult, ALU.add)
    v(V.tensor_scalar, table[:, NTILES:2 * NTILES], expert, float(NX - 1), None, ALU.min)
    t_table = v(V.tensor_tensor, table[:, 2 * NTILES:], first_row, counts, ALU.add)

    regs = {}

    def read_table(key, column, top, on=(sp, nc.sync)):
        def op():
            regs[key] = on[1].value_load(table[0:1, column:column + 1], min_val=0, max_val=top)
        on[0].steps.append((op, (), {}, None, 0))

    def dynamic(lane_, out, in_, after=(), on=(sp, nc.sync)):
        on[0].wait(*after)
        on[0].steps.append((lambda: on[1].dma_start(out(), in_()), (), {}, lane_.sem, 16))
        lane_.count += 16
        return (lane_.sem, lane_.count)

    HT = M // P
    CW = 512
    NR, NS = 2, 5
    W_COLS = ((0, KT * M), (KT * M, (KT + HT) * M), ((KT + HT) * M, (KT + HT) * M + HT * E))
    W_SRC = ((d["W1"], M), (d["W2"], M), (d["W3"], E))
    stacks = [a[:, :, :].rearrange("p h s -> p (h s)").bitcast(F32) for a in stacks0]
    raw_w = [[stacks[i][:, a:b] for i in range(NR)] for a, b in W_COLS]
    l_w3 = [[lane(f"w{n}_{i}") for i in range(NR)] for n in range(3)]
    t_raw, raw_free = {}, {(layer, j - NR): stack_free[B - 2] for layer in range(3) for j in range(NR)}

    def fetch_weights(layer, j, read=True):
        if j >= NTILES:
            return
        src, width = W_SRC[layer]
        if read:
            read_table("expert", NTILES + j, NX - 1)
        t_raw[layer, j] = dynamic(
            l_w3[layer][j % NR], lambda: raw_w[layer][j % NR][:, :].rearrange("p (k m) -> p k m", m=width),
            lambda: src[bass.ds(regs["expert"], 1)].rearrange("e (k p) m -> p (e k) m", p=P),
            after=raw_free.get((layer, j - NR), ()))

    l_pads = [lane("pads_scalar"), lane("pads_sync")]
    t_pads = []
    for n, on in enumerate(((act, nc.scalar), (sp, nc.sync))):
        on[0].wait(t_table, t_small)
        for x in range(n, NX, 2):
            read_table(("pad", n), 2 * NTILES + x, NULL_ROW - TW, on)
            t = dynamic(l_pads[n], lambda n=n: routed[bass.ds(regs["pad", n], TW), :].rearrange("(t p) c -> p t c", p=P),
                        lambda: empty[:, :, :], on=on)
        t_pads.append(t)
    fetch_weights(0, 0)
    attention_done = [pe.now(), act.now(), dve.now(), pool.now(), t_x1[B - 1], *t_sc, *t_pads, t_null]
    for q in (pe, act, dve, pool, sp):
        q.wait(*attention_done)

    phase[0].close()
    phase[0] = ExitStack()
    w_hi = [sb(f"w_hi{i}", [P, W_COLS[2][1]], F32R) for i in range(2)]
    w_lo = [sb(f"w_lo{i}", [P, W_COLS[2][1]], F32R) for i in range(2)]
    bias = [sb(f"bias{i}", [P, 2 * HT]) for i in range(NS)]
    bias3 = [sb(f"bias3_{i}", [P, E]) for i in range(NS)]
    rows = [sb(f"rows{i}", [P, TT, RW]) for i in range(NS)]
    full = [sb(f"full{i}", [P, TW]) for i in range(4)]
    fullT = sb("fullT", [P, KT * TW])
    rowsT = [[sb(f"rowsT{i}_{n}", [P, KT, TW], F32R) for n in range(2)] for i in range(2)]
    hid1 = [[sb(f"hid1_{i}_{n}", [P, HT, TW], F32R) for n in range(2)] for i in range(2)]
    hid2 = [[sb(f"hid2_{i}_{n}", [P, HT, TW], F32R) for n in range(2)] for i in range(2)]
    yout = [sb(f"yout{i}", [P, TT, E]) for i in range(2)]
    ab = [sb(f"ab{i}", [P, KT, E]) for i in range(B)]
    rcob = [sb(f"rcob{i}", [KB, 2, E]) for i in range(2)]
    NL = 4
    x2b = [sb(f"x2b{i}", [P, ST, E]) for i in range(NL)]
    l_row = [lane(f"rows{i}") for i in range(NS)]
    l_bias = [lane(f"bias{i}") for i in range(NS)]

    hidden = Ring(bank[0:4])
    outs = Ring(bank[4:6])
    turns = Ring(bank[6:8])
    fulls = Ring(full)
    t_split, split_free = {}, {}
    t_rows, rows_free, t_bias, bias_free = {}, {}, {}, {}
    t_y, t_rT, rT_free, t_h1, h1_free, t_h2, h2_free, y_free = {}, {}, {}, {}, {}, {}, {}, {}

    def fetch_rows(j):
        if j >= NTILES:
            return
        n = j % NS
        read_table("row", j, NULL_ROW)
        t_rows[j] = dynamic(l_row[n], lambda: rows[n][:, :, :],
                            lambda: routed[bass.ds(regs["row"], TW), :].rearrange("(t p) c -> p t c", p=P),
                            after=rows_free.get(j - NS, ()))
        read_table("expert", NTILES + j, NX - 1)
        dynamic(l_bias[n], lambda: bias[n][:, :],
                lambda: d["b12"][bass.ds(regs["expert"], 1)].rearrange("e p c -> p (e c)"),
                after=bias_free.get(j - NS, ()))
        t_bias[j] = dynamic(l_bias[n], lambda: bias3[n][:, :],
                            lambda: d["b3"][bass.ds(regs["expert"], 1)].to_broadcast([P, E]))

    def split_weights(layer, j, c):
        if j >= NTILES:
            return
        a = W_COLS[layer][0] + c * CW
        src = raw_w[layer][j % NR][:, c * CW:(c + 1) * CW]
        hi, lo = w_hi[j % 2][:, a:a + CW], w_lo[j % 2][:, a:a + CW]
        t = act.do(A.activation, hi, src, ACT.Copy, after=[t_raw[layer, j], *split_free.get((layer, j - 2), ())])
        t = dve.do(V.tensor_tensor, lo, src, hi.bitcast(F32), ALU.subtract,
                   after=[t, *split_free.get((layer, j - 2), ())])
        t_split.setdefault((layer, j), []).append(t)
        raw_free[layer, j] = tuple(t_split[layer, j])
        if (c + 1) * CW == W_COLS[layer][1] - W_COLS[layer][0]:
            fetch_weights(layer, j + NR)

    def products(ps, weights, factors, after):
        for k, (w, x) in enumerate(zip(weights, factors)):
            for n, (p, q) in enumerate(((0, 0), (0, 1), (1, 0))):
                end = k == len(weights) - 1 and n == 2
                t = pe.do(T.matmul, ps, w[p], x[q], start=(k == 0 and n == 0), stop=end, mark=end, after=after[k])
        return t

    def turn(j):
        i, ps, free = turns.take()
        for k in range(KT):
            for tt in range(TT):
                t = pe.do(T.transpose, ps[:, k * TW + tt * P:k * TW + (tt + 1) * P],
                          rows[j % NS][:, tt, k * P:(k + 1) * P], ident[:, :],
                          mark=(k == KT - 1 and tt == TT - 1), after=[t_rows[j], *free])
        hi, lo = (rowsT[j % 2][n][:, :, :].rearrange("p k t -> p (k t)") for n in range(2))
        t = act.do(A.activation, fullT[:, :], ps[:, :], ACT.Copy, after=[t, *fullT_free[0]])
        turns.give(i, t)
        t = dve.do(V.tensor_copy, hi, fullT[:, :], after=[t, *rT_free.get(j - 2, ())])
        t_rT[j] = dve.do(V.tensor_tensor, lo, fullT[:, :], hi.bitcast(F32), ALU.subtract, after=[t])
        fullT_free[0] = (t_rT[j],)

    fullT_free = [()]

    def hidden_part(ps, t, i, bias_column, dst, m, free):
        f, h, ffree = fulls.take()
        t = act.do(A.activation, h[:, :], ps[:, 0:TW], ACT.Relu, bias=bias_column, after=[t, *ffree])
        hidden.give(i, t)
        t_r = t
        hi, lo = dst[0][:, m, :], dst[1][:, m, :]
        t = dve.do(V.tensor_copy, hi, h[:, :], after=[t, *free])
        t = pool.do(G.tensor_tensor, lo, h[:, :], hi.bitcast(F32), ALU.subtract, after=[t, *free])
        fulls.give(f, t)
        return t, t_r

    def layer1(j, m):
        i, ps, free = hidden.take()
        w, r = (w_hi[j % 2], w_lo[j % 2]), rowsT[j % 2]
        t = products(ps[:, 0:TW], [[x[:, k * M + m * P:k * M + (m + 1) * P] for x in w] for k in range(KT)],
                     [[x[:, k, :] for x in r] for k in range(KT)],
                     [[*t_split[0, j], t_rT[j], t_bias[j], *free]] * KT)
        t_h1[j, m], _ = hidden_part(ps, t, i, bias[j % NS][:, m:m + 1], hid1[j % 2], m, h1_free.get(j - 2, ()))
        if m == HT - 1:
            rT_free[j] = split_free[0, j] = (t,)

    def layer2(j, m):
        o = W_COLS[1][0]
        i, ps, free = hidden.take()
        w, r = (w_hi[j % 2], w_lo[j % 2]), hid1[j % 2]
        t = products(ps[:, 0:TW], [[x[:, o + k * M + m * P:o + k * M + (m + 1) * P] for x in w] for k in range(HT)],
                     [[x[:, k, :] for x in r] for k in range(HT)],
                     [[*t_split[1, j], t_h1[j, k], *free] for k in range(HT)])
        t_h2[j, m], t_r = hidden_part(ps, t, i, bias[j % NS][:, HT + m:HT + m + 1], hid2[j % 2], m,
                                      h2_free.get(j - 2, ()))
        if m == HT - 1:
            h1_free[j] = split_free[1, j] = (t,)
            bias_free[j] = (t_r,)

    l_add = lane("add")
    t_add = [None]

    def add_rows(index, src):
        return G.indirect_dma_start(x2_dram, bass.IndirectOffsetOnAxis(ap=index, axis=0), src, None,
                                    compute_op=ALU.add)

    def layer3(j, tt):
        o = W_COLS[2][0]
        i, ps, free = outs.take()
        w = (w_hi[j % 2], w_lo[j % 2])
        t = products(ps[:, 0:E], [[x[:, k, tt * P:(tt + 1) * P] for x in hid2[j % 2]] for k in range(HT)],
                     [[x[:, o + k * E:o + (k + 1) * E] for x in w] for k in range(HT)],
                     [[*t_split[2, j], t_h2[j, k], *free] for k in range(HT)])
        y = yout[j % 2][:, tt]
        t_b = dve.do(V.tensor_tensor, y, ps[:, 0:E], bias3[j % NS][:, :], ALU.add, after=[t, *y_free.get(j - 2, ())])
        outs.give(i, t_b)
        t_w = act.do(A.activation, y, y, ACT.Copy, scale=rows[j % NS][:, tt, E:E + 1], after=[t_b])
        t_y[j, tt] = t_w
        if tt == TT - 1:
            h2_free[j] = split_free[2, j] = (t,)
            bias_free[j] = (*bias_free[j], t_b)

    def add_output(j, tt):
        if j < 0:
            return
        pool.wait(t_y[j, tt], *([t_add[0]] if t_add[0] else []))
        pool.steps.append((add_rows, (rows[j % NS][:, tt, E + 1:E + 2].bitcast(U32), yout[j % 2][:, tt]), {},
                           l_add.sem, 16))
        l_add.count += 16
        t_add[0] = (l_add.sem, l_add.count)
        if tt == TT - 1:
            y_free[j] = (t_add[0],)
            rows_free[j] = (t_add[0], t_y[j, tt])
            fetch_rows(j + NS)

    l_q = lane("quaternions")
    t_quat, t_obm = [], []
    scratch = [x2b[i // 2][:, i % 2 * 2:i % 2 * 2 + 2].rearrange("p s e -> p (s e)") for i in range(2 * NL)]
    QD = E // 4
    t_q = [None]

    def quaternions_load():
        for dst, src, n in ((scratch[0], "cond", B * C), (scratch[1][:, 0:E], "q_right", E)):
            l_q.start(sp, load, dst, d[src].rearrange("b c -> (b c)").unsqueeze(0).to_broadcast([P, n]))
        t_q[0] = l_q.start(sp, load, scratch[1][:, E:E + QD], d["gate"].unsqueeze(0).to_broadcast([P, QD]))

    def quaternions():
        qc = scratch[0].rearrange("p (r d) -> p r d", d=QD)
        qr = scratch[1][:, 0:E].rearrange("p (r d) -> p r d", d=QD)
        gate, norm = scratch[1][:, E:E + QD], scratch[1][:, E + QD:E + 2 * QD]
        inv, tmp = scratch[1][:, E + 2 * QD:E + 3 * QD], scratch[1][:, E + 3 * QD:2 * E]
        sq = scratch[2].rearrange("p (r d) -> p r d", d=QD)
        right = [scratch[3 + i // 2][:, i % 2 * E:(i % 2 + 1) * E].rearrange("p (j d) -> p j d", d=QD) for i in range(4)]
        coef = [scratch[5 + i // 2][:, i % 2 * E:(i % 2 + 1) * E].rearrange("p (j d) -> p j d", d=QD) for i in range(4)]
        prod = scratch[7][:, 0:E].rearrange("p (j d) -> p j d", d=QD)
        t = t_q[0]

        def v(op, *args, **kw):
            return dve.do(op, *args, after=[dve.now(), t], **kw)

        for q, rows in ((qc, B), (qr, 4)):
            v(V.tensor_tensor, sq[:, 0:rows], q, q, ALU.mult)
            v(V.tensor_reduce, norm, sq[:, 0:rows].rearrange("p r d -> p d r"), AX.X, ALU.add)
            v(V.tensor_scalar, norm, norm, 1e-8, None, ALU.add)
            yield
            inverse_root(inv, norm, tmp, dve.now(), on=(dve, V))
            yield
            v(V.tensor_tensor, q[:, 0:4], q[:, 0:4], inv.unsqueeze(1).to_broadcast([P, 4, QD]), ALU.mult)
        v(V.tensor_tensor, qr[:, :, :], qr[:, :, :], gate.unsqueeze(1).to_broadcast([P, 4, QD]), ALU.mult)
        R = (((0, 1), (1, 1), (2, 1), (3, 1)), ((1, -1), (0, 1), (3, -1), (2, 1)),
             ((2, -1), (3, 1), (0, 1), (1, -1)), ((3, -1), (2, -1), (1, 1), (0, 1)))
        L = (((0, 1), (1, -1), (2, -1), (3, -1)), ((1, 1), (0, 1), (3, -1), (2, 1)),
             ((2, 1), (3, 1), (0, 1), (1, -1)), ((3, 1), (2, -1), (1, 1), (0, 1)))
        for i in range(4):
            for j in range(4):
                n, sign = R[i][j]
                v(V.tensor_scalar, right[i][:, j], qr[:, n], float(sign), None, ALU.mult)
            yield
        for i in range(4):
            for k in range(4):
                n, sign = L[i][k]
                left = qc[:, n].unsqueeze(1).to_broadcast([P, 4, QD])
                if k == 0:
                    v(V.tensor_tensor, coef[i], right[k], left, ALU.mult)
                else:
                    v(V.tensor_tensor, prod, right[k], left, ALU.mult)
                    v(V.tensor_tensor, coef[i], coef[i], prod, ALU.add if sign > 0 else ALU.subtract)
                if k % 2:
                    yield
        for j in range(4):
            rows = slice(j % 2 * QD, (j % 2 + 1) * QD)
            for i in range(4):
                t_quat[:] = [v(V.tensor_tensor, quat[rows, j // 2, i * QD:(i + 1) * QD],
                               ident[rows, rows], coef[i][rows, j], ALU.mult)]
            yield
        ob = obm[:, :].rearrange("p (j d) -> p j d", d=QD)
        acc = scratch[2][0:KB, 0:E].rearrange("p (i d) -> p i d", d=QD)
        v(V.tensor_copy, scratch[2][0:KB, 0:E], obm[:, :])
        for i in range(4):
            v(V.tensor_tensor, prod[0:KB], ob, coef[i][0:KB], ALU.mult)
            for j in range(4):
                v(V.tensor_tensor, acc[:, i], acc[:, i], prod[0:KB, j], ALU.add)
            yield
        t = v(V.tensor_copy, obm[:, :], scratch[2][0:KB, 0:E])
        t_obm[:] = [t]

    def combined(b):
        r = rcob[b % 2]
        t = dve.do(V.tensor_scalar, r[:, 0], obm[:, :], cond_cols[:, 1, b:b + 1], None, ALU.mult,
                   after=[*t_obm, t_small, *rc_free.get(b - 2, ())])
        yield
        i, ps, free = turns.take()
        t = pe.do(T.matmul, ps[0:KB, 0:E], mtrT[:, :], r[:, 0], start=True, stop=True, after=[t, *t_mtr, *free])
        t = act.do(A.activation, r[:, 1], ps[0:KB, 0:E], ACT.Copy, scale=cond_cols[:, 0, b:b + 1],
                   after=[t, *rc_free.get(b - 2, ())])
        turns.give(i, t)
        yield
        i, ps, free = turns.take()
        for k in range(KT):
            t = pe.do(T.matmul, ps[:, k * E:(k + 1) * E], basis[:, k * P:(k + 1) * P], r[:, 1], start=True, stop=True,
                      after=[t, *free])
        rc_free[b] = (t,)
        t_ab[b] = dve.do(V.tensor_tensor, ab[b][:, :, :].rearrange("p k e -> p (k e)"), ps[:, :],
                         quat[:, :, :].rearrange("p k e -> p (k e)"), ALU.add, after=[t, *t_quat])
        turns.give(i, t_ab[b])

    t_ab, rc_free = {}, {}
    fetch_rows(0)
    for layer in (1, 2):
        fetch_weights(layer, 0, False)
    fetch_rows(1)
    for layer in range(3):
        fetch_weights(layer, 1, False)
    for j in range(2, NS):
        fetch_rows(j)
    spare[0] = turns
    quaternions_load()
    turn(0)
    split_weights(0, 0, 0)
    split_weights(0, 0, 1)
    for m in range(HT):
        layer1(0, m)
        split_weights(1, 0, m)
    for c in range(2):
        split_weights(2, 0, c)
        split_weights(0, 1, c)
    turn(1)
    for j in range(NTILES):
        for m in range(HT):
            layer2(j, m)
            split_weights(1, j + 1, m)
            if m == 1:
                next(side, None)
        add_output(j - 1, TT - 1)
        for m in range(HT):
            if j + 1 < NTILES:
                layer1(j + 1, m)
            split_weights(2 - m // 2 * 2, j + 1 + m // 2, m % 2)
            if m == 0:
                next(side, None)
        for tt in range(TT):
            layer3(j, tt)
            if tt == 0:
                next(side, None)
        for tt in range(TT - 1):
            add_output(j, tt)
        if j + 2 < NTILES:
            turn(j + 2)
    add_output(NTILES - 1, TT - 1)
    assert next(side, None) is None and len(t_ab) == B

    x2T = [raw_w[1][i][:, 0:KT * S].rearrange("p (k s) -> p k s", k=KT) for i in range(NR)]
    fin = [raw_w[1][i][:, KT * S:].rearrange("p (s e) -> p s e", s=ST) for i in range(NR)]
    x2T_hi, x2T_lo = ([w[i][:, 0:KT * S].rearrange("p (k s) -> p k s", k=KT) for i in range(2)] for w in (w_hi, w_lo))
    ab_hi, ab_lo = ([w[i][:, KT * S:KT * (S + E)] for i in range(2)] for w in (w_hi, w_lo))
    l_x2 = [lane(f"x2_{i}") for i in range(NL)]
    l_out = [lane(f"out{i}") for i in range(2)]
    t_x2, x2_free, x2T_free, t_out, fin_free = {}, {}, {}, {}, {}

    def load_x2(b):
        t_x2[b] = l_x2[b % NL].start(sp, load, x2b[b % NL][:, :, :],
                                     x2_dram[b * S:(b + 1) * S, :].rearrange("(j p) e -> p j e", p=P),
                                     after=[t_add[0], *t_obm, *t_quat, *x2_free.get(b - NL, ())])

    last_product = pe.now()
    for b in range(NL):
        load_x2(b)
    t_split_ab, t_split_x = {}, {}

    def turn_and_split(b):
        whole, hi, lo = ab[b][:, :, :].rearrange("p k e -> p (k e)"), ab_hi[b % 2], ab_lo[b % 2]
        t = act.do(A.activation, hi, whole, ACT.Copy, after=[t_ab[b], last_product, *x2T_free.get(b - 2, ())])
        t_split_ab[b] = dve.do(V.tensor_tensor, lo, whole, hi.bitcast(F32), ALU.subtract,
                               after=[t, *x2T_free.get(b - 2, ())])
        for k in range(KT):
            i, ps, free = turns.take()
            for st in range(ST):
                t = pe.do(T.transpose, ps[:, st * P:(st + 1) * P], x2b[b % NL][:, st, k * P:(k + 1) * P], ident[:, :],
                          mark=(st == ST - 1), after=[t_x2[b], *free])
            whole, hi, lo = x2T[b % 2][:, k, :], x2T_hi[b % 2][:, k, :], x2T_lo[b % 2][:, k, :]
            t = act.do(A.activation, whole, ps[:, :], ACT.Copy, after=[t, *x2T_free.get(b - 2, ())])
            turns.give(i, t)
            t = act.do(A.activation, hi, whole, ACT.Copy, after=[t])
            t_split_x[b, k] = dve.do(V.tensor_tensor, lo, whole, hi.bitcast(F32), ALU.subtract,
                                     after=[t, *x2T_free.get(b - 2, ())])

    turn_and_split(0)
    for b in range(B):
        if b + 1 < B:
            turn_and_split(b + 1)
        for st in range(ST):
            i, ps, free = hidden.take()
            tokens = slice(st * P, (st + 1) * P)
            t = products(ps[:, 0:E], [[x[b % 2][:, k, tokens] for x in (x2T_hi, x2T_lo)] for k in range(KT)],
                         [[a[b % 2][:, k * E:(k + 1) * E] for a in (ab_hi, ab_lo)] for k in range(KT)],
                         [[t_split_x[b, k], t_split_ab[b], *free] for k in range(KT)])
            t_f = dve.do(V.tensor_tensor, fin[b % 2][:, st], ps[:, 0:E], x2b[b % NL][:, st], ALU.add,
                         after=[t, *fin_free.get(b - 2, ())])
            hidden.give(i, t_f)
        x2T_free[b] = (t,)
        x2_free[b] = (t_f,)
        if b + NL < B:
            load_x2(b + NL)
        t_out[b] = l_out[b % 2].start(sp, load, out[b * S:(b + 1) * S, :].rearrange("(j p) e -> p j e", p=P),
                                      fin[b % 2][:, :, :], after=[t_f])
        fin_free[b] = (t_out[b],)
    sp.wait(t_out[B - 2], t_out[B - 1])
    outer.enter_context(phase[0])

    block = ctx.enter_context(nc.Block())
    for start, q in ((block.sync, sp), (block.scalar, act), (block.vector, dve), (block.gpsimd, pool),
                     (block.tensor, pe)):
        start(q.emit)


def kernel(**inputs):
    import concourse.bacc as bacc
    from concourse.bass_utils import run_bass_kernel_spmd
    nc = bacc.Bacc("TRN2", target_bir_lowering=False, num_devices=1)
    a = {n: np.asarray(v) for n, v in inputs.items()}
    x = a["x"].reshape(B * S, E)
    mask = a["mask_SxS_bk1"]

    def columns(b):
        return b.reshape(NX, M // P, P).transpose(0, 2, 1)

    arrays = {
        "x": x, "xT": x.T, "mask": mask, "maskT": mask.T,
        "cond": a["cond_256"], "condT": a["cond_256"].T, "cond64T": a["cond_64"].T,
        "WqT": a["L0_cond_Wq"].T, "WkT": a["L0_cond_Wk"].T, "WvT": a["L0_cond_Wv"].T, "WoT": a["L0_cond_Wo"].T,
        "rms_scale": a["L0_cond_rms_scale"], "WcT": a["L0_cond_Wc"].T, "bc": a["L0_cond_bc"],
        "rms_w": a["L1_cond_rms_w"].reshape(KT, P).T, "wg_W": a["L1_cond_wg_W"], "wg_b": a["L1_cond_wg_b"],
        "gg_W": a["L1_cond_gg_W"], "gg_b": a["L1_cond_gg_b"],
        "W1": a["L1_cond_W1"], "W2": a["L1_cond_W2"], "W3": a["L1_cond_W3"],
        "b12": np.concatenate([columns(a["L1_cond_b1"]), columns(a["L1_cond_b2"])], axis=2), "b3": a["L1_cond_b3"],
        "input_basis": a["L2_cond_input_basis"], "mtr": a["L2_cond_mode_to_rank"],
        "mtrT": a["L2_cond_mode_to_rank"].T, "output_basis": a["L2_cond_output_basis"],
        "q_right": a["L3_cond_q_right"], "gate": a["L3_cond_spectral_gate"].reshape(-1),
    }
    arrays = {"in_" + n: np.ascontiguousarray(v) for n, v in arrays.items()}
    d = {n[3:]: nc.dram_tensor(n, v.shape, mybir.dt.from_np(v.dtype), kind="ExternalInput").ap()
         for n, v in arrays.items()}
    out = nc.dram_tensor("out", (B * S, E), F32, kind="ExternalOutput").ap()
    build(nc, d, out)
    r = run_bass_kernel_spmd(nc, [arrays], core_ids=[0])
    return r.results[0]["out"].reshape(B, S, E)
```
